# Optimizing a Trainium2 kernel written in Bass

```python
import numpy as np
import jax
import jax.numpy as jnp

def _softmax(x, axis=-1):
    return jax.nn.softmax(x, axis=axis)

def _gelu(x):
    return jax.nn.gelu(x, approximate=True)

def _silu(x):
    return jax.nn.silu(x)

def _sigmoid(x):
    return jax.nn.sigmoid(x)

def _layernorm(x, axis=-1, eps=1e-05):
    m = jnp.mean(x, axis=axis, keepdims=True)
    v = jnp.var(x, axis=axis, keepdims=True)
    return (x - m) / jnp.sqrt(v + eps)

def _scatter_add(tgt, idx, src, axis=0):
    return tgt.at[idx].add(src)

def _segment_sum(src, seg, n):
    return jax.ops.segment_sum(src, seg, n)
kernel_name = 'mk_cond_resid_d4_seqx_r4_349e2c'

def setup_inputs(seed: int=0):
    np.random.seed(seed)
    _w = jnp.asarray

    def _rec_inputs():
        import jax
        import jax.numpy as jnp
        _rk = jax.random.key(seed)
        x = 8.748e-05 + 1 * jax.random.normal(jax.random.fold_in(_rk, 1), (4, 512, 512), jnp.float32)
        _lenS = 512 - jax.random.randint(jax.random.fold_in(_rk, 7), (4,), 0, max(1, 512 // 4) + 1, jnp.int32)
        _lenS2 = 512 - jax.random.randint(jax.random.fold_in(_rk, 8), (4,), 0, max(1, 512 // 4) + 1, jnp.int32)
        cond_2048 = -9.80646e-05 + 1.00041 * jax.random.normal(jax.random.fold_in(_rk, 11), (4, 512), jnp.float32)
        return (x, cond_2048)
    x, cond_2048 = _rec_inputs()

    def _L0_cond_setup():
        import jax, jax.numpy as jnp
        import numpy as np
        DT = 0.01
        EPSILON = 0.08
        ALPHA = 0.7
        BETA = 0.8
        CLAMP = 20.0
        B, T, N = (64, 128, 512)

        def _derivative(q, p, drive, coupling, bias):
            i_couple = jnp.tanh(q) @ coupling.T
            dq = q - q ** 3 / 3.0 - p + drive + i_couple + bias
            dp = EPSILON * (q + ALPHA - BETA * p)
            return (dq, dp)

        def _rk4_step(q, p, drive, coupling, bias):
            dq1, dp1 = _derivative(q, p, drive, coupling, bias)
            dq2, dp2 = _derivative(q + 0.5 * DT * dq1, p + 0.5 * DT * dp1, drive, coupling, bias)
            dq3, dp3 = _derivative(q + 0.5 * DT * dq2, p + 0.5 * DT * dp2, drive, coupling, bias)
            dq4, dp4 = _derivative(q + DT * dq3, p + DT * dp3, drive, coupling, bias)
            q_next = q + DT / 6.0 * (dq1 + 2 * dq2 + 2 * dq3 + dq4)
            p_next = p + DT / 6.0 * (dp1 + 2 * dp2 + 2 * dp3 + dp4)
            q_next = jnp.clip(q_next, -CLAMP, CLAMP)
            p_next = jnp.clip(p_next, -CLAMP, CLAMP)
            return (q_next, p_next)
        key = jax.random.key(seed)
        k1, k2, k3, k4 = jax.random.split(key, 4)
        return {'q0': jax.random.normal(k1, (B, N), dtype=jnp.float32), 'p0': jax.random.normal(k2, (B, N), dtype=jnp.float32), 'input_drive_seq': jax.random.normal(k3, (B, T, N), dtype=jnp.float32), 'coupling': jax.random.normal(k4, (N, N), dtype=jnp.float32) * 0.01, 'bias': jnp.zeros((N,), dtype=jnp.float32)}
    _L0_cond_all = _L0_cond_setup()
    _L0_cond_in = {k: v for k, v in _L0_cond_all.items() if k in ('coupling', 'bias')}
    del _L0_cond_all

    def _L1_cond_setup():
        import jax, jax.numpy as jnp
        import numpy as np
        B, T, D = (16, 128, 512)
        key = jax.random.key(seed)
        k0, k1, k2, k3 = jax.random.split(key, 4)
        scale = 1.0 / np.sqrt(D)
        return {'initial_state': jax.random.normal(k0, (B, D), jnp.float32), 'inputs': jax.random.normal(k1, (B, T, D), jnp.float32), 'W_ih': jax.random.normal(k2, (D, 3 * D), jnp.float32) * scale, 'W_hh': jax.random.normal(k3, (D, 3 * D), jnp.float32) * scale, 'b_ih': jnp.zeros((3 * D,), jnp.float32), 'b_hh': jnp.zeros((3 * D,), jnp.float32)}
    _L1_cond_all = _L1_cond_setup()
    _L1_cond_in = {k: v for k, v in _L1_cond_all.items() if k in ('W_ih', 'W_hh', 'b_ih', 'b_hh')}
    del _L1_cond_all

    def _L2_cond_setup():
        import jax, jax.numpy as jnp
        import numpy as np
        HEADS = 16
        EPS = 1e-06

        def _rms_norm(x, g):
            xf = x.astype(jnp.float32)
            y = xf * jax.lax.rsqrt(jnp.mean(xf * xf, axis=-1, keepdims=True) + EPS)
            return y.astype(x.dtype) * g
        key = jax.random.key(seed)
        ks = jax.random.split(key, 6)
        b, n, dim, emb_dim = (4, 512, 512, 512)
        d_head = dim // HEADS
        return {'x': jax.random.normal(ks[0], (b, n, dim), jnp.float32), 'emb': jax.random.normal(ks[1], (b, 1, emb_dim), jnp.float32), 'W_emb': jax.random.normal(ks[2], (emb_dim, 2 * dim), jnp.float32) * emb_dim ** (-0.5), 'b_emb': jnp.zeros((2 * dim,), jnp.float32), 'g_norm': jnp.ones((dim,), jnp.float32), 'W_qkv': jax.random.normal(ks[3], (dim, 3 * dim), jnp.float32) * dim ** (-0.5), 'g_q': jnp.ones((d_head,), jnp.float32), 'g_k': jnp.ones((d_head,), jnp.float32), 'W_out': jax.random.normal(ks[4], (dim, dim), jnp.float32) * dim ** (-0.5)}
    _L2_cond_all = _L2_cond_setup()
    _L2_cond_in = {k: v for k, v in _L2_cond_all.items() if k in ('W_emb', 'b_emb', 'g_norm', 'W_qkv', 'g_q', 'g_k', 'W_out')}
    del _L2_cond_all

    def _L3_cond_setup():
        import jax, jax.numpy as jnp
        import numpy as np
        DIM = 512
        H = 16
        DH = 128
        INNER = H * DH
        MLP = 4 * DIM
        B, T = (2, 512)
        EPS = 1e-06

        def _ln(x):
            mu = jnp.mean(x, axis=-1, keepdims=True)
            var = jnp.var(x, axis=-1, keepdims=True)
            return (x - mu) * jax.lax.rsqrt(var + EPS)
        key = jax.random.key(seed)
        ks = jax.random.split(key, 12)
        s = 0.02
        return {'x': jax.random.normal(ks[0], (B, T, DIM), jnp.float32), 'timestep_embed': jax.random.normal(ks[1], (B, DIM), jnp.float32), 'ada_w': jax.random.normal(ks[2], (DIM, 6 * DIM), jnp.float32) * s, 'ada_b': jnp.zeros((6 * DIM,), jnp.float32), 'qkv_w': jax.random.normal(ks[3], (DIM, 3 * INNER), jnp.float32) * s, 'qkv_b': jnp.zeros((3 * INNER,), jnp.float32), 'out_w': jax.random.normal(ks[4], (INNER, DIM), jnp.float32) * s, 'out_b': jnp.zeros((DIM,), jnp.float32), 'ffn_w1': jax.random.normal(ks[5], (DIM, MLP), jnp.float32) * s, 'ffn_b1': jnp.zeros((MLP,), jnp.float32), 'ffn_w2': jax.random.normal(ks[6], (MLP, DIM), jnp.float32) * s, 'ffn_b2': jnp.zeros((DIM,), jnp.float32)}
    _L3_cond_all = _L3_cond_setup()
    _L3_cond_in = {k: v for k, v in _L3_cond_all.items() if k in ('ada_w', 'ada_b', 'qkv_w', 'qkv_b', 'out_w', 'out_b', 'ffn_w1', 'ffn_b1', 'ffn_w2', 'ffn_b2')}
    del _L3_cond_all
    return {'x': x, 'cond_2048': cond_2048, 'L0_cond_coupling': _L0_cond_in['coupling'], 'L0_cond_bias': _L0_cond_in['bias'], 'L1_cond_W_ih': _L1_cond_in['W_ih'], 'L1_cond_W_hh': _L1_cond_in['W_hh'], 'L1_cond_b_ih': _L1_cond_in['b_ih'], 'L1_cond_b_hh': _L1_cond_in['b_hh'], 'L2_cond_W_emb': _L2_cond_in['W_emb'], 'L2_cond_b_emb': _L2_cond_in['b_emb'], 'L2_cond_g_norm': _L2_cond_in['g_norm'], 'L2_cond_W_qkv': _L2_cond_in['W_qkv'], 'L2_cond_g_q': _L2_cond_in['g_q'], 'L2_cond_g_k': _L2_cond_in['g_k'], 'L2_cond_W_out': _L2_cond_in['W_out'], 'L3_cond_ada_w': _L3_cond_in['ada_w'], 'L3_cond_ada_b': _L3_cond_in['ada_b'], 'L3_cond_qkv_w': _L3_cond_in['qkv_w'], 'L3_cond_qkv_b': _L3_cond_in['qkv_b'], 'L3_cond_out_w': _L3_cond_in['out_w'], 'L3_cond_out_b': _L3_cond_in['out_b'], 'L3_cond_ffn_w1': _L3_cond_in['ffn_w1'], 'L3_cond_ffn_b1': _L3_cond_in['ffn_b1'], 'L3_cond_ffn_w2': _L3_cond_in['ffn_w2'], 'L3_cond_ffn_b2': _L3_cond_in['ffn_b2']}

def reference(x, cond_2048, L0_cond_coupling, L0_cond_bias, L1_cond_W_ih, L1_cond_W_hh, L1_cond_b_ih, L1_cond_b_hh, L2_cond_W_emb, L2_cond_b_emb, L2_cond_g_norm, L2_cond_W_qkv, L2_cond_g_q, L2_cond_g_k, L2_cond_W_out, L3_cond_ada_w, L3_cond_ada_b, L3_cond_qkv_w, L3_cond_qkv_b, L3_cond_out_w, L3_cond_out_b, L3_cond_ffn_w1, L3_cond_ffn_b1, L3_cond_ffn_w2, L3_cond_ffn_b2):
    import jax
    import jax.numpy as jnp

    def _L0_cond_ref(q0, p0, input_drive_seq, coupling, bias):
        import jax, jax.numpy as jnp
        import numpy as np
        DT = 0.01
        EPSILON = 0.08
        ALPHA = 0.7
        BETA = 0.8
        CLAMP = 20.0
        B, T, N = (64, 128, 512)

        def _derivative(q, p, drive, coupling, bias):
            i_couple = jnp.tanh(q) @ coupling.T
            dq = q - q ** 3 / 3.0 - p + drive + i_couple + bias
            dp = EPSILON * (q + ALPHA - BETA * p)
            return (dq, dp)

        def _rk4_step(q, p, drive, coupling, bias):
            dq1, dp1 = _derivative(q, p, drive, coupling, bias)
            dq2, dp2 = _derivative(q + 0.5 * DT * dq1, p + 0.5 * DT * dp1, drive, coupling, bias)
            dq3, dp3 = _derivative(q + 0.5 * DT * dq2, p + 0.5 * DT * dp2, drive, coupling, bias)
            dq4, dp4 = _derivative(q + DT * dq3, p + DT * dp3, drive, coupling, bias)
            q_next = q + DT / 6.0 * (dq1 + 2 * dq2 + 2 * dq3 + dq4)
            p_next = p + DT / 6.0 * (dp1 + 2 * dp2 + 2 * dp3 + dp4)
            q_next = jnp.clip(q_next, -CLAMP, CLAMP)
            p_next = jnp.clip(p_next, -CLAMP, CLAMP)
            return (q_next, p_next)
        drive_tbn = jnp.swapaxes(input_drive_seq, 0, 1)

        def scan_fn(carry, drive):
            q, p = carry
            q, p = _rk4_step(q, p, drive, coupling, bias)
            return ((q, p), q)
        (_, _), q_trace_tbn = jax.lax.scan(scan_fn, (q0, p0), drive_tbn)
        return jnp.swapaxes(q_trace_tbn, 0, 1)

    def _L1_cond_ref(initial_state, inputs, W_ih, W_hh, b_ih, b_hh):
        import jax, jax.numpy as jnp
        import numpy as np
        B, T, D = (16, 128, 512)
        "ScanOverTime(GRU cell): sequential per-timestep module call with\n            dict-state passing; merge_dict_trees stacks the per-step\n            'state_predicted' tensors along axis=1 -> [B, T, D]."

        def cell(h, x):
            gi = x @ W_ih + b_ih
            gh = h @ W_hh + b_hh
            i_r, i_z, i_n = jnp.split(gi, 3, axis=-1)
            h_r, h_z, h_n = jnp.split(gh, 3, axis=-1)
            r = jax.nn.sigmoid(i_r + h_r)
            z = jax.nn.sigmoid(i_z + h_z)
            n = jnp.tanh(i_n + r * h_n)
            h_new = (1.0 - z) * n + z * h
            return (h_new, h_new)
        xs = jnp.swapaxes(inputs, 0, 1)
        _, hs = jax.lax.scan(cell, initial_state, xs)
        return jnp.swapaxes(hs, 0, 1)

    def _L2_cond_ref(x, emb, W_emb, b_emb, g_norm, W_qkv, g_q, g_k, W_out):
        import jax, jax.numpy as jnp
        import numpy as np
        HEADS = 16
        EPS = 1e-06

        def _rms_norm(x, g):
            xf = x.astype(jnp.float32)
            y = xf * jax.lax.rsqrt(jnp.mean(xf * xf, axis=-1, keepdims=True) + EPS)
            return y.astype(x.dtype) * g
        b, n, dim = x.shape
        h = HEADS
        d = dim // h
        scale_shift = emb @ W_emb + b_emb
        scale, shift = jnp.split(scale_shift, 2, axis=-1)
        xn = _rms_norm(x, g_norm) * (1.0 + scale) + shift
        qkv = xn @ W_qkv
        qkv = qkv.reshape(b, n, 3, h, d)
        q, k, v = jnp.moveaxis(qkv, 2, 0)
        q = jnp.swapaxes(q, 1, 2)
        k = jnp.swapaxes(k, 1, 2)
        v = jnp.swapaxes(v, 1, 2)
        q = _rms_norm(q, g_q)
        k = _rms_norm(k, g_k)
        logits = jnp.einsum('bhqd,bhkd->bhqk', q, k) * d ** (-0.5)
        attn = jax.nn.softmax(logits, axis=-1)
        o = jnp.einsum('bhqk,bhkd->bhqd', attn, v)
        o = jnp.swapaxes(o, 1, 2).reshape(b, n, dim)
        return o + o @ W_out

    def _L3_cond_ref(x, timestep_embed, ada_w, ada_b, qkv_w, qkv_b, out_w, out_b, ffn_w1, ffn_b1, ffn_w2, ffn_b2):
        import jax, jax.numpy as jnp
        import numpy as np
        DIM = 512
        H = 16
        DH = 128
        INNER = H * DH
        MLP = 4 * DIM
        B, T = (2, 512)
        EPS = 1e-06

        def _ln(x):
            mu = jnp.mean(x, axis=-1, keepdims=True)
            var = jnp.var(x, axis=-1, keepdims=True)
            return (x - mu) * jax.lax.rsqrt(var + EPS)
        Bc, Tc, D = x.shape
        ada = (timestep_embed @ ada_w + ada_b)[:, None, :]
        shift1, scale1, gate1, shift2, scale2, gate2 = jnp.split(ada, 6, axis=-1)
        x1 = _ln(x) * (1.0 + scale1) + shift1
        qkv = (x1 @ qkv_w + qkv_b).reshape(Bc, Tc, 3, H, DH)
        q, k, v = (qkv[:, :, 0], qkv[:, :, 1], qkv[:, :, 2])
        scale = DH ** (-0.5)
        attn = jnp.einsum('bthd,bshd->bhts', q, k) * scale
        attn = jax.nn.softmax(attn, axis=-1)
        attn_out = jnp.einsum('bhts,bshd->bthd', attn, v).reshape(Bc, Tc, INNER)
        attn_out = attn_out @ out_w + out_b
        x = x + gate1 * attn_out
        x2 = _ln(x) * (1.0 + scale2) + shift2
        h = jax.nn.gelu(x2 @ ffn_w1 + ffn_b1, approximate=False)
        x = x + gate2 * (h @ ffn_w2 + ffn_b2)
        return x
    x = x + _L0_cond_ref(cond_2048, cond_2048, x, L0_cond_coupling, L0_cond_bias)
    x = x + _L1_cond_ref(cond_2048, x, L1_cond_W_ih, L1_cond_W_hh, L1_cond_b_ih, L1_cond_b_hh)
    x = x + _L2_cond_ref(x, cond_2048[:, None, :], L2_cond_W_emb, L2_cond_b_emb, L2_cond_g_norm, L2_cond_W_qkv, L2_cond_g_q, L2_cond_g_k, L2_cond_W_out)
    x = x + _L3_cond_ref(x, cond_2048, L3_cond_ada_w, L3_cond_ada_b, L3_cond_qkv_w, L3_cond_qkv_b, L3_cond_out_w, L3_cond_out_b, L3_cond_ffn_w1, L3_cond_ffn_b1, L3_cond_ffn_w2, L3_cond_ffn_b2)
    return x

_drawn_inputs = setup_inputs


def setup_inputs(seed=0):
    import zlib

    import numpy as np

    out = dict(_drawn_inputs(seed))
    spreads = {'L0_cond_bias': (0.0, 0.1),
     'L1_cond_b_ih': (0.0, 0.1),
     'L1_cond_b_hh': (0.0, 0.401),
     'L2_cond_b_emb': (0.0, 0.1),
     'L2_cond_g_norm': (1.0, 0.2),
     'L2_cond_g_q': (1.0, 0.2),
     'L2_cond_g_k': (1.0, 0.6),
     'L3_cond_ada_b': (0.0, 0.648),
     'L3_cond_qkv_b': (0.0, 0.8),
     'L3_cond_out_b': (0.0, 0.8),
     'L3_cond_ffn_b1': (0.0, 0.8),
     'L3_cond_ffn_b2': (0.0, 0.8)}
    factors = {}
    for name, (base, spread) in spreads.items():
        noise = np.random.default_rng([zlib.crc32(name.encode()), seed]).standard_normal(out[name].shape)
        drawn = base * np.exp(spread * noise) if base else spread * noise
        out[name] = jnp.asarray(drawn.astype(out[name].dtype))
    for name, factor in factors.items():
        out[name] = (out[name] * factor).astype(out[name].dtype)
    return out
```

```python
import concourse.bass as bass
from concourse import mybir
from contextlib import ExitStack

F32, F16 = mybir.dt.float32, mybir.dt.float16
ACT, ALU, AX = mybir.ActivationFunctionType, mybir.AluOpType, mybir.AxisListType

B, T, D, P = 4, 512, 512, 128
K = D // P
S = K * B
CH = 16
NCH = T // CH
G3 = 3 * K
WSCALE = 256.0
DT, EPS_P, ALPHA, BETA, CLAMP = 0.01, 0.08, 0.7, 0.8, 20.0
STEP = [0.5 * DT, 0.5 * DT, DT, DT / 6.0]


class PhaseSemaphores:

    def __init__(self):
        self.ctx, self.nums = ExitStack(), []

    def take(self, nc, name):
        handle = self.ctx.enter_context(nc.semaphore(name))
        self.nums.append(handle.num)
        return handle

    def close(self, nc):
        with nc.Block() as block:
            @block.gpsimd
            def _(pool):
                for n in sorted(self.nums):
                    if n - 1 not in self.nums:
                        last = n
                        while last + 1 in self.nums:
                            last += 1
                        nc.gpsimd.sem_clear(range(n, last + 1))
        self.ctx.close()


def recurrence(nc, ctx, sems, phase_block, XT, q0, coupling, bias0, w_ih, w_hh, b_ih, b_hh, hn_bias, x):
    def sb(name, shape, dt=F32):
        return ctx.enter_context(nc.sbuf_tensor(name, shape, dt))

    def ps(name, shape):
        return ctx.enter_context(nc.psum_tensor(name, shape, F32))

    def sem(name):
        return sems.take(nc, name)

    C = [sb(f"coupling_{n}", [P, K, D], F16) for n in ("hi", "lo")]
    WI = [sb(f"w_ih_{n}", [P, K, 3 * D], F16) for n in ("hi", "lo")]
    WH = [sb(f"w_hh_{n}", [P, K, 3 * D], F16) for n in ("hi", "lo")]
    stage_w = sb("stage_w", [P, K, 3 * D])
    biasq = sb("biasq", [P, S])
    gib, bhh = sb("gib", [P, G3]), sb("bhh", [P, G3])
    SQP = [[sb(f"state{s}_{z}", [P, 2 * S]) for z in range(2)] for s in range(4)]
    raw = sb("raw", [P, 2 * S])
    TX = [sb(f"tanh_parts{i}", [P, K, 2 * B], F16) for i in range(2)]
    T32 = sb("tanh32", [P, S])
    SQ, RS, W3 = sb("sq", [P, S]), sb("rs", [P, S]), sb("w3", [P, S])
    PRE = sb("pre", [P, S])
    FS = sb("fs", [P, S])
    U = sb("u", [P, S])
    AP_ = sb("ap", [P, S])
    DBX = [sb(f"drive{z}", [P, 2 * S]) for z in range(2)]
    GH, GD, G6 = (sb(n, [P, 2 * S]) for n in ("g_half", "g_full", "g_sixth"))
    E2, F1, C6, FB = (sb(n, [P, 2 * S]) for n in ("e2", "f1", "c6", "fb"))
    H = [sb(f"h{z}", [P, S]) for z in range(2)]
    HX = sb("h_parts", [P, K, 2 * B], F16)
    GI = sb("gi", [P, CH, 4 * S])
    S1, S2, RZ = (sb(n, [P, 3 * S]) for n in ("s1", "s2", "rz"))
    M1, M2, NN, DD, ZD = (sb(n, [P, S]) for n in ("m1", "m2", "nn", "dd", "zd"))
    XH = [sb(f"x1_{n}", [P, K, CH * B], F16) for n in ("hi", "lo")]
    warm = sb("warm", [P, 2])

    PL = [[ps(f"osc{i}{h}", [P, 512]) for h in "ab"] for i in range(2)]
    PG = ps("gates", [P, 512])
    PI = [ps("gi_a", [P, 512]), ps("gi_b", [P, 512])]

    NAMES = ["mm_done", "u_done", "q_raw", "q_ready", "hi_ready", "t32_ready", "lo_ready", "sq_ready",
             "rs_ready", "w3_done", "pre_ready", "f_ready", "g_done", "a_done", "p_raw", "p_ready",
             "drive_ready", "e_done", "c6_ready",
             "gates_done", "s1_done", "s2_ready", "rz_ready", "m1_done", "m2_ready", "nn_ready",
             "d_done", "h_ready", "hhi_done", "hx_ready", "x2_done"]
    sets = [{n: sem(f"{n}_{z}") for n in NAMES} for z in range(2)]
    for z in range(2):
        nums = [sets[z][n].num for n in NAMES]
        assert nums == list(range(nums[0], nums[0] + len(NAMES))), nums
    ranges = [range(sets[z][NAMES[0]].num, sets[z][NAMES[-1]].num + 1) for z in range(2)]
    loaded, staged, w_free, wdone = sem("loaded"), sem("staged"), sem("w_free"), sem("wdone")
    xload, init = sem("xload"), sem("init")
    x1_done, xs_hi, xs_done, gi_mm, gi_done = (
        sem(n) for n in ("x1_done", "xs_hi", "xs_done", "gi_mm", "gi_done"))
    pool_passed, pe_passed = sem("pool_passed"), sem("pe_passed")
    gib_done = sem("gib_done")

    def at(t, width=S, off=0):
        return XT[:, bass.ds((t + 1) * S + off, width)]

    def kcols(tile, a, b):
        return tile[:, a * B:b * B]

    half = [(0, 2), (2, 4)]

    def pe_osc(z, s):
        c = sets[z]
        first = [True, True]

        def mm(m, k, w, cols, last=False):
            h = m // 2
            r = nc.tensor.matmul(PL[s % 2][h][:, (m % 2) * 8:(m % 2) * 8 + cols], w[:, k, m * P:(m + 1) * P],
                                 TX[s % 2][:, k, 0:cols], start=first[h], stop=last, skip_group_check=True)
            first[h] = False
            return r
        for i, (a, b) in enumerate(half):
            nc.tensor.wait_ge(c["hi_ready"], 2 * s + 1 + i)
            for k in range(a, b):
                for m in range(K):
                    mm(m, k, C[1], B)
        nc.tensor.wait_ge(c["lo_ready"], s + 1)
        for a, b in half:
            for m in range(a, b):
                for k in range(K):
                    r = mm(m, k, C[0], 2 * B, last=(k == K - 1 and m == b - 1))
            r.then_inc(c["mm_done"], 1)

    gru_list = [(m, k, w) for w in (1, 0) for m in range(G3) for k in range(K)]

    def pe_gru(z, lo, hi):
        c = sets[z]
        if lo == 0:
            nc.tensor.wait_ge(c["hx_ready"], 1)
        for n in range(lo, hi):
            m, k, w = gru_list[n]
            r = nc.tensor.matmul(PG[:, m * 8:m * 8 + 8], WH[w][:, k, m * P:(m + 1) * P], HX[:, k, :],
                                 start=(n == 0), stop=(n == len(gru_list) - 1), skip_group_check=True)
        if hi == len(gru_list):
            r.then_inc(c["gates_done"], 1)

    def pe_step(z, osc, gru):
        for s in range(4):
            if osc:
                pe_osc(z, s)
            if gru and s < 3:
                pe_gru(z, 32 * s, 32 * s + 32)
        if not osc:
            nc.tensor.wait_ge(sets[z]["s2_ready"], 1)
            nc.tensor.sem_inc(pe_passed, 1)

    def act_step(z, osc, gru):
        c, prev = sets[z], sets[1 - z]
        for s in range(4):
            if osc:
                q = SQP[s][z]
                for i, (a, b) in enumerate(half):
                    if s == 0:
                        nc.scalar.wait_ge(prev["q_ready"], 7 + i)
                    else:
                        nc.scalar.wait_ge(c["q_ready"], 2 * s - 1 + i)
                    nc.scalar.activation(TX[s % 2][:, a:b, 0:B], kcols(q, a, b).rearrange("p (k b) -> p k b", b=B),
                                         ACT.Tanh).then_inc(c["hi_ready"], 1)
                nc.scalar.activation(T32[:, :], q[:, 0:S], ACT.Tanh).then_inc(c["t32_ready"], 1)
                nc.scalar.activation(SQ[:, :], q[:, 0:S], ACT.Square).then_inc(c["sq_ready"], 1)
                nc.scalar.wait_ge(c["sq_ready"], s + 1)
                nc.scalar.activation(RS[:, :], SQ[:, :], ACT.Copy, scale=-STEP[s] / 3.0,
                                     bias=STEP[s]).then_inc(c["rs_ready"], 1)
                if s == 1:
                    nc.scalar.wait_ge(c["drive_ready"], 1)
                    nc.scalar.mul(C6[:, :], DBX[z][:, :], DT / 6.0).then_inc(c["c6_ready"], 1)
            if gru and s == 3:
                nc.scalar.wait_ge(c["s2_ready"], 1)
                nc.scalar.activation(RZ[:, 0:2 * S], S2[:, 0:2 * S], ACT.Sigmoid).then_inc(c["rz_ready"], 1)
                nc.scalar.wait_ge(c["m2_ready"], 1)
                nc.scalar.activation(NN[:, :], M2[:, :], ACT.Tanh).then_inc(c["nn_ready"], 1)

    def pool_step(z, t, osc, gru):
        c, prev = sets[z], sets[1 - z]
        for s in range(4):
            if osc:
                if s == 0:
                    nc.gpsimd.tensor_tensor(DBX[z][:, 0:S], at(t), biasq[:, :], ALU.add).then_inc(c["drive_ready"], 1)
                nc.gpsimd.wait_ge(c["rs_ready"], s + 1)
                nc.gpsimd.tensor_tensor(W3[:, :], RS[:, :], SQP[s][z][:, 0:S], ALU.mult).then_inc(c["w3_done"], 1)
                nc.gpsimd.wait_ge(c["w3_done"], s + 1)
                nc.gpsimd.wait_ge(c["f_ready"], s + 1)
                nc.gpsimd.tensor_tensor(PRE[:, :], W3[:, :], FS[:, :], ALU.add).then_inc(c["pre_ready"], 1)
            if gru and s == 0:
                nc.gpsimd.wait_ge(c["h_ready"], 1)
                nc.gpsimd.tensor_tensor(at(t - CH - 1), at(t - CH - 1), H[z][:, :], ALU.add).then_inc(c["x2_done"], 1)
        if not osc:
            nc.gpsimd.wait_ge(c["s2_ready"], 1)
            nc.gpsimd.sem_inc(pool_passed, 1)
        if osc:
            nc.gpsimd.wait_ge(c["q_ready"], 8)
            nc.gpsimd.tensor_tensor(at(t), at(t), SQP[0][1 - z][:, 0:S], ALU.add).then_inc(x1_done, 1)

    def gru_update(z):
        c, prev = sets[z], sets[1 - z]
        nc.vector.wait_ge(prev["nn_ready"], 1)
        nc.vector.tensor_tensor(DD[:, :], H[1 - z][:, :], NN[:, :], ALU.subtract).then_inc(c["d_done"], 1)
        nc.vector.wait_ge(c["d_done"], 1)
        nc.vector.tensor_tensor(ZD[:, :], RZ[:, S:2 * S], DD[:, :], ALU.mult).then_inc(c["d_done"], 1)
        nc.vector.wait_ge(c["d_done"], 2)
        nc.vector.tensor_tensor(H[z][:, :], NN[:, :], ZD[:, :], ALU.add).then_inc(c["h_ready"], 1)
        nc.vector.wait_ge(c["h_ready"], 1)
        hv = H[z][:, :].rearrange("p (k b) -> p k b", b=B)
        nc.vector.tensor_copy(HX[:, :, 0:B], hv).then_inc(c["hhi_done"], 1)
        nc.vector.wait_ge(c["hhi_done"], 1)
        nc.vector.tensor_tensor(HX[:, :, B:2 * B], hv, HX[:, :, 0:B], ALU.subtract).then_inc(c["hx_ready"], 1)

    def gru_gates(z, j):
        c = sets[z]
        gi = lambda a, b: GI[:, bass.ds(j, 1), a * S:b * S].rearrange("p o c -> p (o c)")
        pg = PG[:, 0:G3 * 8].rearrange("p (m c) -> p m c", c=8)
        v3 = lambda x: x.rearrange("p (m b) -> p m b", b=B)
        nc.vector.wait_ge(c["gates_done"], 1)
        nc.vector.scalar_tensor_tensor(v3(S1[:, :]), pg[:, :, 0:B], 1 / WSCALE, v3(gi(0, 3)),
                                       ALU.mult, ALU.add).then_inc(c["s1_done"], 1)
        nc.vector.wait_ge(c["s1_done"], 1)
        nc.vector.scalar_tensor_tensor(v3(S2[:, :]), pg[:, :, B:2 * B], 1 / WSCALE, v3(S1[:, :]),
                                       ALU.mult, ALU.add).then_inc(c["s2_ready"], 1)
        nc.vector.wait_ge(c["rz_ready"], 1)
        nc.vector.tensor_tensor(M1[:, :], RZ[:, 0:S], S2[:, 2 * S:3 * S], ALU.mult).then_inc(c["m1_done"], 1)
        nc.vector.wait_ge(c["m1_done"], 1)
        nc.vector.tensor_tensor(M2[:, :], M1[:, :], gi(3, 4), ALU.add).then_inc(c["m2_ready"], 1)

    def dve_step(z, j, osc, gru):
        c, prev = sets[z], sets[1 - z]
        st = [SQP[s][z] for s in range(4)]
        nxt = SQP[0][1 - z]
        stt = nc.vector.scalar_tensor_tensor
        for s in range(4):
            h = STEP[s]
            if osc:
                if s == 0:
                    nc.vector.wait_ge(prev["p_ready"], 4)
                    nc.vector.wait_ge(c["drive_ready"], 1)
                    stt(GH[:, :], DBX[z][:, :], STEP[0], st[0][:, :], ALU.mult, ALU.add).then_inc(c["g_done"], 1)
                    stt(GD[:, :], DBX[z][:, :], STEP[2], st[0][:, :], ALU.mult, ALU.add).then_inc(c["g_done"], 1)
                    nc.vector.wait_ge(c["g_done"], 1)
                    g = GH
                elif s == 1:
                    nc.vector.wait_ge(c["p_ready"], 1)
                elif s == 2:
                    nc.vector.wait_ge(c["p_ready"], 2)
                    g = GD
                else:
                    nc.vector.wait_ge(c["p_ready"], 3)
                    stt(G6[:, :], st[3][:, :], 1 / 3.0, FB[:, :], ALU.mult, ALU.add).then_inc(c["g_done"], 1)
                    nc.vector.wait_ge(c["g_done"], 3)
                    g = G6
                stt(FS[:, :], st[s][:, S:2 * S], -h, g[:, 0:S], ALU.mult, ALU.add).then_inc(c["f_ready"], 1)
                stt(AP_[:, :], st[s][:, S:2 * S], -BETA, st[s][:, 0:S], ALU.mult, ALU.add).then_inc(c["a_done"], 1)
                nc.vector.wait_ge(c["t32_ready"], s + 1)
                nc.vector.tensor_tensor(TX[s % 2][:, :, B:2 * B], T32[:, :].rearrange("p (k b) -> p k b", b=B),
                                        TX[s % 2][:, :, 0:B], ALU.subtract).then_inc(c["lo_ready"], 1)
                nc.vector.wait_ge(c["a_done"], s + 1)
                if s < 3:
                    stt(st[s + 1][:, S:2 * S], AP_[:, :], h * EPS_P, g[:, S:2 * S],
                        ALU.mult, ALU.add).then_inc(c["p_ready"], 1)
                else:
                    stt(raw[:, S:2 * S], AP_[:, :], h * EPS_P, g[:, S:2 * S], ALU.mult, ALU.add).then_inc(c["p_raw"], 1)
                    nc.vector.wait_ge(c["p_raw"], 1)
                    nc.vector.tensor_scalar(nxt[:, S:2 * S], raw[:, S:2 * S], CLAMP, -CLAMP, ALU.min,
                                            ALU.max).then_inc(c["p_ready"], 1)
                if s == 2:
                    stt(E2[:, :], st[2][:, :], 2.0, st[1][:, :], ALU.mult, ALU.add).then_inc(c["e_done"], 1)
                    nc.vector.wait_ge(c["e_done"], 1)
                    nc.vector.tensor_tensor(F1[:, :], E2[:, :], st[0][:, :], ALU.subtract).then_inc(c["e_done"], 1)
                    nc.vector.wait_ge(c["e_done"], 2)
                    nc.vector.wait_ge(c["c6_ready"], 1)
                    stt(FB[:, :], F1[:, :], 1 / 3.0, C6[:, :], ALU.mult, ALU.add).then_inc(c["e_done"], 1)
            if gru and s == 0:
                gru_update(z)
            if gru and s == 3:
                gru_gates(z, j)
            if s == (1 if osc else 0):
                if not osc:
                    nc.vector.wait_ge(c["gates_done"], 1)
                    nc.vector.wait_ge(c["x2_done"], 1)
                nc.vector.sem_clear(ranges[1 - z])
            if osc:
                nc.vector.wait_ge(c["pre_ready"], s + 1)
                out = raw if s == 3 else st[s + 1]
                for i, (a, b) in enumerate(half):
                    pv = PL[s % 2][i][:, 0:16].rearrange("p (m c) -> p m c", c=8)
                    k3 = lambda x: kcols(x, a, b).rearrange("p (k b) -> p k b", b=B)
                    nc.vector.wait_ge(c["mm_done"], 2 * s + 1 + i)
                    stt(k3(U), pv[:, :, 0:B], h / WSCALE, k3(PRE), ALU.mult, ALU.add).then_inc(c["u_done"], 1)
                    nc.vector.wait_ge(c["u_done"], 2 * s + 1 + i)
                    r = stt(k3(out), pv[:, :, B:2 * B], h / WSCALE, k3(U), ALU.mult, ALU.add)
                    if s < 3:
                        r.then_inc(c["q_ready"], 1)
                    else:
                        r.then_inc(c["q_raw"], 1)
                        nc.vector.wait_ge(c["q_raw"], 1 + i)
                        nc.vector.tensor_scalar(kcols(nxt, a, b), kcols(raw, a, b), CLAMP, -CLAMP, ALU.min,
                                                ALU.max).then_inc(c["q_ready"], 1)
                if s < 3:
                    nc.vector.wait_ge(c["q_ready"], 2 * s + 2)
                else:
                    nc.vector.wait_ge(c["q_ready"], 8)

    block = phase_block

    def chunks(eng, step, between):
        with eng.Fori(0, CH // 2) as j:
            for z in range(2):
                step(z, 0, j * 2 + z, True, False)
        between(0)
        with eng.Fori(1, NCH) as c:
            with eng.Fori(0, CH // 2) as j:
                for z in range(2):
                    step(z, c, j * 2 + z, True, True)
            between(c)
        with eng.Fori(0, CH // 2) as j:
            for z in range(2):
                step(z, NCH, j * 2 + z, False, True)

    @block.sync
    def _(sp):
        sp.dma_start(XT[:, S:(T + 1) * S], x).then_inc(xload, 16)
        for n, (tile, src) in enumerate([(biasq, bias0), (gib, b_ih), (bhh, b_hh), (SQP[0][0][:, 0:S], q0),
                                         (SQP[0][0][:, S:2 * S], q0), (H[1], q0)]):
            sp.dma_start(tile[:, :] if n < 3 or n == 5 else tile, src).then_inc(loaded, 16)
        for j in range(CH):
            sp.dma_start(GI[:, j, 2 * S:3 * S], hn_bias).then_inc(loaded, 16)
        for n, (w, cols) in enumerate([(coupling, D), (w_ih, 3 * D), (w_hh, 3 * D)]):
            if n:
                sp.wait_ge(w_free, n)
            sp.dma_start(stage_w[:, :, 0:cols], w.rearrange("(k p) n -> p k n", p=P)).then_inc(staged, 16)

    @block.tensor
    def _(pe):
        pe.wait_ge(wdone, 3)

        def between(c):
            nc.tensor.wait_ge(xs_done, c + 1)
            todo = [(m, k, w, x) for m in range(G3) for w, x in ((0, 0), (0, 1), (1, 0)) for k in range(K)]
            for n, (m, k, w, x) in enumerate(todo):
                r = nc.tensor.matmul(PI[m // 8][:, (m % 8) * 64:(m % 8) * 64 + 64], WI[w][:, k, m * P:(m + 1) * P],
                                     XH[x][:, k, :], start=(n % 12 == 0), stop=(n % 12 == 11))
            r.then_inc(gi_mm, 1)
        chunks(pe, lambda z, c, j, o, g: pe_step(z, o, g), between)

    @block.scalar
    def _(act):
        nc.scalar.wait_ge(init, 1)
        nc.scalar.activation(warm[:, 1:2], warm[:, 0:1], ACT.Sigmoid)
        chunks(act, lambda z, c, j, o, g: act_step(z, o, g), lambda c: None)

    @block.gpsimd
    def _(pool):
        pool.wait_ge(xload, 16)
        pool.wait_ge(loaded, 16 * (6 + CH))
        pool.wait_ge(init, 2)

        def between(c):
            src = XT[:, bass.ds((c * CH + 1) * S, CH * S)].rearrange("p (t k b) -> p k t b", k=K, b=B)
            hi, lo = (XH[n][:, :, :].rearrange("p k (t b) -> p k t b", b=B) for n in range(2))
            for k in range(K):
                if k == 0:
                    nc.gpsimd.wait_ge(x1_done, (c + 1) * CH)
                    nc.gpsimd.sem_inc(pool_passed, 1)
                nc.gpsimd.tensor_copy(hi[:, k], src[:, k]).then_inc(xs_hi, 1)
            for k in range(K):
                if k == 0:
                    nc.gpsimd.wait_ge(xs_hi, (c + 1) * K)
                    nc.gpsimd.sem_inc(pool_passed, 1)
                r = nc.gpsimd.tensor_tensor(lo[:, k], src[:, k], hi[:, k], ALU.subtract)
            r.then_inc(xs_done, 1)
        chunks(pool, lambda z, c, j, o, g: pool_step(z, c * CH + j, o, g), between)

    @block.vector
    def _(dve):
        nc.vector.memset(warm[:, :], 0.0).then_inc(init, 1)
        nc.vector.memset(DBX[0][:, S:2 * S], EPS_P * ALPHA)
        nc.vector.memset(DBX[1][:, S:2 * S], EPS_P * ALPHA)
        nc.vector.memset(XT[:, 0:S], 0.0)
        nc.vector.memset(NN[:, :], 0.0)
        nc.vector.memset(RZ[:, :], 1.0).then_inc(init, 1)
        dve.wait_ge(init, 2)
        for n, (w, cols) in enumerate([(C, D), (WI, 3 * D), (WH, 3 * D)]):
            dve.wait_ge(staged, 16 * (n + 1))
            nc.vector.tensor_scalar(w[0][:, :, :], stage_w[:, :, 0:cols], WSCALE, None, ALU.mult).then_inc(wdone, 1)
            dve.wait_ge(wdone, n + 1)
            for k in range(K):
                r = nc.vector.scalar_tensor_tensor(w[1][:, k, :], stage_w[:, k, 0:cols], WSCALE, w[0][:, k, :],
                                                   ALU.mult, ALU.subtract)
            r.then_inc(w_free, 1)
        dve.wait_ge(w_free, 3)
        dve.wait_ge(loaded, 16 * (6 + CH))
        nc.vector.tensor_tensor(gib[:, 0:2 * K], gib[:, 0:2 * K], bhh[:, 0:2 * K], ALU.add).then_inc(gib_done, 1)
        dve.wait_ge(gib_done, 1)
        dve.sem_inc(sets[1]["p_ready"], 4)
        dve.sem_inc(sets[1]["q_ready"], 8)

        def between(c):
            if type(c) is int:
                dve.sem_inc(sets[1]["nn_ready"], 1)
            nc.vector.wait_ge(gi_mm, c + 1)
            for i, (a, m0, m1) in enumerate(((0, 0, 8), (3 * S, 8, 12))):
                for m in range(m0, m1):
                    pi = PI[i][:, (m - m0) * 64:(m - m0) * 64 + 64].rearrange("p (t b) -> p t b", b=B)
                    o = GI[:, :, a + (m - m0) * B:a + (m - m0) * B + B]
                    r = nc.vector.tensor_scalar(o, pi, 1 / WSCALE, gib[:, m:m + 1], ALU.mult, ALU.add)
            r.then_inc(gi_done, 1)
            nc.vector.wait_ge(gi_done, c + 1)
        chunks(dve, lambda z, c, j, o, g: dve_step(z, j, o, g), between)
        gru_update(0)
        dve.wait_ge(sets[0]["h_ready"], 1)
        dve.wait_ge(sets[1]["x2_done"], 1)
        nc.vector.tensor_tensor(at(T - 1), at(T - 1), H[0][:, :], ALU.add)

def layer2(nc, ctx, sems, phase_block, XT, cond, w_emb, b_emb, g_norm, w_qkv, g_qk, w_out):
    def sb(name, shape, dt=F32):
        return ctx.enter_context(nc.sbuf_tensor("l2_" + name, shape, dt))

    def sem(name):
        return sems.take(nc, "l2_" + name)

    HEADS, DH = 16, 32
    XV = XT[:, S:(T + 1) * S].rearrange("p (t k b) -> p k b t", k=K, b=B)
    WQKV, WO = sb("w_qkv", [P, K, 3 * D]), sb("w_out", [P, K, D])
    ones_d, ones_h, ident = sb("ones_d", [P, P]), sb("ones_h", [P, P]), sb("ident", [P, P])
    eps, gqk, bemb, gn = sb("eps", [P, 1]), sb("gqk", [P, 2]), sb("bemb", [P, 2 * K]), sb("gn", [P, K])
    WE, CT = sb("w_emb", [P, K, 2 * D]), sb("cond", [P, K, B])
    MOD = sb("mod", [P, 2 * K, B])
    SQX, XN, TMP = sb("sqx", [P, K, T]), sb("xn", [P, K, T]), sb("tmp", [P, K, T])
    LNT, RSTD = sb("lnt", [P, T]), sb("rstd", [P, T])
    SQH, LNH, RH = ([sb(f"{n}{i}", [P, T]) for i in range(2)] for n in ("sqh", "lnh", "rh"))
    QK, V = sb("qk", [P, 2 * K, T]), sb("v", [P, K, D])
    PR = [sb(f"prob{i}", [P, T]) for i in range(2)]
    PT = [sb(f"probT{i}", [P, K, T]) for i in range(2)]
    NM, RSUM, RINV = (sb(n, [P, 2]) for n in ("negmax", "rowsum", "rowinv"))
    OT = sb("oT", [P, K, T])
    YS = [sb(f"ys{i}", [P, T]) for i in range(2)]

    PA = [ctx.enter_context(nc.psum_tensor(f"l2_pa{i}", [P, T], F32)) for i in range(2)]
    PB = [ctx.enter_context(nc.psum_tensor(f"l2_pb{i}", [P, T], F32)) for i in range(2)]
    PO = [ctx.enter_context(nc.psum_tensor(f"l2_po{i}", [P, T], F32)) for i in range(2)]

    loaded, consts, emb_mm, mod_done, mod_raw = (sem(n) for n in ("loaded", "consts", "emb_mm", "mod_done", "mod_raw"))
    sqx, ms, lnt, rstd, xt, xn = (sem(n) for n in ("sqx", "ms", "lnt", "rstd", "xt", "xn"))
    qk_mm, sqh, nh_mm, lnh, rh, qn, v_mm, v_done = (
        sem(n) for n in ("qk_mm", "sqh", "nh_mm", "lnh", "rh", "qn", "v_mm", "v_done"))
    sc, nmax, ex, rinv, pr, tr, ev, o_mm, o_done = (
        sem(n) for n in ("sc", "nmax", "ex", "rinv", "pr", "tr", "ev", "o_mm", "o_done"))
    y_mm, ys, x_done, ident_done = (sem(n) for n in ("y_mm", "ys", "x_done", "ident_done"))
    NU = HEADS * K

    block = phase_block

    @block.sync
    def _(sp):
        for tile, src in ((CT[:, :, :], cond), (WE[:, :, :], w_emb.rearrange("(k p) n -> p k n", p=P)),
                          (bemb[:, :], b_emb), (gn[:, :], g_norm), (gqk[:, :], g_qk),
                          (WQKV[:, :, :], w_qkv.rearrange("(k p) n -> p k n", p=P)),
                          (WO[:, :, :], w_out.rearrange("(k p) n -> p k n", p=P))):
            sp.dma_start(tile, src).then_inc(loaded, 16)

    @block.gpsimd
    def _(pool):
        nc.gpsimd.memset(ident[:, :], 0.0).then_inc(ident_done, 1)
        pool.wait_ge(ident_done, 1)
        nc.gpsimd.affine_select(out=ident[:, :], in_=ident[:, :], compare_op=ALU.not_equal, fill=1.0, base=0,
                                pattern=[[-1, P]], channel_multiplier=1).then_inc(ident_done, 1)

    @block.tensor
    def _(pe):
        mm = nc.tensor.matmul
        pe.wait_ge(loaded, 16 * 7)
        for m in range(2 * K):
            for k in range(K):
                r = mm(PA[0][:, m * B:(m + 1) * B], WE[:, k, m * P:(m + 1) * P], CT[:, k, :],
                       start=(k == 0), stop=(k == K - 1))
        r.then_inc(emb_mm, 1)
        pe.wait_ge(consts, 3)
        pe.wait_ge(ident_done, 2)
        pe.wait_ge(mod_done, 1)
        with pe.Fori(0, B) as b:
            for k in range(K):
                pe.wait_ge(sqx, b * K + k + 1)
                r = mm(PB[0][:, :], ones_d[:, :], SQX[:, k, :], start=(k == 0), stop=(k == K - 1))
            r.then_inc(ms, 1)
            pe.wait_ge(xn, (b + 1) * K)

            def head_norm(c):
                pe.wait_ge(sqh, b * 2 * K + c + 1)
                mm(PB[c % 2][:, :], ones_h[:, :], SQH[c % 2][:, :], start=True, stop=True).then_inc(nh_mm, 1)
            for c in range(2 * K):
                if c >= 2:
                    pe.wait_ge(qn, b * 2 * K + c - 1)
                for k in range(K):
                    r = mm(PA[c % 2][:, :], WQKV[:, k, c * P:(c + 1) * P], XN[:, k, :], start=(k == 0), stop=(k == K - 1))
                r.then_inc(qk_mm, 1)
                if c >= 1:
                    head_norm(c - 1)
            head_norm(2 * K - 1)
            for tc in range(K):
                if tc >= 2:
                    pe.wait_ge(v_done, b * K + tc - 1)
                for k in range(K):
                    r = mm(PO[tc % 2][:, :], XN[:, k, tc * P:(tc + 1) * P], WQKV[:, k, 2 * D:3 * D],
                           start=(k == 0), stop=(k == K - 1))
                r.then_inc(v_mm, 1)
            pe.wait_ge(qn, (b + 1) * 2 * K)
            pe.wait_ge(v_done, (b + 1) * K)

            def scores(n):
                h, i = divmod(n, K)
                c, j = divmod(h, 4)
                r0 = 32 * j
                if n >= 2:
                    pe.wait_ge(ex, b * NU + n - 1)
                mm(PA[n % 2][:, :], QK[r0:r0 + 32, c, i * P:(i + 1) * P], QK[r0:r0 + 32, K + c, :],
                   start=True, stop=True, tile_position=(r0, 0)).then_inc(sc, 1)

            def transposes(n):
                pe.wait_ge(pr, b * NU + n + 1)
                if n >= 2:
                    pe.wait_ge(ev, b * NU + n - 1)
                for kc in range(K):
                    r = nc.tensor.transpose(PB[n % 2][:, kc * P:(kc + 1) * P], PR[n % 2][:, kc * P:(kc + 1) * P],
                                            ident[:, :])
                r.then_inc(tr, 1)

            def values(h):
                c, j = divmod(h, 4)
                pe.wait_ge(ev, b * NU + (h + 1) * K)
                if j == 0 and c >= 2:
                    pe.wait_ge(o_done, b * K + c - 1)
                for kc in range(K):
                    r = mm(PO[c % 2][32 * j:32 * j + 32, :], V[:, kc, h * DH:(h + 1) * DH], PT[h % 2][:, kc, :],
                           start=(kc == 0), stop=(kc == K - 1), tile_position=(0, 32 * j))
                r.then_inc(o_mm, 1)
            scores(0)
            for n in range(NU):
                if n + 1 < NU:
                    scores(n + 1)
                transposes(n)
                if n % K == 0 and n:
                    values(n // K - 1)
            values(HEADS - 1)
            pe.wait_ge(o_done, (b + 1) * K)
            for m in range(K):
                if m >= 2:
                    pe.wait_ge(ys, b * K + m - 1)
                for k in range(K):
                    r = mm(PA[m % 2][:, :], WO[:, k, m * P:(m + 1) * P], OT[:, k, :], start=(k == 0), stop=(k == K - 1))
                r.then_inc(y_mm, 1)
            pe.wait_ge(ys, (b + 1) * K)

    @block.scalar
    def _(act):
        act.wait_ge(consts, 3)
        with act.Fori(0, B) as b:
            for k in range(K):
                nc.scalar.activation(SQX[:, k, :], XV[:, k, bass.ds(b, 1), :].rearrange("p o t -> p (o t)"),
                                     ACT.Square).then_inc(sqx, 1)
            act.wait_ge(ms, b + 1)
            nc.scalar.activation(LNT[:, :], PB[0][:, :], ACT.Ln, bias=eps[:, :]).then_inc(lnt, 1)
            act.wait_ge(lnt, b + 1)
            nc.scalar.activation(RSTD[:, :], LNT[:, :], ACT.Exp, scale=-0.5).then_inc(rstd, 1)

            def head_rstd(c):
                act.wait_ge(nh_mm, b * 2 * K + c + 1)
                nc.scalar.activation(LNH[c % 2][:, :], PB[c % 2][:, :], ACT.Ln, bias=eps[:, :]).then_inc(lnh, 1)
                act.wait_ge(lnh, b * 2 * K + c + 1)
                nc.scalar.activation(RH[c % 2][:, :], LNH[c % 2][:, :], ACT.Exp, scale=-0.5).then_inc(rh, 1)
            for c in range(2 * K):
                act.wait_ge(qk_mm, b * 2 * K + c + 1)
                nc.scalar.activation(SQH[c % 2][:, :], PA[c % 2][:, :], ACT.Square).then_inc(sqh, 1)
                if c >= 1:
                    head_rstd(c - 1)
            head_rstd(2 * K - 1)
            for tc in range(K):
                act.wait_ge(v_mm, b * K + tc + 1)
                nc.scalar.copy(V[:, tc, :], PO[tc % 2][:, :]).then_inc(v_done, 1)

            def evacuate(n):
                h, i = divmod(n, K)
                act.wait_ge(tr, b * NU + n + 1)
                if i == 0 and h >= 2:
                    act.wait_ge(o_mm, b * HEADS + h - 1)
                nc.scalar.copy(PT[h % 2][:, :, i * P:(i + 1) * P],
                               PB[n % 2][:, :].rearrange("p (k q) -> p k q", k=K)).then_inc(ev, 1)
            for n in range(NU):
                act.wait_ge(nmax, b * NU + n + 1)
                if n >= 2:
                    act.wait_ge(tr, b * NU + n - 1)
                nc.scalar.activation(PR[n % 2][:, :], PA[n % 2][:, :], ACT.Exp, bias=NM[:, n % 2:n % 2 + 1],
                                     accum_out=RSUM[:, n % 2:n % 2 + 1]).then_inc(ex, 1)
                if n >= 1:
                    evacuate(n - 1)
            evacuate(NU - 1)
            act.wait_ge(x_done, (b + 1) * K)

    @block.vector
    def _(dve):
        stt, tt, ts = nc.vector.scalar_tensor_tensor, nc.vector.tensor_tensor, nc.vector.tensor_scalar
        nc.vector.memset(ones_d[:, :], 1.0 / D)
        nc.vector.memset(eps[:, :], 1e-6)
        nc.vector.memset(ones_h[:, :], 0.0).then_inc(consts, 1)
        dve.wait_ge(consts, 1)
        for j in range(4):
            r = nc.vector.memset(ones_h[32 * j:32 * j + 32, 32 * j:32 * j + 32], 1.0 / DH)
        r.then_inc(consts, 1)
        dve.wait_ge(loaded, 16 * 7)
        dve.wait_ge(emb_mm, 1)
        tt(MOD[:, :, :], PA[0][:, 0:2 * K * B].rearrange("p (m b) -> p m b", b=B),
           bemb[:, :].unsqueeze(2).to_broadcast([P, 2 * K, B]), ALU.add).then_inc(mod_raw, 1)
        dve.wait_ge(mod_raw, 1)
        stt(MOD[:, 0:K, :], MOD[:, 0:K, :], 1.0, gn[:, :].unsqueeze(2).to_broadcast([P, K, B]), ALU.add,
            ALU.mult).then_inc(mod_done, 1)
        ts(gqk[:, 0:1], gqk[:, 0:1], DH ** -0.5, None, ALU.mult).then_inc(consts, 1)
        dve.wait_ge(consts, 3)
        dve.wait_ge(mod_done, 1)
        with dve.Fori(0, B) as b:
            xb = lambda k: XV[:, k, bass.ds(b, 1), :].rearrange("p o t -> p (o t)")
            dve.wait_ge(rstd, b + 1)
            for k in range(K):
                tt(TMP[:, k, :], xb(k), RSTD[:, :], ALU.mult).then_inc(xt, 1)
            for k in range(K):
                dve.wait_ge(xt, b * K + k + 1)
                ts(XN[:, k, :], TMP[:, k, :], MOD[:, k, bass.ds(b, 1)], MOD[:, K + k, bass.ds(b, 1)],
                   ALU.mult, ALU.add).then_inc(xn, 1)
            for c in range(2 * K):
                dve.wait_ge(rh, b * 2 * K + c + 1)
                stt(QK[:, c, :], PA[c % 2][:, :], gqk[:, c // K:c // K + 1], RH[c % 2][:, :], ALU.mult,
                    ALU.mult).then_inc(qn, 1)

            def normalise(n):
                dve.wait_ge(ex, b * NU + n + 1)
                nc.vector.reciprocal(RINV[:, n % 2:n % 2 + 1], RSUM[:, n % 2:n % 2 + 1]).then_inc(rinv, 1)
                dve.wait_ge(rinv, b * NU + n + 1)
                ts(PR[n % 2][:, :], PR[n % 2][:, :], RINV[:, n % 2:n % 2 + 1], None, ALU.mult).then_inc(pr, 1)
            for n in range(NU):
                dve.wait_ge(sc, b * NU + n + 1)
                nc.vector.tensor_reduce(NM[:, n % 2:n % 2 + 1], PA[n % 2][:, :], AX.X, ALU.max,
                                        negate=True).then_inc(nmax, 1)
                if n >= 1:
                    normalise(n - 1)
                if n % 16 == 6 and n > 16:
                    c = n // 16 - 1
                    dve.wait_ge(o_mm, b * HEADS + 4 * (c + 1))
                    nc.vector.tensor_copy(OT[:, c, :], PO[c % 2][:, :]).then_inc(o_done, 1)
            normalise(NU - 1)
            dve.wait_ge(o_mm, (b + 1) * HEADS)
            nc.vector.tensor_copy(OT[:, K - 1, :], PO[(K - 1) % 2][:, :]).then_inc(o_done, 1)
            for m in range(K):
                dve.wait_ge(y_mm, b * K + m + 1)
                tt(YS[m % 2][:, :], PA[m % 2][:, :], OT[:, m, :], ALU.add).then_inc(ys, 1)
                dve.wait_ge(ys, b * K + m + 1)
                tt(xb(m), xb(m), YS[m % 2][:, :], ALU.add).then_inc(x_done, 1)

def layer3(nc, ctx, sems, XT, cond, ada_w, ada_b, qkv_w, qkv_b, out_w, out_b, w1, b1, w2, b2, out):
    def sb(name, shape, dt=F32, c=ctx):
        return c.enter_context(nc.sbuf_tensor("l3_" + name, shape, dt))

    def sem(name):
        return sems.take(nc, "l3_" + name)

    HEADS, DH, F = 16, 128, 4 * D // P
    SHIFT1, SCALE1, GATE1, SHIFT2, SCALE2, GATE2 = (K * n for n in range(6))
    XV = XT[:, S:(T + 1) * S].rearrange("p (t k b) -> p k b t", k=K, b=B)
    ones_d, ident, eps = sb("ones_d", [P, P]), sb("ident", [P, P]), sb("eps", [P, 1])
    MOD = sb("mod", [P, 6 * K, B])
    Y = sb("y", [P, B, K, T])
    ob, bb2, bb1, bqkv = sb("ob", [P, K]), sb("bb2", [P, K]), sb("bb1", [P, F]), sb("bqkv", [P, 3 * HEADS])
    BH = [sb(f"bias_head{i}", [P, 3]) for i in range(2)]
    PA, PB, PO, PY = ([ctx.enter_context(nc.psum_tensor(f"l3_{n}{i}", [P, T], F32)) for i in range(2)]
                      for n in ("pa", "pb", "po", "py"))
    mm = nc.tensor.matmul
    stt, tt, ts = nc.vector.scalar_tensor_tensor, nc.vector.tensor_tensor, nc.vector.tensor_scalar
    ds = bass.ds

    def norm_sems(tag):
        return {n: sem(tag + n) for n in ("mean", "xc", "sqx", "var", "lnt", "rstd", "xt", "xn")}

    def norm_pe(s, it, xin):
        for k in range(K):
            r = mm(PA[0][:, :], ones_d[:, :], xin(k), start=(k == 0), stop=(k == K - 1))
        r.then_inc(s["mean"], 1)
        for k in range(K):
            nc.tensor.wait_ge(s["sqx"], it * K + k + 1)
            r = mm(PB[0][:, :], ones_d[:, :], SQX[:, k, :], start=(k == 0), stop=(k == K - 1))
        r.then_inc(s["var"], 1)

    def norm_act(s, it):
        for k in range(K):
            nc.scalar.wait_ge(s["xc"], it * K + k + 1)
            nc.scalar.activation(SQX[:, k, :], XC[:, k, :], ACT.Square).then_inc(s["sqx"], 1)
        nc.scalar.wait_ge(s["var"], it + 1)
        nc.scalar.activation(LNT[:, :], PB[0][:, :], ACT.Sqrt, bias=eps[:, :]).then_inc(s["lnt"], 1)

    def norm_dve(s, it, xin, xout, scale, shift, b):
        nc.vector.wait_ge(s["mean"], it + 1)
        for k in range(K):
            tt(XC[:, k, :], xin(k), PA[0][:, :], ALU.subtract).then_inc(s["xc"], 1)
        nc.vector.wait_ge(s["lnt"], it + 1)
        nc.vector.reciprocal(RSTD[:, :], LNT[:, :]).then_inc(s["rstd"], 1)
        nc.vector.wait_ge(s["rstd"], it + 1)
        for k in range(K):
            tt(XC[:, k, :], XC[:, k, :], RSTD[:, :], ALU.mult).then_inc(s["xt"], 1)
        for k in range(K):
            nc.vector.wait_ge(s["xt"], it * K + k + 1)
            ts(xout(k), XC[:, k, :], MOD[:, scale + k, ds(b, 1)], MOD[:, shift + k, ds(b, 1)],
               ALU.mult, ALU.add).then_inc(s["xn"], 1)

    loaded, consts, ident_done, ada_mm, mod_raw, mod_done, y0 = (
        sem(n) for n in ("loaded", "consts", "ident_done", "ada_mm", "mod_raw", "mod_done", "y0"))

    with ExitStack() as c:
        AW, CT, ab = sb("ada_w", [P, K, 6 * D], c=c), sb("cond", [P, K, B], c=c), sb("ada_b", [P, 6 * K], c=c)
        with nc.Block() as block:
            @block.sync
            def _(sp):
                for tile, src in ((CT[:, :, :], cond), (AW[:, :, :], ada_w.rearrange("(k p) n -> p k n", p=P)),
                                  (ab[:, :], ada_b), (ob[:, :], out_b), (bb2[:, :], b2), (bb1[:, :], b1),
                                  (bqkv[:, :], qkv_b)):
                    sp.dma_start(tile, src).then_inc(loaded, 16)

            @block.gpsimd
            def _(pool):
                nc.gpsimd.memset(ident[:, :], 0.0).then_inc(ident_done, 1)
                pool.wait_ge(ident_done, 1)
                nc.gpsimd.affine_select(out=ident[:, :], in_=ident[:, :], compare_op=ALU.not_equal, fill=1.0, base=0,
                                        pattern=[[-1, P]], channel_multiplier=1).then_inc(ident_done, 1)
                nc.gpsimd.memset(Y[:, :, :, :], 0.0).then_inc(y0, 1)

            @block.tensor
            def _(pe):
                pe.wait_ge(loaded, 16 * 7)
                for m in range(6 * K):
                    for k in range(K):
                        r = mm(PA[0][:, m * B:(m + 1) * B], AW[:, k, m * P:(m + 1) * P], CT[:, k, :],
                               start=(k == 0), stop=(k == K - 1))
                r.then_inc(ada_mm, 1)

            @block.vector
            def _(dve):
                nc.vector.memset(ones_d[:, :], 1.0 / D)
                nc.vector.memset(eps[:, :], 1e-6).then_inc(consts, 1)
                dve.wait_ge(loaded, 16 * 7)
                dve.wait_ge(ada_mm, 1)
                tt(MOD[:, :, :], PA[0][:, 0:6 * K * B].rearrange("p (m b) -> p m b", b=B),
                   ab[:, :].unsqueeze(2).to_broadcast([P, 6 * K, B]), ALU.add).then_inc(mod_raw, 1)
                dve.wait_ge(mod_raw, 1)
                for m in (SCALE1, SCALE2):
                    ts(MOD[:, m:m + K, :], MOD[:, m:m + K, :], 1.0, None, ALU.add).then_inc(mod_done, 1)
                ts(bqkv[:, 0:HEADS], bqkv[:, 0:HEADS], DH ** -0.5, None, ALU.mult).then_inc(mod_done, 1)
                dve.wait_ge(mod_done, 3)
                dve.wait_ge(consts, 1)

    with ExitStack() as c:
        X1 = sb("x1", [P, B, K, T], c=c)
        with ExitStack() as cn:
            SQX, XC = sb("sqx", [P, K, T], c=cn), sb("xc", [P, K, T], c=cn)
            LNT, RSTD = sb("lnt", [P, T], c=cn), sb("rstd", [P, T], c=cn)
            s1 = norm_sems("n1_")
            with nc.Block() as block:
                @block.tensor
                def _(pe):
                    for b in range(B):
                        if b:
                            pe.wait_ge(s1["xn"], b * K)
                        norm_pe(s1, b, lambda k: XV[:, k, b, :])

                @block.scalar
                def _(act):
                    for b in range(B):
                        norm_act(s1, b)

                @block.vector
                def _(dve):
                    for b in range(B):
                        norm_dve(s1, b, lambda k: XV[:, k, b, :], lambda k: X1[:, b, k, :], SCALE1, SHIFT1, b)
                    dve.wait_ge(s1["xn"], B * K)

        WQ = [sb(f"wq{i}", [P, K, 3, P], c=c) for i in range(2)]
        WO = [sb(f"wo{i}", [P, D], c=c) for i in range(2)]
        Q, KT, V, O = (sb(n, [P, T], c=c) for n in ("q", "kT", "v", "o"))
        PR = [sb(f"prob{i}", [P, T], c=c) for i in range(2)]
        PT = sb("probT", [P, K, T], c=c)
        NM, RSUM, RINV = (sb(n, [P, 2], c=c) for n in ("negmax", "rowsum", "rowinv"))
        (bias_in, qk_mm, qk, v_mm, v_done, sc, nmax, ex, rinv, pr, tr, ev, o_mm, o_done, y_mm, y_done) = (
            sem("a_" + n) for n in ("bias_in", "qk_mm", "qk", "v_mm", "v_done", "sc", "nmax", "ex", "rinv",
                                    "pr", "tr", "ev", "o_mm", "o_done", "y_mm", "y_done"))
        w_in = [sem(f"a_w_in{i}") for i in range(2)]
        NH = 2 * B
        NU = NH * K
        qkv_h = qkv_w.rearrange("(k p) (w h d) -> h p k w d", p=P, w=3, d=DH)
        out_h = out_w.rearrange("(h p) n -> h p n", p=P)
        with nc.Block() as block:
            @block.sync
            def _(sp):
                with sp.Fori(0, HEADS // 2) as it:
                    for i in range(2):
                        sp.wait_ge(y_mm, (it * 2 + i + 1) * B * K)
                        for w in range(3):
                            sp.dma_start(WQ[i][:, :, w, :], qkv_h[ds(it * 2 + i, 1), :, :, w, :].rearrange("o p k d -> (o p) k d")).then_inc(w_in[i], 16)
                        sp.dma_start(WO[i][:, :], out_h[ds(it * 2 + i, 1), :, :].rearrange("o p n -> (o p) n")).then_inc(w_in[i], 16)

            @block.tensor
            def _(pe):
                pe.sem_inc(y_mm, 2 * B * K)
                pe.wait_ge(y0, 1)
                with pe.Fori(0, HEADS // 2) as it:
                    def scores(u):
                        n, i = divmod(u, K)
                        pe.wait_ge(ex, it * NU + u + 1)
                        mm(PA[u % 2][:, :], Q[:, i * P:(i + 1) * P], KT[:, :], start=True, stop=True).then_inc(sc, 1)

                    def transposes(u):
                        pe.wait_ge(pr, it * NU + u + 1)
                        pe.wait_ge(ev, it * NU + u + 1)
                        for kc in range(K):
                            r = nc.tensor.transpose(PB[u % 2][:, kc * P:(kc + 1) * P],
                                                    PR[u % 2][:, kc * P:(kc + 1) * P], ident[:, :])
                        r.then_inc(tr, 1)
                    for n in range(NH):
                        i, b = divmod(n, B)
                        if b == 0:
                            pe.wait_ge(w_in[i], (it + 1) * 64)
                        for w in range(2):
                            pe.wait_ge(y_done, (it * NH + n) * K + 3 + w)
                            for k in range(K):
                                r = mm(PY[w][:, :], WQ[i][:, k, w, :], X1[:, b, k, :], start=(k == 0), stop=(k == K - 1))
                            r.then_inc(qk_mm, 1)
                        pe.wait_ge(o_done, it * NH + n + 1)
                        for tc in range(K):
                            for k in range(K):
                                r = mm(PO[n % 2][:, tc * P:(tc + 1) * P], X1[:, b, k, tc * P:(tc + 1) * P],
                                       WQ[i][:, k, 2, :], start=(k == 0), stop=(k == K - 1))
                        r.then_inc(v_mm, 1)
                        pe.wait_ge(qk, (it * NH + n + 1) * 2)
                        scores(n * K)
                        for t in range(K):
                            if t + 1 < K:
                                scores(n * K + t + 1)
                            transposes(n * K + t)
                        pe.wait_ge(ev, (it * NH + n + 1) * K + 2)
                        pe.wait_ge(v_done, it * NH + n + 1)
                        for kc in range(K):
                            r = mm(PO[n % 2][:, :], V[:, kc * P:(kc + 1) * P], PT[:, kc, :], start=(kc == 0), stop=(kc == K - 1))
                        r.then_inc(o_mm, 1)
                        pe.wait_ge(o_done, it * NH + n + 3)
                        for m in range(K):
                            if m >= 2:
                                pe.wait_ge(y_done, (it * NH + n) * K + m + 3)
                            r = mm(PY[m % 2][:, :], WO[i][:, m * P:(m + 1) * P], O[:, :], start=True, stop=True)
                            r.then_inc(y_mm, 1)

            @block.scalar
            def _(act):
                act.sem_inc(ex, 2)
                act.sem_inc(ev, 2)
                with act.Fori(0, HEADS // 2) as it:
                    def evacuate(u):
                        act.wait_ge(tr, it * NU + u + 1)
                        nc.scalar.copy(PT[:, :, (u % K) * P:(u % K + 1) * P],
                                       PB[u % 2][:, :].rearrange("p (k q) -> p k q", k=K)).then_inc(ev, 1)
                    for n in range(NH):
                        i, b = divmod(n, B)
                        if b == 0:
                            act.wait_ge(bias_in, it * 2 + i + 1)
                        act.wait_ge(qk_mm, (it * NH + n) * 2 + 1)
                        nc.scalar.activation(Q[:, :], PY[0][:, :], ACT.Identity, bias=BH[i][:, 0:1],
                                             scale=DH ** -0.5).then_inc(qk, 1)
                        act.wait_ge(qk_mm, (it * NH + n) * 2 + 2)
                        nc.scalar.activation(KT[:, :], PY[1][:, :], ACT.Identity, bias=BH[i][:, 1:2]
                                             ).then_inc(qk, 1)
                        act.wait_ge(v_mm, it * NH + n + 1)
                        nc.scalar.copy(V[:, :], PO[n % 2][:, :]).then_inc(v_done, 1)
                        for t in range(K):
                            u = n * K + t
                            act.wait_ge(nmax, it * NU + u + 1)
                            nc.scalar.activation(PR[u % 2][:, :], PA[u % 2][:, :], ACT.Exp, bias=NM[:, u % 2:u % 2 + 1],
                                                 accum_out=RSUM[:, u % 2:u % 2 + 1]).then_inc(ex, 1)
                            if t:
                                evacuate(u - 1)
                        evacuate(n * K + K - 1)

            @block.vector
            def _(dve):
                dve.sem_inc(y_done, K)
                dve.sem_inc(o_done, 2)
                with dve.Fori(0, HEADS // 2) as it:
                    def normalise(u):
                        j = u % 2
                        dve.wait_ge(ex, it * NU + u + 3)
                        nc.vector.reciprocal(RINV[:, j:j + 1], RSUM[:, j:j + 1]).then_inc(rinv, 1)
                        dve.wait_ge(rinv, it * NU + u + 1)
                        ts(PR[j][:, :], PR[j][:, :], RINV[:, j:j + 1], None, ALU.mult).then_inc(pr, 1)
                    for n in range(NH):
                        i, b = divmod(n, B)
                        if b == 0:
                            for w in range(3):
                                r = nc.vector.tensor_copy(BH[i][:, w:w + 1], bqkv[:, ds(it * 2 + (i + w * HEADS), 1)])
                            r.then_inc(bias_in, 1)
                        for t in range(K):
                            u = n * K + t
                            dve.wait_ge(sc, it * NU + u + 1)
                            nc.vector.tensor_reduce(NM[:, u % 2:u % 2 + 1], PA[u % 2][:, :], AX.X, ALU.max,
                                                    negate=True).then_inc(nmax, 1)
                            if t:
                                normalise(u - 1)
                        normalise(n * K + K - 1)
                        dve.wait_ge(o_mm, it * NH + n + 1)
                        ts(O[:, :], PO[n % 2][:, :], BH[i][:, 2:3], None, ALU.add).then_inc(o_done, 1)
                        for m in range(K):
                            dve.wait_ge(y_mm, (it * NH + n + 2 * B) * K + m + 1)
                            tt(Y[:, b, m, :], Y[:, b, m, :], PY[m % 2][:, :], ALU.add).then_inc(y_done, 1)
                dve.wait_ge(y_done, (HEADS * B + 1) * K)

    with ExitStack() as c:
        W1, W2 = sb("w1", [P, K, 4 * D], c=c), sb("w2", [P, F, D], c=c)
        SQX, XC = sb("sqx2", [P, K, T], c=c), sb("xc2", [P, K, T], c=c)
        LNT, RSTD = sb("lnt2", [P, T], c=c), sb("rstd2", [P, T], c=c)
        XP, X2, HF = sb("xp", [P, K, T], c=c), sb("x2", [P, K, T], c=c), sb("hf", [P, F, T], c=c)
        R, R2, OUT = sb("r", [P, K, T], c=c), SQX, X2
        s2 = norm_sems("n2_")
        w_in, yg, xp, h_mm, h_done, z_mm, r1, r2, o_ready, o_out = (
            sem("m_" + n) for n in ("w_in", "yg", "xp", "h_mm", "h_done", "z_mm", "r1", "r2", "o_ready", "o_out"))
        with nc.Block() as block:
            @block.sync
            def _(sp):
                sp.dma_start(W1[:, :, :], w1.rearrange("(k p) n -> p k n", p=P)).then_inc(w_in, 16)
                sp.dma_start(W2[:, :, :], w2.rearrange("(k p) n -> p k n", p=P)).then_inc(w_in, 16)
                with sp.Fori(0, B) as b:
                    sp.wait_ge(o_ready, (b + 1) * K)
                    sp.dma_start(out[ds(b, 1), :, :, :].rearrange("o k p t -> p (o k) t"), OUT[:, :, :]).then_inc(o_out, 16)
                sp.wait_ge(o_out, 16 * (B + 1))

            @block.tensor
            def _(pe):
                with pe.Fori(0, B) as b:
                    pe.wait_ge(xp, (b + 1) * K)
                    norm_pe(s2, b, lambda k: XP[:, k, :])
                    pe.wait_ge(w_in, 32)
                    pe.wait_ge(s2["xn"], (b + 1) * K)
                    for m in range(F):
                        if m >= 2:
                            pe.wait_ge(h_done, b * F + m - 1)
                        for k in range(K):
                            r = mm(PO[m % 2][:, :], W1[:, k, m * P:(m + 1) * P], X2[:, k, :], start=(k == 0), stop=(k == K - 1))
                        r.then_inc(h_mm, 1)
                    pe.wait_ge(h_done, (b + 1) * F)
                    for m in range(K):
                        if m >= 2:
                            pe.wait_ge(r1, b * K + m - 1)
                        for k in range(F):
                            r = mm(PY[m % 2][:, :], W2[:, k, m * P:(m + 1) * P], HF[:, k, :], start=(k == 0), stop=(k == F - 1))
                        r.then_inc(z_mm, 1)

            @block.scalar
            def _(act):
                with act.Fori(0, B) as b:
                    norm_act(s2, b)
                    for m in range(F):
                        act.wait_ge(h_mm, b * F + m + 1)
                        nc.scalar.activation(HF[:, m, :], PO[m % 2][:, :], ACT.Gelu, bias=bb1[:, m:m + 1]).then_inc(h_done, 1)

            @block.vector
            def _(dve):
                dve.sem_inc(o_out, 16)
                with dve.Fori(0, B) as b:
                    xb = lambda k: XV[:, k, ds(b, 1), :].rearrange("p o t -> p (o t)")
                    yb = lambda k: Y[:, ds(b, 1), k, :].rearrange("p o t -> p (o t)")
                    dve.wait_ge(o_out, b * 16 + 16)
                    for k in range(K):
                        ts(R[:, k, :], yb(k), ob[:, k:k + 1], MOD[:, GATE1 + k, ds(b, 1)], ALU.add, ALU.mult).then_inc(yg, 1)
                    for k in range(K):
                        dve.wait_ge(yg, b * K + k + 1)
                        tt(XP[:, k, :], R[:, k, :], xb(k), ALU.add).then_inc(xp, 1)
                    dve.wait_ge(xp, (b + 1) * K)
                    norm_dve(s2, b, lambda k: XP[:, k, :], lambda k: X2[:, k, :], SCALE2, SHIFT2, b)
                    for m in range(K):
                        dve.wait_ge(z_mm, b * K + m + 1)
                        ts(R[:, m, :], PY[m % 2][:, :], bb2[:, m:m + 1], MOD[:, GATE2 + m, ds(b, 1)], ALU.add,
                           ALU.mult).then_inc(r1, 1)
                        dve.wait_ge(r1, b * K + m + 1)
                        tt(R2[:, m, :], R[:, m, :], XP[:, m, :], ALU.add).then_inc(r2, 1)
                        dve.wait_ge(r2, b * K + m + 1)
                        tt(OUT[:, m, :], R2[:, m, :], xb(m), ALU.add).then_inc(o_ready, 1)


def program(nc, x, state, coupling, osc_bias, w_ih, w_hh, b_ih, b_hh, hn_bias, l2, l3, out):
    with ExitStack() as ctx:
        XT = ctx.enter_context(nc.sbuf_tensor("x_time_major", [P, (T + 1) * S], F32))
        cond = state.rearrange("p (k b) -> p k b", b=B)
        sems = PhaseSemaphores()
        with ExitStack() as c:
            with nc.Block() as block:
                recurrence(nc, c, sems, block, XT, state, coupling, osc_bias, w_ih, w_hh, b_ih, b_hh, hn_bias, x)
        sems.close(nc)
        sems = PhaseSemaphores()
        with ExitStack() as c:
            with nc.Block() as block:
                layer2(nc, c, sems, block, XT, cond, *l2)
        sems.close(nc)
        sems = PhaseSemaphores()
        with ExitStack() as c:
            layer3(nc, c, sems, XT, cond, *l3, out)
        sems.close(nc)


def kernel(**inputs):
    import numpy as np
    import concourse.bacc as bacc
    from concourse.bass_utils import run_bass_kernel_spmd

    def cols(name):
        return inputs[name].reshape(-1, P).T

    inputs = {n: np.asarray(a) for n, a in inputs.items()}
    arrays = {
        "x": inputs["x"].reshape(B, T, K, P).transpose(3, 1, 2, 0).reshape(P, T * S),
        "state": inputs["cond_2048"].reshape(B, K, P).transpose(2, 1, 0).reshape(P, S),
        "coupling": inputs["L0_cond_coupling"].T,
        "osc_bias": np.repeat(cols("L0_cond_bias"), B, axis=1),
        "w_ih": inputs["L1_cond_W_ih"], "w_hh": inputs["L1_cond_W_hh"],
        "b_ih": cols("L1_cond_b_ih"), "b_hh": cols("L1_cond_b_hh"),
        "hn_bias": np.repeat(cols("L1_cond_b_hh")[:, 2 * K:], B, axis=1),
        "w_emb": inputs["L2_cond_W_emb"], "b_emb": cols("L2_cond_b_emb"), "g_norm": cols("L2_cond_g_norm"),
        "w_qkv": inputs["L2_cond_W_qkv"],
        "g_qk": np.stack([np.tile(inputs["L2_cond_g_q"], 4), np.tile(inputs["L2_cond_g_k"], 4)], 1),
        "w_out": inputs["L2_cond_W_out"],
        "ada_w": inputs["L3_cond_ada_w"], "ada_b": cols("L3_cond_ada_b"), "qkv_w": inputs["L3_cond_qkv_w"],
        "qkv_b": cols("L3_cond_qkv_b"), "out_w": inputs["L3_cond_out_w"], "out_b": cols("L3_cond_out_b"),
        "w1": inputs["L3_cond_ffn_w1"], "b1": cols("L3_cond_ffn_b1"), "w2": inputs["L3_cond_ffn_w2"],
        "b2": cols("L3_cond_ffn_b2"),
    }
    arrays = {n: np.ascontiguousarray(a) for n, a in arrays.items()}
    nc = bacc.Bacc("TRN2", target_bir_lowering=False, num_devices=1)
    ap = {n: nc.dram_tensor("in_" + n, a.shape, mybir.dt.from_np(a.dtype), kind="ExternalInput").ap()
          for n, a in arrays.items()}
    out = nc.dram_tensor("out", (B, K, P, T), F32, kind="ExternalOutput").ap()
    names = list(ap)
    i2, i3 = names.index("w_emb"), names.index("ada_w")
    program(nc, *(ap[n] for n in names[:i2]), [ap[n] for n in names[i2:i3]], [ap[n] for n in names[i3:]], out)
    r = run_bass_kernel_spmd(nc, [{"in_" + n: a for n, a in arrays.items()}], core_ids=[0])
    return r.results[0]["out"].transpose(0, 3, 1, 2).reshape(B, T, D)
```

```python
import concourse.bass as bass
from concourse import mybir
from contextlib import ExitStack

F32, F16 = mybir.dt.float32, mybir.dt.float16
ds = bass.ds
ACT, ALU, AX = mybir.ActivationFunctionType, mybir.AluOpType, mybir.AxisListType

B, T, D, P = 4, 512, 512, 128
K = D // P
S = K * B
CH = 16
NCH = T // CH
UN = 4
G3 = 3 * K
WSCALE = 256.0
DT, EPS_P, ALPHA, BETA, CLAMP = 0.01, 0.08, 0.7, 0.8, 20.0
STEP = [0.5 * DT, 0.5 * DT, DT, DT / 6.0]


class PhaseSemaphores:

    def __init__(self):
        self.ctx, self.nums = ExitStack(), []

    def take(self, nc, name):
        handle = self.ctx.enter_context(nc.semaphore(name))
        self.nums.append(handle.num)
        return handle

    def close(self, nc):
        with nc.Block() as block:
            @block.gpsimd
            def _(pool):
                for n in sorted(self.nums):
                    if n - 1 not in self.nums:
                        last = n
                        while last + 1 in self.nums:
                            last += 1
                        nc.gpsimd.sem_clear(range(n, last + 1))
        self.ctx.close()


def recurrence(nc, ctx, sems, phase_block, XT, q0, coupling, bias0, w_ih, w_hh, b_ih, b_hh, hn_bias, x):
    def sb(name, shape, dt=F32):
        return ctx.enter_context(nc.sbuf_tensor(name, shape, dt))

    def ps(name, shape):
        return ctx.enter_context(nc.psum_tensor(name, shape, F32))

    def sem(name):
        return sems.take(nc, name)

    C = [sb(f"coupling_{n}", [P, K, D], F16) for n in ("hi", "lo")]
    WI = [sb(f"w_ih_{n}", [P, K, 3 * D], F16) for n in ("hi", "lo")]
    WH = [sb(f"w_hh_{n}", [P, K, 3 * D], F16) for n in ("hi", "lo")]
    stage_w = sb("stage_w", [P, K, 3 * D])
    biasq = sb("biasq", [P, S])
    gib, bhh = sb("gib", [P, G3]), sb("bhh", [P, G3])
    SQP = [[sb(f"state{s}_{z}", [P, 2 * S]) for z in range(2)] for s in range(4)]
    raw = sb("raw", [P, 2 * S])
    TX = [sb(f"tanh_parts{i}", [P, K, 2 * B], F16) for i in range(2)]
    T32 = sb("tanh32", [P, S])
    SQ, W3 = sb("sq", [P, S]), sb("w3", [P, S])
    PRE = sb("pre", [P, S])
    FS = sb("fs", [P, S])
    U = sb("u", [P, S])
    AP_ = sb("ap", [P, S])
    DBX = [sb(f"drive{z}", [P, 2 * S]) for z in range(2)]
    GH, GD, G6 = (sb(n, [P, 2 * S]) for n in ("g_half", "g_full", "g_sixth"))
    EA, EB, EC, ED, C6, FB = (sb(n, [P, 2 * S]) for n in ("ea", "eb", "ec", "ed", "c6", "fb"))
    CH_, CD = ([sb(f"drive_{n}{z}", [P, 2 * S]) for z in range(2)] for n in ("half", "full"))
    H = [sb(f"h{z}", [P, S]) for z in range(2)]
    HX = sb("h_parts", [P, K, 2 * B], F16)
    GI = sb("gi", [P, CH, 4 * S])
    S1, S2, RZ = (sb(n, [P, 3 * S]) for n in ("s1", "s2", "rz"))
    M1, M2, NN, OMZ, ON, ZH = (sb(n, [P, S]) for n in ("m1", "m2", "nn", "one_minus_z", "on", "zh"))
    XH = [sb(f"x1_{n}", [P, K, CH * B], F16) for n in ("hi", "lo")]
    warm = sb("warm", [P, 2])

    PL = [[ps(f"osc{i}{h}", [P, 512]) for h in "ab"] for i in range(2)]
    PG = ps("gates", [P, 512])
    PI = [ps(f"gi{i}", [P, 512]) for i in range(3)]

    NAMES = ["mm_done", "g6_done", "f_done", "cd_ready", "ch_ready", "fb_ready", "gi_mm", "gi_done", "zh_done", "u_done", "q_raw", "q_ready", "hi_ready", "t32_ready", "lo_ready", "sq_ready",
             "w3_done", "pre_ready", "g_done", "a_done", "p_raw", "p_ready",
             "drive_ready", "e_done",
             "gates_done", "s1_done", "s2_ready", "rz_ready", "m1_done", "m2_ready", "nn_ready",
             "on_done", "h_ready", "hhi_done", "hx_ready", "x2_done", "x1_done"]
    sets = [{n: sem(f"{n}_{z}") for n in NAMES} for z in range(2)]
    for z in range(2):
        nums = [sets[z][n].num for n in NAMES]
        assert nums == list(range(nums[0], nums[0] + len(NAMES))), nums
    ranges = [range(sets[z][NAMES[0]].num, sets[z][NAMES[-1]].num + 1) for z in range(2)]
    loaded, staged, w_free, wdone = sem("loaded"), sem("staged"), sem("w_free"), sem("wdone")
    xload, init = sem("xload"), sem("init")
    xs_done = sem("xs_done")
    pool_passed, pe_passed = sem("pool_passed"), sem("pe_passed")
    gib_done = sem("gib_done")

    def at(t, width=S, off=0):
        return XT[:, bass.ds((t + 1) * S + off, width)]

    def kcols(tile, a, b):
        return tile[:, a * B:b * B]

    half = [(0, K // 2), (K // 2, K)]
    HB = K // 2

    def pe_osc(z, s, t0=0):
        c = sets[z]
        first = [True, True]

        def mm(m, k, w, cols, last=False):
            h = m // HB
            col = (m - h * HB) * 2 * B
            r = nc.tensor.matmul(PL[s % 2][h][:, col:col + cols], w[:, k, m * P:(m + 1) * P], TX[s % 2][:, k, 0:cols],
                                 start=first[h], stop=last, skip_group_check=True)
            first[h] = False
            return r
        for i, (a, b) in enumerate(half):
            nc.tensor.wait_ge(c["hi_ready"], 2 * s + 1 + i)
            for k in range(a, b):
                for m in range(K):
                    mm(m, k, C[1], B)
        nc.tensor.wait_ge(c["lo_ready"], s + 1)
        for a, b in half:
            for m in range(a, b):
                for k in range(K):
                    r = mm(m, k, C[0], 2 * B, last=(k == K - 1 and m == b - 1))
            r.then_inc(c["mm_done"], 1)

    gru_list = [(m, k, w) for w in (1, 0) for m in range(G3) for k in range(K)]

    def pe_gru(z, lo, hi):
        c = sets[z]
        if lo == 0:
            nc.tensor.wait_ge(c["hx_ready"], 1)
        for n in range(lo, hi):
            m, k, w = gru_list[n]
            r = nc.tensor.matmul(PG[:, m * 8:m * 8 + 8], WH[w][:, k, m * P:(m + 1) * P], HX[:, k, :],
                                 start=(n == 0), stop=(n == len(gru_list) - 1), skip_group_check=True)
        if hi == len(gru_list):
            r.then_inc(c["gates_done"], 1)

    def pe_gates_in(z, n, xs):
        c = sets[z]
        if n == 0:
            nc.tensor.wait_ge(xs_done, xs)
        for m in range(4 * n, 4 * n + 4):
            for w, x in ((0, 0), (0, 1), (1, 0)):
                for k in range(K):
                    r = nc.tensor.matmul(PI[n][:, (m % 4) * CH * B:(m % 4 + 1) * CH * B], WI[w][:, k, m * P:(m + 1) * P],
                                         XH[x][:, k, :], start=(w == x == k == 0), stop=(w == 1 and k == K - 1))
        r.then_inc(c["gi_mm"], 1)

    def pe_step(z, osc, gru, xs=None):
        if osc:
            for s in range(4):
                pe_osc(z, s)
                if s < 3:
                    if xs is not None:
                        pe_gates_in(z, s, xs)
                    if gru:
                        pe_gru(z, 32 * s, 32 * s + 32)
        else:
            for n in range(3 if xs is not None else 0):
                pe_gates_in(z, n, xs)
            pe_gru(z, 0, 96)
            nc.tensor.wait_ge(sets[z]["s2_ready"], 1)
            nc.tensor.sem_inc(pe_passed, 1)

    def gru_candidate(z):
        nc.scalar.wait_ge(sets[z]["m2_ready"], 1)
        nc.scalar.activation(NN[:, :], M2[:, :], ACT.Tanh).then_inc(sets[z]["nn_ready"], 1)

    def gates_in(z, n):
        c = sets[z]
        nc.scalar.wait_ge(c["gi_mm"], n + 1)
        for m in range(4 * n, 4 * n + 4):
            a = m * B if m < 2 * K else 3 * S + (m - 2 * K) * B
            pi = PI[n][:, (m % 4) * CH * B:(m % 4 + 1) * CH * B].rearrange("p (t b) -> p t b", b=B)
            r = nc.scalar.activation(GI[:, :, a:a + B], pi, ACT.Identity, bias=gib[:, m:m + 1], scale=1 / WSCALE)
        if n == 2:
            r.then_inc(c["gi_done"], 1)

    def act_step(z, osc, gru, xs=None):
        c, prev = sets[z], sets[1 - z]
        for s in range(4):
            if osc:
                q = SQP[s][z]
                for i, (a, b) in enumerate(half):
                    if s == 0:
                        nc.scalar.wait_ge(prev["q_ready"], 7 + i)
                    else:
                        nc.scalar.wait_ge(c["q_ready"], 2 * s - 1 + i)
                    nc.scalar.activation(TX[s % 2][:, a:b, 0:B], kcols(q, a, b).rearrange("p (k b) -> p k b", b=B),
                                         ACT.Tanh).then_inc(c["hi_ready"], 1)
                nc.scalar.activation(T32[:, :], q[:, 0:S], ACT.Tanh).then_inc(c["t32_ready"], 1)
                nc.scalar.activation(SQ[:, :], q[:, 0:S], ACT.Square,
                                     scale=(STEP[s] / 3.0) ** 0.5).then_inc(c["sq_ready"], 1)
                if s == 0:
                    nc.scalar.wait_ge(prev["drive_ready"], 1)
                    nc.scalar.mul(CD[z][:, :], DBX[z][:, :], STEP[2]).then_inc(c["cd_ready"], 1)
                    nc.scalar.mul(C6[:, :], DBX[z][:, :], 3 * STEP[3]).then_inc(c["cd_ready"], 1)
                if s == 2:
                    nc.scalar.wait_ge(c["e_done"], 4)
                    nc.scalar.mul(FB[:, :], ED[:, :], 1 / 3.0).then_inc(c["fb_ready"], 1)
                    nc.scalar.wait_ge(c["drive_ready"], 1)
                    nc.scalar.mul(CH_[1 - z][:, :], DBX[1 - z][:, :], STEP[0]).then_inc(c["ch_ready"], 1)
            if xs is not None and s < 3:
                gates_in(z, s)
            if gru and s == 3:
                nc.scalar.wait_ge(c["s2_ready"], 1)
                nc.scalar.activation(RZ[:, 0:2 * S], S2[:, 0:2 * S], ACT.Sigmoid).then_inc(c["rz_ready"], 1)
                nc.scalar.wait_ge(c["rz_ready"], 1)
                nc.scalar.activation(OMZ[:, :], RZ[:, S:2 * S], ACT.Copy, scale=-1.0, bias=1.0)
                gru_candidate(z)

    def pool_step(z, t, j, osc, gru):
        c, prev = sets[z], sets[1 - z]
        j_is_zero = isinstance(j, int) and j == 0
        first = isinstance(t, int) and t == 0
        st = [SQP[s][z] for s in range(4)]
        add = lambda o, a, b, op=ALU.add: nc.gpsimd.tensor_tensor(o, a, b, op)
        if osc:
            nc.gpsimd.wait_ge(prev["p_ready"], 4)
            nc.gpsimd.wait_ge(prev["q_ready"], 8)
            nc.gpsimd.wait_ge(prev["ch_ready"], 1)
            add(GH[:, :], CH_[z][:, :], st[0][:, :]).then_inc(c["g_done"], 1)
            nc.gpsimd.wait_ge(c["cd_ready"], 1)
            add(GD[:, :], CD[z][:, :], st[0][:, :]).then_inc(c["g_done"], 1)
            if not first:
                pool_x1(z, t, j)
        elif j_is_zero:
            nc.gpsimd.wait_ge(prev["q_ready"], 8)
            pool_x1(z, t, j)
        if gru:
            nc.gpsimd.wait_ge(c["h_ready"], 1)
            add(at(t - CH - 1), at(t - CH - 1), H[z][:, :]).then_inc(c["x2_done"], 1)
        if osc:
            nc.gpsimd.wait_ge(c["p_ready"], 1)
            nc.gpsimd.wait_ge(c["q_ready"], 2)
            add(EA[:, :], st[1][:, :], st[0][:, :], ALU.subtract).then_inc(c["e_done"], 1)
            nc.gpsimd.wait_ge(c["e_done"], 1)
            nc.gpsimd.wait_ge(c["cd_ready"], 2)
            add(EB[:, :], EA[:, :], C6[:, :]).then_inc(c["e_done"], 1)
            nc.gpsimd.wait_ge(c["p_ready"], 2)
            nc.gpsimd.wait_ge(c["q_ready"], 4)
            nc.gpsimd.wait_ge(c["e_done"], 2)
            add(EC[:, :], EB[:, :], st[2][:, :]).then_inc(c["e_done"], 1)
            nc.gpsimd.wait_ge(c["e_done"], 3)
            add(ED[:, :], EC[:, :], st[2][:, :]).then_inc(c["e_done"], 1)
            add(DBX[1 - z][:, 0:S], at(t + 1), biasq[:, :]).then_inc(c["drive_ready"], 1)
        if gru:
            nc.gpsimd.wait_ge(c["rz_ready"], 1)
            add(ZH[:, :], RZ[:, S:2 * S], H[z][:, :], ALU.mult).then_inc(c["zh_done"], 1)
        if not osc:
            nc.gpsimd.wait_ge(c["s2_ready"], 1)
            nc.gpsimd.sem_inc(pool_passed, 1)

    def pool_x1(z, t, j):
        c = sets[z]
        jp = CH - 1 if isinstance(j, int) and j == 0 else j - 1
        x1 = at(t - 1).rearrange("p (k b) -> p k b", b=B)
        hi, lo = (XH[n][:, :, ds(jp * B, B)] for n in range(2))
        nc.gpsimd.tensor_tensor(at(t - 1), at(t - 1), SQP[0][z][:, 0:S], ALU.add).then_inc(c["x1_done"], 1)
        nc.gpsimd.wait_ge(c["x1_done"], 1)
        nc.gpsimd.tensor_copy(hi, x1).then_inc(c["x1_done"], 1)
        nc.gpsimd.wait_ge(c["x1_done"], 2)
        nc.gpsimd.tensor_tensor(lo, x1, hi, ALU.subtract).then_inc(xs_done, 1)

    def gru_update(z):
        c, prev = sets[z], sets[1 - z]
        v = lambda x: x[:, :].rearrange("p (k b) -> p k b", b=B)
        nc.vector.wait_ge(prev["zh_done"], 1)
        nc.vector.wait_ge(prev["on_done"], 1)
        nc.vector.tensor_tensor(HX[:, :, 0:B], v(ON), v(ZH), ALU.add).then_inc(c["hhi_done"], 1)
        nc.vector.tensor_tensor(H[z][:, :], ON[:, :], ZH[:, :], ALU.add).then_inc(c["h_ready"], 1)
        yield
        nc.vector.wait_ge(c["h_ready"], 1)
        nc.vector.tensor_tensor(HX[:, :, B:2 * B], v(H[z]), HX[:, :, 0:B], ALU.subtract).then_inc(c["hx_ready"], 1)
        yield

    def gru_gates(z, j, xs):
        c = sets[z]
        gi = lambda a, b: GI[:, ds(j, 1), a * S:b * S].rearrange("p o c -> p (o c)")
        pg = PG[:, 0:G3 * 8].rearrange("p (m c) -> p m c", c=8)
        v3 = lambda x: x.rearrange("p (m b) -> p m b", b=B)
        if xs is not None:
            nc.vector.wait_ge(c["gi_done"], 1)
        nc.vector.wait_ge(c["gates_done"], 1)
        nc.vector.scalar_tensor_tensor(v3(S1[:, :]), pg[:, :, 0:B], 1 / WSCALE, v3(gi(0, 3)),
                                       ALU.mult, ALU.add).then_inc(c["s1_done"], 1)
        yield
        nc.vector.wait_ge(c["s1_done"], 1)
        nc.vector.scalar_tensor_tensor(v3(S2[:, :]), pg[:, :, B:2 * B], 1 / WSCALE, v3(S1[:, :]),
                                       ALU.mult, ALU.add).then_inc(c["s2_ready"], 1)
        yield
        nc.vector.wait_ge(c["rz_ready"], 1)
        nc.vector.tensor_tensor(M1[:, :], RZ[:, 0:S], S2[:, 2 * S:3 * S], ALU.mult).then_inc(c["m1_done"], 1)
        yield
        nc.vector.wait_ge(c["m1_done"], 1)
        nc.vector.tensor_tensor(M2[:, :], M1[:, :], gi(3, 4), ALU.add).then_inc(c["m2_ready"], 1)
        yield
        nc.vector.wait_ge(c["nn_ready"], 1)
        nc.vector.tensor_tensor(ON[:, :], OMZ[:, :], NN[:, :], ALU.mult).then_inc(c["on_done"], 1)
        yield

    def dve_step(z, j, osc, gru, xs=None):
        c, prev = sets[z], sets[1 - z]
        update, gates = gru_update(z), gru_gates(z, j, xs)
        if not osc:
            for _ in update:
                pass
            nc.vector.wait_ge(c["gates_done"], 1)
            nc.vector.wait_ge(c["x2_done"], 1)
            nc.vector.sem_clear(ranges[1 - z])
            for _ in gates:
                pass
            return

        def gru_part(work):
            if gru:
                next(work)
        st = [SQP[s][z] for s in range(4)]
        nxt = SQP[0][1 - z]
        stt = nc.vector.scalar_tensor_tensor
        for s in range(4):
            h = STEP[s]
            g = (GH, GH, GD, G6)[s]
            stt(AP_[:, :], st[s][:, S:2 * S], -BETA, st[s][:, 0:S], ALU.mult, ALU.add).then_inc(c["a_done"], 1)
            if s == 3:
                nc.vector.wait_ge(c["fb_ready"], 1)
                stt(G6[:, :], st[3][:, :], 1 / 3.0, FB[:, :], ALU.mult, ALU.add).then_inc(c["g6_done"], 1)

            def without_product():
                stt(FS[:, :], st[s][:, S:2 * S], -h, g[:, 0:S], ALU.mult, ALU.add).then_inc(c["f_done"], 1)

            def tanh_low():
                nc.vector.wait_ge(c["t32_ready"], s + 1)
                nc.vector.tensor_tensor(TX[s % 2][:, :, B:2 * B], T32[:, :].rearrange("p (k b) -> p k b", b=B),
                                        TX[s % 2][:, :, 0:B], ALU.subtract).then_inc(c["lo_ready"], 1)

            def cube():
                nc.vector.wait_ge(c["sq_ready"], s + 1)
                stt(W3[:, :], SQ[:, :], h, st[s][:, 0:S], ALU.subtract, ALU.mult).then_inc(c["w3_done"], 1)
            if s == 0:
                gru_part(update)
                tanh_low()
                gru_part(update)
                cube()
                nc.vector.wait_ge(c["g_done"], 1)
                without_product()
            elif s == 3:
                gru_part(gates)
                tanh_low()
                gru_part(gates)
                nc.vector.wait_ge(c["g6_done"], 1)
                without_product()
                cube()
            else:
                if s == 2:
                    nc.vector.wait_ge(c["g_done"], 2)
                without_product()
                tanh_low()
                cube()
            nc.vector.wait_ge(c["a_done"], s + 1)
            if s < 3:
                stt(st[s + 1][:, S:2 * S], AP_[:, :], h * EPS_P, g[:, S:2 * S],
                    ALU.mult, ALU.add).then_inc(c["p_ready"], 1)
            else:
                stt(raw[:, S:2 * S], AP_[:, :], h * EPS_P, g[:, S:2 * S], ALU.mult, ALU.add).then_inc(c["p_raw"], 1)
            if s == 3:
                gru_part(gates)
            nc.vector.wait_ge(c["f_done"], s + 1)
            nc.vector.wait_ge(c["w3_done"], s + 1)
            nc.vector.tensor_tensor(PRE[:, :], FS[:, :], W3[:, :], ALU.subtract).then_inc(c["pre_ready"], 1)
            if s == 2:
                nc.vector.wait_ge(c["e_done"], 4)
                nc.vector.sem_clear(ranges[1 - z])
            if s == 3:
                nc.vector.wait_ge(c["p_raw"], 1)
                nc.vector.tensor_scalar(nxt[:, S:2 * S], raw[:, S:2 * S], CLAMP, -CLAMP, ALU.min,
                                        ALU.max).then_inc(c["p_ready"], 1)
                gru_part(gates)
            out = raw if s == 3 else st[s + 1]
            pv = [PL[s % 2][i][:, 0:HB * 2 * B].rearrange("p (m c) -> p m c", c=2 * B) for i in range(2)]
            k3 = lambda x, i: kcols(x, *half[i]).rearrange("p (k b) -> p k b", b=B)

            def with_high(i):
                if i == 0:
                    nc.vector.wait_ge(c["pre_ready"], s + 1)
                nc.vector.wait_ge(c["mm_done"], 2 * s + 1 + i)
                stt(k3(U, i), pv[i][:, :, 0:B], h / WSCALE, k3(PRE, i), ALU.mult, ALU.add).then_inc(c["u_done"], 1)

            def with_low(i):
                nc.vector.wait_ge(c["u_done"], 2 * s + 1 + i)
                r = stt(k3(out, i), pv[i][:, :, B:2 * B], h / WSCALE, k3(U, i), ALU.mult, ALU.add)
                r.then_inc(c["q_raw" if s == 3 else "q_ready"], 1)

            def clip(i):
                nc.vector.wait_ge(c["q_raw"], 1 + i)
                nc.vector.tensor_scalar(kcols(nxt, *half[i]), kcols(raw, *half[i]), CLAMP, -CLAMP, ALU.min,
                                        ALU.max).then_inc(c["q_ready"], 1)
            with_high(0)
            if s < 3:
                with_low(0)
                with_high(1)
                with_low(1)
            else:
                with_high(1)
                with_low(0)
                with_low(1)
                gru_part(gates)
                clip(0)
                clip(1)
            nc.vector.wait_ge(c["q_ready"], 2 * s + 2)

    block = phase_block

    def chunks(eng, step):
        def chunk(c, osc, gru):
            for i in range(UN):
                step(i % 2, c, i, osc, gru, c if gru and i == 0 else None)
            with eng.Fori(1, CH // UN) as j:
                for i in range(UN):
                    step(i % 2, c, j * UN + i, osc, gru, None)
        chunk(0, True, False)
        yield
        with eng.Fori(1, NCH) as c:
            chunk(c, True, True)
        chunk(NCH, False, True)
        yield

    @block.sync
    def _(sp):
        sp.dma_start(XT[:, S:(T + 1) * S], x).then_inc(xload, 16)
        for n, (tile, src) in enumerate([(biasq, bias0), (gib, b_ih), (bhh, b_hh), (SQP[0][0][:, 0:S], q0),
                                         (SQP[0][0][:, S:2 * S], q0), (ZH, q0)]):
            sp.dma_start(tile[:, :] if n < 3 or n == 5 else tile, src).then_inc(loaded, 16)
        for j in range(CH):
            sp.dma_start(GI[:, j, 2 * S:3 * S], hn_bias).then_inc(loaded, 16)
        for n, (w, cols) in enumerate([(coupling, D), (w_ih, 3 * D), (w_hh, 3 * D)]):
            if n:
                sp.wait_ge(w_free, n)
            sp.dma_start(stage_w[:, :, 0:cols], w.rearrange("(k p) n -> p k n", p=P)).then_inc(staged, 16)

    @block.tensor
    def _(pe):
        pe.wait_ge(wdone, 3)

        for _ in chunks(pe, lambda z, c, j, o, g, x: pe_step(z, o, g, None if x is None else x * CH)):
            pass

    @block.scalar
    def _(act):
        nc.scalar.wait_ge(init, 1)
        nc.scalar.activation(warm[:, 1:2], warm[:, 0:1], ACT.Sigmoid)
        nc.scalar.wait_ge(sets[1]["drive_ready"], 1)
        nc.scalar.mul(CH_[0][:, :], DBX[0][:, :], STEP[0]).then_inc(sets[1]["ch_ready"], 1)
        for _ in chunks(act, lambda z, c, j, o, g, x: act_step(z, o, g, x)):
            pass

    @block.gpsimd
    def _(pool):
        pool.wait_ge(xload, 16)
        pool.wait_ge(loaded, 16 * (6 + CH))
        pool.wait_ge(init, 2)

        nc.gpsimd.tensor_tensor(DBX[0][:, 0:S], at(0), biasq[:, :], ALU.add).then_inc(sets[1]["drive_ready"], 1)
        for _ in chunks(pool, lambda z, c, j, o, g, x: pool_step(z, c * CH + j, j, o, g)):
            pass

    @block.vector
    def _(dve):
        nc.vector.memset(warm[:, :], 0.0).then_inc(init, 1)
        nc.vector.memset(DBX[0][:, S:2 * S], EPS_P * ALPHA)
        nc.vector.memset(DBX[1][:, S:2 * S], EPS_P * ALPHA)
        nc.vector.memset(XT[:, 0:S], 0.0)
        nc.vector.memset(XT[:, (T + 1) * S:], 0.0)
        nc.vector.memset(ON[:, :], 0.0).then_inc(init, 1)
        dve.wait_ge(init, 2)
        for n, (w, cols) in enumerate([(C, D), (WI, 3 * D), (WH, 3 * D)]):
            dve.wait_ge(staged, 16 * (n + 1))
            nc.vector.tensor_scalar(w[0][:, :, :], stage_w[:, :, 0:cols], WSCALE, None, ALU.mult).then_inc(wdone, 1)
            dve.wait_ge(wdone, n + 1)
            for k in range(K):
                r = nc.vector.scalar_tensor_tensor(w[1][:, k, :], stage_w[:, k, 0:cols], WSCALE, w[0][:, k, :],
                                                   ALU.mult, ALU.subtract)
            r.then_inc(w_free, 1)
        dve.wait_ge(w_free, 3)
        dve.wait_ge(loaded, 16 * (6 + CH))
        nc.vector.tensor_tensor(gib[:, 0:2 * K], gib[:, 0:2 * K], bhh[:, 0:2 * K], ALU.add).then_inc(gib_done, 1)
        dve.wait_ge(gib_done, 1)
        dve.sem_inc(sets[1]["p_ready"], 4)
        dve.sem_inc(sets[1]["q_ready"], 8)

        for n, _ in enumerate(chunks(dve, lambda z, c, j, o, g, x: dve_step(z, j, o, g, x))):
            if n == 0:
                dve.sem_inc(sets[1]["on_done"], 1)
                dve.sem_inc(sets[1]["zh_done"], 1)
        for _ in gru_update(0):
            pass
        dve.wait_ge(sets[0]["h_ready"], 1)
        dve.wait_ge(sets[1]["x2_done"], 1)
        nc.vector.tensor_tensor(at(T - 1), at(T - 1), H[0][:, :], ALU.add)

def layer2(nc, ctx, sems, phase_block, XT, cond, w_emb, b_emb, g_norm, w_qkv, g_qk, w_out):
    def sb(name, shape, dt=F32):
        return ctx.enter_context(nc.sbuf_tensor("l2_" + name, shape, dt))

    def sem(name):
        return sems.take(nc, "l2_" + name)

    HEADS, DH = 16, 32
    XV = XT[:, S:(T + 1) * S].rearrange("p (t k b) -> p k b t", k=K, b=B)
    WQKV, WO = sb("w_qkv", [P, K, 3 * D]), sb("w_out", [P, K, D])
    ones_d, ones_h, ident = sb("ones_d", [P, P]), sb("ones_h", [P, P]), sb("ident", [P, P])
    eps, gqk, bemb, gn = sb("eps", [P, 1]), sb("gqk", [P, 2]), sb("bemb", [P, 2 * K]), sb("gn", [P, K])
    WE, CT = sb("w_emb", [P, K, 2 * D]), sb("cond", [P, K, B])
    MOD = sb("mod", [P, 2 * K, B])
    SQX, XN, TMP = sb("sqx", [P, K, T]), sb("xn", [P, K, T]), sb("tmp", [P, K, T])
    LNT, RSTD = sb("lnt", [P, T]), sb("rstd", [P, T])
    SQH, LNH, RH = ([sb(f"{n}{i}", [P, T]) for i in range(2)] for n in ("sqh", "lnh", "rh"))
    QK, V = sb("qk", [P, 2 * K, T]), sb("v", [P, K, D])
    PR = [sb(f"prob{i}", [P, T]) for i in range(4)]
    PT = [sb(f"probT{i}", [P, K, T]) for i in range(2)]
    NM, RSUM, RINV = (sb(n, [P, 4]) for n in ("negmax", "rowsum", "rowinv"))
    OT = sb("oT", [P, K, T])
    YS = [sb(f"ys{i}", [P, T]) for i in range(2)]

    PA = [ctx.enter_context(nc.psum_tensor(f"l2_pa{i}", [P, T], F32)) for i in range(4)]
    PB = [ctx.enter_context(nc.psum_tensor(f"l2_pb{i}", [P, T], F32)) for i in range(2)]
    PO = [ctx.enter_context(nc.psum_tensor(f"l2_po{i}", [P, T], F32)) for i in range(2)]

    loaded, consts, emb_mm, mod_done, mod_raw = (sem(n) for n in ("loaded", "consts", "emb_mm", "mod_done", "mod_raw"))
    sqx, ms, lnt, rstd, xt, xn = (sem(n) for n in ("sqx", "ms", "lnt", "rstd", "xt", "xn"))
    qk_mm, sqh, nh_mm, lnh, rh, qn, v_mm, v_done = (
        sem(n) for n in ("qk_mm", "sqh", "nh_mm", "lnh", "rh", "qn", "v_mm", "v_done"))
    sc, nmax, ex, rinv, pr, tr, ev, o_mm, o_done = (
        sem(n) for n in ("sc", "nmax", "ex", "rinv", "pr", "tr", "ev", "o_mm", "o_done"))
    y_mm, ys, x_done, ident_done = (sem(n) for n in ("y_mm", "ys", "x_done", "ident_done"))
    NU = HEADS * K

    block = phase_block

    @block.sync
    def _(sp):
        for tile, src in ((CT[:, :, :], cond), (WE[:, :, :], w_emb.rearrange("(k p) n -> p k n", p=P)),
                          (bemb[:, :], b_emb), (gn[:, :], g_norm), (gqk[:, :], g_qk),
                          (WQKV[:, :, :], w_qkv.rearrange("(k p) n -> p k n", p=P)),
                          (WO[:, :, :], w_out.rearrange("(k p) n -> p k n", p=P))):
            sp.dma_start(tile, src).then_inc(loaded, 16)

    @block.gpsimd
    def _(pool):
        nc.gpsimd.memset(ident[:, :], 0.0).then_inc(ident_done, 1)
        pool.wait_ge(ident_done, 1)
        nc.gpsimd.affine_select(out=ident[:, :], in_=ident[:, :], compare_op=ALU.not_equal, fill=1.0, base=0,
                                pattern=[[-1, P]], channel_multiplier=1).then_inc(ident_done, 1)

    @block.tensor
    def _(pe):
        mm = nc.tensor.matmul
        pe.wait_ge(loaded, 16 * 7)
        for m in range(2 * K):
            for k in range(K):
                r = mm(PA[0][:, m * B:(m + 1) * B], WE[:, k, m * P:(m + 1) * P], CT[:, k, :],
                       start=(k == 0), stop=(k == K - 1))
        r.then_inc(emb_mm, 1)
        pe.wait_ge(consts, 3)
        pe.wait_ge(ident_done, 2)
        pe.wait_ge(mod_done, 1)
        with pe.Fori(0, B) as b:
            for k in range(K):
                pe.wait_ge(sqx, b * K + k + 1)
                r = mm(PB[0][:, :], ones_d[:, :], SQX[:, k, :], start=(k == 0), stop=(k == K - 1))
            r.then_inc(ms, 1)
            pe.wait_ge(xn, (b + 1) * K)

            def head_norm(c):
                pe.wait_ge(sqh, b * 2 * K + c + 1)
                mm(PB[c % 2][:, :], ones_h[:, :], SQH[c % 2][:, :], start=True, stop=True).then_inc(nh_mm, 1)
            for c in range(2 * K):
                if c >= 2:
                    pe.wait_ge(qn, b * 2 * K + c - 1)
                for k in range(K):
                    r = mm(PA[c % 2][:, :], WQKV[:, k, c * P:(c + 1) * P], XN[:, k, :], start=(k == 0), stop=(k == K - 1))
                r.then_inc(qk_mm, 1)
                if c >= 1:
                    head_norm(c - 1)
            head_norm(2 * K - 1)
            for tc in range(K):
                if tc >= 2:
                    pe.wait_ge(v_done, b * K + tc - 1)
                for k in range(K):
                    r = mm(PO[tc % 2][:, :], XN[:, k, tc * P:(tc + 1) * P], WQKV[:, k, 2 * D:3 * D],
                           start=(k == 0), stop=(k == K - 1))
                r.then_inc(v_mm, 1)
            pe.wait_ge(qn, (b + 1) * 2 * K)
            pe.wait_ge(v_done, (b + 1) * K)

            def scores(n):
                h, i = divmod(n, K)
                c, j = divmod(h, 4)
                r0 = 32 * j
                if n >= 4:
                    pe.wait_ge(ex, b * NU + n - 3)
                mm(PA[n % 4][:, :], QK[r0:r0 + 32, c, i * P:(i + 1) * P], QK[r0:r0 + 32, K + c, :],
                   start=True, stop=True, tile_position=(r0, 0)).then_inc(sc, 1)

            def transposes(n):
                pe.wait_ge(pr, b * NU + n + 1)
                if n >= 2:
                    pe.wait_ge(ev, b * NU + n - 1)
                for kc in range(K):
                    r = nc.tensor.transpose(PB[n % 2][:, kc * P:(kc + 1) * P], PR[n % 4][:, kc * P:(kc + 1) * P],
                                            ident[:, :])
                r.then_inc(tr, 1)

            def values(h):
                c, j = divmod(h, 4)
                pe.wait_ge(ev, b * NU + (h + 1) * K)
                if j == 0 and c >= 2:
                    pe.wait_ge(o_done, b * K + c - 1)
                for kc in range(K):
                    r = mm(PO[c % 2][32 * j:32 * j + 32, :], V[:, kc, h * DH:(h + 1) * DH], PT[h % 2][:, kc, :],
                           start=(kc == 0), stop=(kc == K - 1), tile_position=(0, 32 * j))
                r.then_inc(o_mm, 1)
            scores(0)
            scores(1)
            for n in range(NU):
                if n + 2 < NU:
                    scores(n + 2)
                transposes(n)
                if n % K == 1 and n > K:
                    values(n // K - 1)
            values(HEADS - 1)
            pe.wait_ge(o_done, (b + 1) * K)
            for m in range(K):
                if m >= 2:
                    pe.wait_ge(ys, b * K + m - 1)
                for k in range(K):
                    r = mm(PA[m % 2][:, :], WO[:, k, m * P:(m + 1) * P], OT[:, k, :], start=(k == 0), stop=(k == K - 1))
                r.then_inc(y_mm, 1)
            pe.wait_ge(ys, (b + 1) * K)

    @block.scalar
    def _(act):
        act.wait_ge(consts, 3)
        with act.Fori(0, B) as b:
            for k in range(K):
                nc.scalar.activation(SQX[:, k, :], XV[:, k, bass.ds(b, 1), :].rearrange("p o t -> p (o t)"),
                                     ACT.Square).then_inc(sqx, 1)
            act.wait_ge(ms, b + 1)
            nc.scalar.activation(LNT[:, :], PB[0][:, :], ACT.Sqrt, bias=eps[:, :]).then_inc(lnt, 1)

            def head_rstd(c):
                act.wait_ge(nh_mm, b * 2 * K + c + 1)
                nc.scalar.activation(LNH[c % 2][:, :], PB[c % 2][:, :], ACT.Sqrt, bias=eps[:, :]).then_inc(lnh, 1)
            for c in range(2 * K):
                act.wait_ge(qk_mm, b * 2 * K + c + 1)
                nc.scalar.activation(SQH[c % 2][:, :], PA[c % 2][:, :], ACT.Square).then_inc(sqh, 1)
                if c >= 1:
                    head_rstd(c - 1)
            head_rstd(2 * K - 1)
            for tc in range(K):
                act.wait_ge(v_mm, b * K + tc + 1)
                nc.scalar.copy(V[:, tc, :], PO[tc % 2][:, :]).then_inc(v_done, 1)

            def evacuate(n):
                h, i = divmod(n, K)
                act.wait_ge(tr, b * NU + n + 1)
                if i == 0 and h >= 2:
                    act.wait_ge(o_mm, b * HEADS + h - 1)
                nc.scalar.copy(PT[h % 2][:, :, i * P:(i + 1) * P],
                               PB[n % 2][:, :].rearrange("p (k q) -> p k q", k=K)).then_inc(ev, 1)
            for n in range(NU):
                act.wait_ge(nmax, b * NU + n + 1)
                j = n % 4
                nc.scalar.activation(PR[j][:, :], PA[j][:, :], ACT.Exp, bias=NM[:, j:j + 1],
                                     accum_out=RSUM[:, j:j + 1]).then_inc(ex, 1)
                if n >= 2:
                    evacuate(n - 2)
            evacuate(NU - 2)
            evacuate(NU - 1)
            act.wait_ge(x_done, (b + 1) * K)

    @block.vector
    def _(dve):
        stt, tt, ts = nc.vector.scalar_tensor_tensor, nc.vector.tensor_tensor, nc.vector.tensor_scalar
        nc.vector.memset(ones_d[:, :], 1.0 / D)
        nc.vector.memset(eps[:, :], 1e-6)
        nc.vector.memset(ones_h[:, :], 0.0).then_inc(consts, 1)
        dve.wait_ge(consts, 1)
        for j in range(4):
            r = nc.vector.memset(ones_h[32 * j:32 * j + 32, 32 * j:32 * j + 32], 1.0 / DH)
        r.then_inc(consts, 1)
        dve.wait_ge(loaded, 16 * 7)
        dve.wait_ge(emb_mm, 1)
        tt(MOD[:, :, :], PA[0][:, 0:2 * K * B].rearrange("p (m b) -> p m b", b=B),
           bemb[:, :].unsqueeze(2).to_broadcast([P, 2 * K, B]), ALU.add).then_inc(mod_raw, 1)
        dve.wait_ge(mod_raw, 1)
        stt(MOD[:, 0:K, :], MOD[:, 0:K, :], 1.0, gn[:, :].unsqueeze(2).to_broadcast([P, K, B]), ALU.add,
            ALU.mult).then_inc(mod_done, 1)
        ts(gqk[:, 0:1], gqk[:, 0:1], DH ** -0.5, None, ALU.mult).then_inc(consts, 1)
        dve.wait_ge(consts, 3)
        dve.wait_ge(mod_done, 1)
        with dve.Fori(0, B) as b:
            xb = lambda k: XV[:, k, bass.ds(b, 1), :].rearrange("p o t -> p (o t)")
            dve.wait_ge(lnt, b + 1)
            nc.vector.reciprocal(RSTD[:, :], LNT[:, :]).then_inc(rstd, 1)
            dve.wait_ge(rstd, b + 1)
            for k in range(K):
                tt(TMP[:, k, :], xb(k), RSTD[:, :], ALU.mult).then_inc(xt, 1)
            for k in range(K):
                dve.wait_ge(xt, b * K + k + 1)
                ts(XN[:, k, :], TMP[:, k, :], MOD[:, k, bass.ds(b, 1)], MOD[:, K + k, bass.ds(b, 1)],
                   ALU.mult, ALU.add).then_inc(xn, 1)
            for c in range(2 * K):
                dve.wait_ge(lnh, b * 2 * K + c + 1)
                nc.vector.reciprocal(RH[c % 2][:, :], LNH[c % 2][:, :]).then_inc(rh, 1)
                dve.wait_ge(rh, b * 2 * K + c + 1)
                stt(QK[:, c, :], PA[c % 2][:, :], gqk[:, c // K:c // K + 1], RH[c % 2][:, :], ALU.mult,
                    ALU.mult).then_inc(qn, 1)

            def normalise(n):
                dve.wait_ge(ex, b * NU + n + 1)
                j = n % 4
                nc.vector.reciprocal(RINV[:, j:j + 1], RSUM[:, j:j + 1]).then_inc(rinv, 1)
                dve.wait_ge(rinv, b * NU + n + 1)
                ts(PR[j][:, :], PR[j][:, :], RINV[:, j:j + 1], None, ALU.mult).then_inc(pr, 1)
            for n in range(NU):
                dve.wait_ge(sc, b * NU + n + 1)
                nc.vector.tensor_reduce(NM[:, n % 4:n % 4 + 1], PA[n % 4][:, :], AX.X, ALU.max,
                                        negate=True).then_inc(nmax, 1)
                if n >= 1:
                    normalise(n - 1)
                if n % 16 == 8 and n > 16:
                    c = n // 16 - 1
                    dve.wait_ge(o_mm, b * HEADS + 4 * (c + 1))
                    nc.vector.tensor_copy(OT[:, c, :], PO[c % 2][:, :]).then_inc(o_done, 1)
            normalise(NU - 1)
            dve.wait_ge(o_mm, (b + 1) * HEADS)
            nc.vector.tensor_copy(OT[:, K - 1, :], PO[(K - 1) % 2][:, :]).then_inc(o_done, 1)
            for m in range(K):
                dve.wait_ge(y_mm, b * K + m + 1)
                tt(YS[m % 2][:, :], PA[m % 2][:, :], OT[:, m, :], ALU.add).then_inc(ys, 1)
                dve.wait_ge(ys, b * K + m + 1)
                tt(xb(m), xb(m), YS[m % 2][:, :], ALU.add).then_inc(x_done, 1)

def layer3(nc, ctx, sems, XT, cond, ada_w, ada_b, qkv_w, qkv_b, out_w, out_b, w1, b1, w2, b2, out):
    def sb(name, shape, dt=F32, c=ctx):
        return c.enter_context(nc.sbuf_tensor("l3_" + name, shape, dt))

    def sem(name):
        return sems.take(nc, "l3_" + name)

    HEADS, DH, F = 16, 128, 4 * D // P
    SHIFT1, SCALE1, GATE1, SHIFT2, SCALE2, GATE2 = (K * n for n in range(6))
    XV = XT[:, S:(T + 1) * S].rearrange("p (t k b) -> p k b t", k=K, b=B)
    ones_d, ident, eps = sb("ones_d", [P, P]), sb("ident", [P, P]), sb("eps", [P, 1])
    MOD = sb("mod", [P, 6 * K, B])
    Y = sb("y", [P, B, K, T])
    ob, bb2, bb1, bqkv = sb("ob", [P, K]), sb("bb2", [P, K]), sb("bb1", [P, F]), sb("bqkv", [P, 3 * HEADS])
    BH = [sb(f"bias_head{i}", [P, 3]) for i in range(2)]
    PA, PB, PO, PY = ([ctx.enter_context(nc.psum_tensor(f"l3_{n}{i}", [P, T], F32)) for i in range(2)]
                      for n in ("pa", "pb", "po", "py"))
    mm = nc.tensor.matmul
    stt, tt, ts = nc.vector.scalar_tensor_tensor, nc.vector.tensor_tensor, nc.vector.tensor_scalar
    ds = bass.ds

    def norm_sems(tag):
        return {n: sem(tag + n) for n in ("mean", "xc", "sqx", "var", "lnt", "rstd", "xt", "xn")}

    def norm_pe(s, it, xin):
        for k in range(K):
            r = mm(PA[0][:, :], ones_d[:, :], xin(k), start=(k == 0), stop=(k == K - 1))
        r.then_inc(s["mean"], 1)
        for k in range(K):
            nc.tensor.wait_ge(s["sqx"], it * K + k + 1)
            r = mm(PB[0][:, :], ones_d[:, :], SQX[:, k, :], start=(k == 0), stop=(k == K - 1))
        r.then_inc(s["var"], 1)

    def norm_act(s, it):
        for k in range(K):
            nc.scalar.wait_ge(s["xc"], it * K + k + 1)
            nc.scalar.activation(SQX[:, k, :], XC[:, k, :], ACT.Square).then_inc(s["sqx"], 1)
        nc.scalar.wait_ge(s["var"], it + 1)
        nc.scalar.activation(LNT[:, :], PB[0][:, :], ACT.Sqrt, bias=eps[:, :]).then_inc(s["lnt"], 1)

    def norm_dve(s, it, xin, xout, scale, shift, b):
        nc.vector.wait_ge(s["mean"], it + 1)
        for k in range(K):
            tt(XC[:, k, :], xin(k), PA[0][:, :], ALU.subtract).then_inc(s["xc"], 1)
        nc.vector.wait_ge(s["lnt"], it + 1)
        nc.vector.reciprocal(RSTD[:, :], LNT[:, :]).then_inc(s["rstd"], 1)
        nc.vector.wait_ge(s["rstd"], it + 1)
        for k in range(K):
            tt(XC[:, k, :], XC[:, k, :], RSTD[:, :], ALU.mult).then_inc(s["xt"], 1)
        for k in range(K):
            nc.vector.wait_ge(s["xt"], it * K + k + 1)
            ts(xout(k), XC[:, k, :], MOD[:, scale + k, ds(b, 1)], MOD[:, shift + k, ds(b, 1)],
               ALU.mult, ALU.add).then_inc(s["xn"], 1)

    loaded, consts, ident_done, ada_mm, mod_raw, mod_done, y0 = (
        sem(n) for n in ("loaded", "consts", "ident_done", "ada_mm", "mod_raw", "mod_done", "y0"))

    with ExitStack() as c:
        AW, CT, ab = sb("ada_w", [P, K, 6 * D], c=c), sb("cond", [P, K, B], c=c), sb("ada_b", [P, 6 * K], c=c)
        with nc.Block() as block:
            @block.sync
            def _(sp):
                for tile, src in ((CT[:, :, :], cond), (AW[:, :, :], ada_w.rearrange("(k p) n -> p k n", p=P)),
                                  (ab[:, :], ada_b), (ob[:, :], out_b), (bb2[:, :], b2), (bb1[:, :], b1),
                                  (bqkv[:, :], qkv_b)):
                    sp.dma_start(tile, src).then_inc(loaded, 16)

            @block.gpsimd
            def _(pool):
                nc.gpsimd.memset(ident[:, :], 0.0).then_inc(ident_done, 1)
                pool.wait_ge(ident_done, 1)
                nc.gpsimd.affine_select(out=ident[:, :], in_=ident[:, :], compare_op=ALU.not_equal, fill=1.0, base=0,
                                        pattern=[[-1, P]], channel_multiplier=1).then_inc(ident_done, 1)
                nc.gpsimd.memset(Y[:, :, :, :], 0.0).then_inc(y0, 1)

            @block.tensor
            def _(pe):
                pe.wait_ge(loaded, 16 * 7)
                for m in range(6 * K):
                    for k in range(K):
                        r = mm(PA[0][:, m * B:(m + 1) * B], AW[:, k, m * P:(m + 1) * P], CT[:, k, :],
                               start=(k == 0), stop=(k == K - 1))
                r.then_inc(ada_mm, 1)

            @block.vector
            def _(dve):
                nc.vector.memset(ones_d[:, :], 1.0 / D)
                nc.vector.memset(eps[:, :], 1e-6).then_inc(consts, 1)
                dve.wait_ge(loaded, 16 * 7)
                dve.wait_ge(ada_mm, 1)
                tt(MOD[:, :, :], PA[0][:, 0:6 * K * B].rearrange("p (m b) -> p m b", b=B),
                   ab[:, :].unsqueeze(2).to_broadcast([P, 6 * K, B]), ALU.add).then_inc(mod_raw, 1)
                dve.wait_ge(mod_raw, 1)
                for m in (SCALE1, SCALE2):
                    ts(MOD[:, m:m + K, :], MOD[:, m:m + K, :], 1.0, None, ALU.add).then_inc(mod_done, 1)
                ts(bqkv[:, 0:HEADS], bqkv[:, 0:HEADS], DH ** -0.5, None, ALU.mult).then_inc(mod_done, 1)
                dve.wait_ge(mod_done, 3)
                dve.wait_ge(consts, 1)

    with ExitStack() as c:
        X1 = sb("x1", [P, B, K, T], c=c)
        with ExitStack() as cn:
            SQX, XC = sb("sqx", [P, K, T], c=cn), sb("xc", [P, K, T], c=cn)
            LNT, RSTD = sb("lnt", [P, T], c=cn), sb("rstd", [P, T], c=cn)
            s1 = norm_sems("n1_")
            with nc.Block() as block:
                @block.tensor
                def _(pe):
                    for b in range(B):
                        if b:
                            pe.wait_ge(s1["xn"], b * K)
                        norm_pe(s1, b, lambda k: XV[:, k, b, :])

                @block.scalar
                def _(act):
                    for b in range(B):
                        norm_act(s1, b)

                @block.vector
                def _(dve):
                    for b in range(B):
                        norm_dve(s1, b, lambda k: XV[:, k, b, :], lambda k: X1[:, b, k, :], SCALE1, SHIFT1, b)
                    dve.wait_ge(s1["xn"], B * K)

        WQ = [sb(f"wq{i}", [P, K, 3, P], c=c) for i in range(2)]
        WO = [sb(f"wo{i}", [P, D], c=c) for i in range(2)]
        Q, KT, V = ([sb(f"{n}{i}", [P, T], c=c) for i in range(2)] for n in ("q", "kT", "v"))
        O = sb("o", [P, T], c=c)
        PR = [sb(f"prob{i}", [P, T], c=c) for i in range(2)]
        PT = sb("probT", [P, K, T], c=c)
        NM, RSUM, RINV = (sb(n, [P, 2], c=c) for n in ("negmax", "rowsum", "rowinv"))
        (bias_in, qk_mm, qk, v_mm, v_done, sc, nmax, ex, rinv, pr, tr, ev, o_mm, o_done, y_mm, y_done) = (
            sem("a_" + n) for n in ("bias_in", "qk_mm", "qk", "v_mm", "v_done", "sc", "nmax", "ex", "rinv",
                                    "pr", "tr", "ev", "o_mm", "o_done", "y_mm", "y_done"))
        w_in = [sem(f"a_w_in{i}") for i in range(2)]
        NH, NIT = 2 * B, HEADS // 2
        qkv_h = qkv_w.rearrange("(k p) (w h d) -> h p k w d", p=P, w=3, d=DH)
        out_h = out_w.rearrange("(h p) n -> h p n", p=P)

        def wait(eng, s, value):
            if not isinstance(value, int) or value > 0:
                eng.wait_ge(s, value)

        def head_batch(n):
            return n // B % 2, n % B

        def iterations(eng, body):
            body(0, True, False)
            with eng.Fori(1, NIT - 1) as it:
                body(it, False, False)
            body(NIT - 1, False, True)
        with nc.Block() as block:
            @block.sync
            def _(sp):
                def load(it):
                    for i in range(2):
                        wait(sp, y_mm, (it * 2 + i - 1) * B * K)
                        for w in range(3):
                            sp.dma_start(WQ[i][:, :, w, :], qkv_h[ds(it * 2 + i, 1), :, :, w, :]
                                         .rearrange("o p k d -> (o p) k d")).then_inc(w_in[i], 16)
                        sp.dma_start(WO[i][:, :], out_h[ds(it * 2 + i, 1), :, :].rearrange("o p n -> (o p) n")
                                     ).then_inc(w_in[i], 16)
                load(0)
                with sp.Fori(1, NIT) as it:
                    load(it)

            @block.tensor
            def _(pe):
                def project_qk(g, n, w):
                    i, b = head_batch(n)
                    if isinstance(g, int) and g < 2:
                        wait(pe, qk, 2 * (g - 1) + w + 1)
                    else:
                        wait(pe, y_done, (g - 2) * K + 3 + w)
                    for k in range(K):
                        r = mm(PY[w][:, :], WQ[i][:, k, w, :], X1[:, b, k, :], start=(k == 0), stop=(k == K - 1))
                    r.then_inc(qk_mm, 1)

                def project_v(g, n):
                    i, b = head_batch(n)
                    wait(pe, o_done, g - 1)
                    for tc in range(K):
                        for k in range(K):
                            r = mm(PO[n % 2][:, tc * P:(tc + 1) * P], X1[:, b, k, tc * P:(tc + 1) * P],
                                   WQ[i][:, k, 2, :], start=(k == 0), stop=(k == K - 1))
                    r.then_inc(v_mm, 1)

                def scores(g, n, t):
                    j = t % 2
                    wait(pe, ex, g * K + t - 1)
                    mm(PA[j][:, :], Q[n % 2][:, t * P:(t + 1) * P], KT[n % 2][:, :], start=True, stop=True
                       ).then_inc(sc, 1)

                def transposes(g, t):
                    j = t % 2
                    wait(pe, ev, g * K + t - 1)
                    wait(pe, pr, g * K + t + 1)
                    for kc in range(K):
                        r = nc.tensor.transpose(PB[j][:, kc * P:(kc + 1) * P], PR[j][:, kc * P:(kc + 1) * P],
                                                ident[:, :])
                    r.then_inc(tr, 1)

                def values(g, n):
                    wait(pe, ev, (g + 1) * K)
                    wait(pe, v_done, g + 1)
                    for kc in range(K):
                        r = mm(PO[n % 2][:, :], V[n % 2][:, kc * P:(kc + 1) * P], PT[:, kc, :], start=(kc == 0),
                               stop=(kc == K - 1))
                    r.then_inc(o_mm, 1)

                def project_out(g, n, last):
                    i, b = head_batch(n)
                    wait(pe, o_done, g + 1)
                    for m in range(K):
                        if m < 2 and not last:
                            wait(pe, qk, 2 * (g + 1) + m + 1)
                        else:
                            wait(pe, y_done, g * K + m - 1)
                        mm(PY[m % 2][:, :], WO[i][:, m * P:(m + 1) * P], O[:, :], start=True, stop=True
                           ).then_inc(y_mm, 1)

                def body(it, first, last):
                    for n in range(NH):
                        g = it * NH + n
                        ahead = not (last and n == NH - 1)
                        wait(pe, qk, 2 * (g + 1))
                        scores(g, n, 0)
                        scores(g, n, 1)
                        if n or not first:
                            project_out(g - 1, n - 1, False)
                        if ahead:
                            if (n + 1) % B == 0:
                                i = head_batch(n + 1)[0]
                                wait(pe, w_in[i], (it + (n + 1) // NH + 1) * 64)
                            project_qk(g + 1, n + 1, 0)
                        transposes(g, 0)
                        scores(g, n, 2)
                        transposes(g, 1)
                        scores(g, n, 3)
                        if ahead:
                            project_qk(g + 1, n + 1, 1)
                        transposes(g, 2)
                        transposes(g, 3)
                        if ahead:
                            project_v(g + 1, n + 1)
                        values(g, n)
                pe.wait_ge(y0, 1)
                pe.wait_ge(w_in[0], 64)
                project_qk(0, 0, 0)
                project_qk(0, 0, 1)
                project_v(0, 0)
                iterations(pe, body)
                project_out(NIT * NH - 1, NH - 1, True)

            @block.scalar
            def _(act):
                def evacuate_qk(g, n, w):
                    i, b = head_batch(n)
                    wait(act, qk_mm, g * 2 + w + 1)
                    nc.scalar.activation((Q, KT)[w][n % 2][:, :], PY[w][:, :], ACT.Identity, bias=BH[i][:, w:w + 1],
                                         scale=(DH ** -0.5, 1.0)[w]).then_inc(qk, 1)

                def evacuate_v(g, n):
                    wait(act, v_mm, g + 1)
                    nc.scalar.copy(V[n % 2][:, :], PO[n % 2][:, :]).then_inc(v_done, 1)

                def exps(g, t):
                    j = t % 2
                    wait(act, nmax, g * K + t + 1)
                    nc.scalar.activation(PR[j][:, :], PA[j][:, :], ACT.Exp, bias=NM[:, j:j + 1],
                                         accum_out=RSUM[:, j:j + 1]).then_inc(ex, 1)

                def evacuate_t(g, t):
                    wait(act, tr, g * K + t + 1)
                    nc.scalar.copy(PT[:, :, t * P:(t + 1) * P],
                                   PB[t % 2][:, :].rearrange("p (k q) -> p k q", k=K)).then_inc(ev, 1)

                def body(it, first, last):
                    for n in range(NH):
                        g = it * NH + n
                        ahead = not (last and n == NH - 1)
                        exps(g, 0)
                        exps(g, 1)
                        if ahead:
                            if (n + 1) % B == 0:
                                wait(act, bias_in, it * 2 + (n + 1) // B + 1)
                            evacuate_qk(g + 1, n + 1, 0)
                        evacuate_t(g, 0)
                        exps(g, 2)
                        evacuate_t(g, 1)
                        exps(g, 3)
                        if ahead:
                            evacuate_qk(g + 1, n + 1, 1)
                        evacuate_t(g, 2)
                        evacuate_t(g, 3)
                        if ahead:
                            evacuate_v(g + 1, n + 1)
                act.wait_ge(bias_in, 1)
                evacuate_qk(0, 0, 0)
                evacuate_qk(0, 0, 1)
                evacuate_v(0, 0)
                iterations(act, body)

            @block.vector
            def _(dve):
                def biases(head, i):
                    for w in range(3):
                        r = nc.vector.tensor_copy(BH[i][:, w:w + 1], bqkv[:, ds(head + w * HEADS, 1)])
                    r.then_inc(bias_in, 1)

                def maximum(g, t):
                    j = t % 2
                    wait(dve, sc, g * K + t + 1)
                    nc.vector.tensor_reduce(NM[:, j:j + 1], PA[j][:, :], AX.X, ALU.max, negate=True
                                            ).then_inc(nmax, 1)

                def normalise(g, t):
                    j = t % 2
                    wait(dve, ex, g * K + t + 1)
                    nc.vector.reciprocal(RINV[:, j:j + 1], RSUM[:, j:j + 1]).then_inc(rinv, 1)
                    wait(dve, rinv, g * K + t + 1)
                    ts(PR[j][:, :], PR[j][:, :], RINV[:, j:j + 1], None, ALU.mult).then_inc(pr, 1)

                def head_out(g, n):
                    wait(dve, y_mm, g * K)
                    wait(dve, o_mm, g + 1)
                    ts(O[:, :], PO[n % 2][:, :], BH[head_batch(n)[0]][:, 2:3], None, ALU.add).then_inc(o_done, 1)

                def add_out(g, n, m):
                    b = head_batch(n)[1]
                    wait(dve, y_mm, g * K + m + 1)
                    tt(Y[:, b, m, :], Y[:, b, m, :], PY[m % 2][:, :], ALU.add).then_inc(y_done, 1)

                def body(it, first, last):
                    for n in range(NH):
                        g = it * NH + n
                        before = n > 0 or not first
                        if before:
                            head_out(g - 1, n - 1)
                        if (n + 1) % B == 0 and not (last and n == NH - 1):
                            biases(it * 2 + (n + 1) // B, head_batch(n + 1)[0])
                        maximum(g, 0)
                        maximum(g, 1)
                        if before:
                            add_out(g - 1, n - 1, 0)
                        normalise(g, 0)
                        if before:
                            add_out(g - 1, n - 1, 1)
                        normalise(g, 1)
                        if before:
                            add_out(g - 1, n - 1, 2)
                            add_out(g - 1, n - 1, 3)
                        maximum(g, 2)
                        normalise(g, 2)
                        maximum(g, 3)
                        normalise(g, 3)
                biases(0, 0)
                iterations(dve, body)
                head_out(NIT * NH - 1, NH - 1)
                for m in range(K):
                    add_out(NIT * NH - 1, NH - 1, m)
                dve.wait_ge(y_done, HEADS * B * K)

    with ExitStack() as c:
        W1, W2 = sb("w1", [P, K, 4 * D], c=c), sb("w2", [P, F, D], c=c)
        SQX, XC = sb("sqx2", [P, K, T], c=c), sb("xc2", [P, K, T], c=c)
        LNT, RSTD = sb("lnt2", [P, T], c=c), sb("rstd2", [P, T], c=c)
        XP, X2, HF = sb("xp", [P, K, T], c=c), sb("x2", [P, K, T], c=c), sb("hf", [P, F, T], c=c)
        R, R2, OUT = sb("r", [P, K, T], c=c), SQX, X2
        s2 = norm_sems("n2_")
        w_in, yg, xp, h_mm, h_done, z_mm, r1, r2, o_ready, o_out = (
            sem("m_" + n) for n in ("w_in", "yg", "xp", "h_mm", "h_done", "z_mm", "r1", "r2", "o_ready", "o_out"))
        with nc.Block() as block:
            @block.sync
            def _(sp):
                sp.dma_start(W1[:, :, :], w1.rearrange("(k p) n -> p k n", p=P)).then_inc(w_in, 16)
                sp.dma_start(W2[:, :, :], w2.rearrange("(k p) n -> p k n", p=P)).then_inc(w_in, 16)
                with sp.Fori(0, B) as b:
                    sp.wait_ge(o_ready, (b + 1) * K)
                    sp.dma_start(out[ds(b, 1), :, :, :].rearrange("o k p t -> p (o k) t"), OUT[:, :, :]).then_inc(o_out, 16)
                sp.wait_ge(o_out, 16 * (B + 1))

            @block.tensor
            def _(pe):
                with pe.Fori(0, B) as b:
                    pe.wait_ge(xp, (b + 1) * K)
                    norm_pe(s2, b, lambda k: XP[:, k, :])
                    pe.wait_ge(w_in, 32)
                    pe.wait_ge(s2["xn"], (b + 1) * K)
                    for m in range(F):
                        if m >= 2:
                            pe.wait_ge(h_done, b * F + m - 1)
                        for k in range(K):
                            r = mm(PO[m % 2][:, :], W1[:, k, m * P:(m + 1) * P], X2[:, k, :], start=(k == 0), stop=(k == K - 1))
                        r.then_inc(h_mm, 1)
                    pe.wait_ge(h_done, (b + 1) * F)
                    for m in range(K):
                        if m >= 2:
                            pe.wait_ge(r1, b * K + m - 1)
                        for k in range(F):
                            r = mm(PY[m % 2][:, :], W2[:, k, m * P:(m + 1) * P], HF[:, k, :], start=(k == 0), stop=(k == F - 1))
                        r.then_inc(z_mm, 1)

            @block.scalar
            def _(act):
                with act.Fori(0, B) as b:
                    norm_act(s2, b)
                    for m in range(F):
                        act.wait_ge(h_mm, b * F + m + 1)
                        nc.scalar.activation(HF[:, m, :], PO[m % 2][:, :], ACT.Gelu, bias=bb1[:, m:m + 1]).then_inc(h_done, 1)

            @block.vector
            def _(dve):
                dve.sem_inc(o_out, 16)
                with dve.Fori(0, B) as b:
                    xb = lambda k: XV[:, k, ds(b, 1), :].rearrange("p o t -> p (o t)")
                    yb = lambda k: Y[:, ds(b, 1), k, :].rearrange("p o t -> p (o t)")
                    dve.wait_ge(o_out, b * 16 + 16)
                    for k in range(K):
                        ts(R[:, k, :], yb(k), ob[:, k:k + 1], MOD[:, GATE1 + k, ds(b, 1)], ALU.add, ALU.mult).then_inc(yg, 1)
                    for k in range(K):
                        dve.wait_ge(yg, b * K + k + 1)
                        tt(XP[:, k, :], R[:, k, :], xb(k), ALU.add).then_inc(xp, 1)
                    dve.wait_ge(xp, (b + 1) * K)
                    norm_dve(s2, b, lambda k: XP[:, k, :], lambda k: X2[:, k, :], SCALE2, SHIFT2, b)
                    for m in range(K):
                        dve.wait_ge(z_mm, b * K + m + 1)
                        ts(R[:, m, :], PY[m % 2][:, :], bb2[:, m:m + 1], MOD[:, GATE2 + m, ds(b, 1)], ALU.add,
                           ALU.mult).then_inc(r1, 1)
                        dve.wait_ge(r1, b * K + m + 1)
                        tt(R2[:, m, :], R[:, m, :], XP[:, m, :], ALU.add).then_inc(r2, 1)
                        dve.wait_ge(r2, b * K + m + 1)
                        tt(OUT[:, m, :], R2[:, m, :], xb(m), ALU.add).then_inc(o_ready, 1)


def program(nc, x, state, coupling, osc_bias, w_ih, w_hh, b_ih, b_hh, hn_bias, l2, l3, out):
    with ExitStack() as ctx:
        XT = ctx.enter_context(nc.sbuf_tensor("x_time_major", [P, (T + 2) * S], F32))
        cond = state.rearrange("p (k b) -> p k b", b=B)
        sems = PhaseSemaphores()
        with ExitStack() as c:
            with nc.Block() as block:
                recurrence(nc, c, sems, block, XT, state, coupling, osc_bias, w_ih, w_hh, b_ih, b_hh, hn_bias, x)
        sems.close(nc)
        sems = PhaseSemaphores()
        with ExitStack() as c:
            with nc.Block() as block:
                layer2(nc, c, sems, block, XT, cond, *l2)
        sems.close(nc)
        sems = PhaseSemaphores()
        with ExitStack() as c:
            layer3(nc, c, sems, XT, cond, *l3, out)
        sems.close(nc)


def kernel(**inputs):
    import numpy as np
    import concourse.bacc as bacc
    from concourse.bass_utils import run_bass_kernel_spmd

    def cols(name):
        return inputs[name].reshape(-1, P).T

    inputs = {n: np.asarray(a) for n, a in inputs.items()}
    arrays = {
        "x": inputs["x"].reshape(B, T, K, P).transpose(3, 1, 2, 0).reshape(P, T * S),
        "state": inputs["cond_2048"].reshape(B, K, P).transpose(2, 1, 0).reshape(P, S),
        "coupling": inputs["L0_cond_coupling"].T,
        "osc_bias": np.repeat(cols("L0_cond_bias"), B, axis=1),
        "w_ih": inputs["L1_cond_W_ih"], "w_hh": inputs["L1_cond_W_hh"],
        "b_ih": cols("L1_cond_b_ih"), "b_hh": cols("L1_cond_b_hh"),
        "hn_bias": np.repeat(cols("L1_cond_b_hh")[:, 2 * K:], B, axis=1),
        "w_emb": inputs["L2_cond_W_emb"], "b_emb": cols("L2_cond_b_emb"), "g_norm": cols("L2_cond_g_norm"),
        "w_qkv": inputs["L2_cond_W_qkv"],
        "g_qk": np.stack([np.tile(inputs["L2_cond_g_q"], 4), np.tile(inputs["L2_cond_g_k"], 4)], 1),
        "w_out": inputs["L2_cond_W_out"],
        "ada_w": inputs["L3_cond_ada_w"], "ada_b": cols("L3_cond_ada_b"), "qkv_w": inputs["L3_cond_qkv_w"],
        "qkv_b": cols("L3_cond_qkv_b"), "out_w": inputs["L3_cond_out_w"], "out_b": cols("L3_cond_out_b"),
        "w1": inputs["L3_cond_ffn_w1"], "b1": cols("L3_cond_ffn_b1"), "w2": inputs["L3_cond_ffn_w2"],
        "b2": cols("L3_cond_ffn_b2"),
    }
    arrays = {n: np.ascontiguousarray(a) for n, a in arrays.items()}
    nc = bacc.Bacc("TRN2", target_bir_lowering=False, num_devices=1)
    ap = {n: nc.dram_tensor("in_" + n, a.shape, mybir.dt.from_np(a.dtype), kind="ExternalInput").ap()
          for n, a in arrays.items()}
    out = nc.dram_tensor("out", (B, K, P, T), F32, kind="ExternalOutput").ap()
    names = list(ap)
    i2, i3 = names.index("w_emb"), names.index("ada_w")
    program(nc, *(ap[n] for n in names[:i2]), [ap[n] for n in names[i2:i3]], [ap[n] for n in names[i3:]], out)
    r = run_bass_kernel_spmd(nc, [{"in_" + n: a for n, a in arrays.items()}], core_ids=[0])
    return r.results[0]["out"].transpose(0, 3, 1, 2).reshape(B, T, D)
```

```python
import concourse.bass as bass
from concourse import mybir
from contextlib import ExitStack

F32, F16 = mybir.dt.float32, mybir.dt.float16
ds = bass.ds
ACT, ALU, AX = mybir.ActivationFunctionType, mybir.AluOpType, mybir.AxisListType

B, T, D, P = 4, 512, 512, 128
K = D // P
S = K * B
CH = 8
LAG = 2 * CH
NCH = T // CH
GIN = 4
G3 = 3 * K
WSCALE = 256.0
DT, EPS_P, ALPHA, BETA, CLAMP = 0.01, 0.08, 0.7, 0.8, 20.0
STEP = [0.5 * DT, 0.5 * DT, DT, DT / 6.0]


class PhaseSemaphores:

    def __init__(self):
        self.ctx, self.nums = ExitStack(), []

    def take(self, nc, name):
        handle = self.ctx.enter_context(nc.semaphore(name))
        self.nums.append(handle.num)
        return handle

    def close(self, nc):
        with nc.Block() as block:
            @block.gpsimd
            def _(pool):
                for n in sorted(self.nums):
                    if n - 1 not in self.nums:
                        last = n
                        while last + 1 in self.nums:
                            last += 1
                        nc.gpsimd.sem_clear(range(n, last + 1))
        self.ctx.close()


def recurrence(nc, ctx, sems, phase_block, XT, q0, coupling, bias0, w_ih, w_hh, b_ih, b_hh, hn_bias, x, later):
    def sb(name, shape, dt=F32):
        return ctx.enter_context(nc.sbuf_tensor(name, shape, dt))

    def ps(name, shape):
        return ctx.enter_context(nc.psum_tensor(name, shape, F32))

    def sem(name):
        return sems.take(nc, name)

    C = [sb(f"coupling_{n}", [P, K, D], F16) for n in ("hi", "lo")]
    WI = [sb(f"w_ih_{n}", [P, K, 3 * D], F16) for n in ("hi", "lo")]
    WH = [sb(f"w_hh_{n}", [P, K, 3 * D], F16) for n in ("hi", "lo")]
    stage_w = sb("stage_w", [P, K, 3 * D])
    biasq = sb("biasq", [P, S])
    gib, bhh = sb("gib", [P, G3]), sb("bhh", [P, G3])
    SQP = [[sb(f"state{s}_{z}", [P, 2 * S]) for z in range(2)] for s in range(4)]
    raw = sb("raw", [P, 2 * S])
    TX = [sb(f"tanh_parts{i}", [P, K, 2 * B], F16) for i in range(2)]
    T32 = sb("tanh32", [P, S])
    SQ, W3 = sb("sq", [P, S]), sb("w3", [P, S])
    PRE, FS, U = sb("pre", [P, S]), sb("fs", [P, S]), sb("u", [P, S])
    PRATE = sb("p_rate", [P, S])
    DBX = [sb(f"drive{z}", [P, 2 * S]) for z in range(2)]
    GH, GD, G6 = (sb(n, [P, 2 * S]) for n in ("g_half", "g_full", "g_sixth"))
    EA, EB, EC, ED, DSIXTH, ESIXTH = (
        sb(n, [P, 2 * S]) for n in ("e_diff", "e_drive", "e_q3", "e_sum", "drive_sixth", "e_third"))
    DHALF, DFULL = ([sb(f"drive_{n}{z}", [P, 2 * S]) for z in range(2)] for n in ("half", "full"))
    H = [sb(f"h{z}", [P, S]) for z in range(2)]
    HX = sb("h_parts", [P, K, 2 * B], F16)
    GI = sb("gi", [P, CH, 4 * S])
    S1, S2, RZ = (sb(n, [P, 3 * S]) for n in ("s1", "s2", "rz"))
    M1, M2, NN, OMZ, ON, ZH = (sb(n, [P, S]) for n in ("m1", "m2", "nn", "one_minus_z", "on", "zh"))
    XH = [sb(f"x1_{n}", [P, K, T * B], F16) for n in ("hi", "lo")]
    warm = sb("warm", [P, 2])

    PL = [[ps(f"osc{i}{h}", [P, 512]) for h in "ab"] for i in range(2)]
    PG = ps("gates", [P, 512])
    PI = [ps(f"gi{i}", [P, 512]) for i in range(3)]

    NAMES = ["mm_done", "g6_done", "f_done", "cd_ready", "ch_ready", "fb_ready", "gi_done", "zh_done",
             "u_done", "q_raw", "q_ready", "hi_ready", "t32_ready", "lo_ready", "sq_ready", "w3_done",
             "pre_ready", "g_done", "a_done", "p_raw", "p_ready", "drive_ready", "e_done", "gates_done",
             "s1_done", "s2_ready", "rz_ready", "m1_done", "m2_ready", "nn_ready", "on_done", "h_ready",
             "hhi_done", "hx_ready", "x2_done", "x1_done"]
    sets = [{n: sem(f"{n}_{z}") for n in NAMES} for z in range(2)]
    for z in range(2):
        nums = [sets[z][n].num for n in NAMES]
        assert nums == list(range(nums[0], nums[0] + len(NAMES))), nums
    ranges = [range(sets[z][NAMES[0]].num, sets[z][NAMES[-1]].num + 1) for z in range(2)]
    loaded, staged, w_free, wdone = sem("loaded"), sem("staged"), sem("w_free"), sem("wdone")
    xload, init = sem("xload"), sem("init")
    xs_done, gi_mm = sem("xs_done"), sem("gi_mm")
    pool_passed, pe_passed = sem("pool_passed"), sem("pe_passed")
    gib_done = sem("gib_done")

    def at(t):
        return XT[:, ds((t + 1) * S, S)]

    def kcols(tile, a, b):
        return tile[:, a * B:b * B]

    half = [(0, K // 2), (K // 2, K)]
    HB = K // 2

    def pe_osc(z, s, t0=0):
        c = sets[z]
        first = [True, True]

        def mm(m, k, w, cols, last=False):
            h = m // HB
            col = (m - h * HB) * 2 * B
            r = nc.tensor.matmul(PL[s % 2][h][:, col:col + cols], w[:, k, m * P:(m + 1) * P], TX[s % 2][:, k, 0:cols],
                                 start=first[h], stop=last, skip_group_check=True)
            first[h] = False
            return r
        for i, (a, b) in enumerate(half):
            nc.tensor.wait_ge(c["hi_ready"], 2 * s + 1 + i)
            for k in range(a, b):
                for m in range(K):
                    mm(m, k, C[1], B)
        nc.tensor.wait_ge(c["lo_ready"], s + 1)
        for a, b in half:
            for m in range(a, b):
                for k in range(K):
                    r = mm(m, k, C[0], 2 * B, last=(k == K - 1 and m == b - 1))
            r.then_inc(c["mm_done"], 1)

    gru_list = [(m, k, w) for w in (1, 0) for m in range(G3) for k in range(K)]

    def pe_gru(z, lo, hi):
        c = sets[z]
        if lo == 0:
            nc.tensor.wait_ge(c["hx_ready"], 1)
        for n in range(lo, hi):
            m, k, w = gru_list[n]
            r = nc.tensor.matmul(PG[:, m * 8:m * 8 + 8], WH[w][:, k, m * P:(m + 1) * P], HX[:, k, :],
                                 start=(n == 0), stop=(n == len(gru_list) - 1), skip_group_check=True)
        if hi == len(gru_list):
            r.then_inc(c["gates_done"], 1)

    def pe_gates_in(z, chunk, i, gru):
        if i == 0:
            nc.tensor.wait_ge(xs_done, chunk * CH)
            if gru:
                nc.tensor.wait_ge(sets[z]["gi_done"], 1)
        for m in range(i * G3 // GIN, (i + 1) * G3 // GIN):
            for w, x in ((0, 0), (0, 1), (1, 0)):
                for k in range(K):
                    r = nc.tensor.matmul(PI[m // 4][:, (m % 4) * CH * B:(m % 4 + 1) * CH * B],
                                         WI[w][:, k, m * P:(m + 1) * P], XH[x][:, k, ds((chunk - 1) * CH * B, CH * B)],
                                         start=(w == x == k == 0), stop=(w == 1 and k == K - 1))
        if i == GIN - 1:
            r.then_inc(gi_mm, 1)

    def pe_step(z, chunk, j, osc, gru, gates_in):
        if osc:
            for s in range(4):
                pe_osc(z, s)
                if s < 3 and gru:
                    pe_gru(z, 32 * s, 32 * s + 32)
        else:
            pe_gru(z, 0, 96)
        if gates_in:
            pe_gates_in(z, chunk, j, gru)
        if not osc:
            nc.tensor.wait_ge(sets[z]["s2_ready"], 1)
            nc.tensor.sem_inc(pe_passed, 1)

    def gru_candidate(z):
        nc.scalar.wait_ge(sets[1 - z]["m2_ready"], 1)
        nc.scalar.activation(NN[:, :], M2[:, :], ACT.Tanh).then_inc(sets[z]["nn_ready"], 1)

    def gates_in(z, n, chunk):
        c = sets[z]
        if n == 0:
            nc.scalar.wait_ge(gi_mm, chunk - 1)
        for m in range(4 * n, 4 * n + 4):
            a = m * B if m < 2 * K else 3 * S + (m - 2 * K) * B
            pi = PI[n][:, (m % 4) * CH * B:(m % 4 + 1) * CH * B].rearrange("p (t b) -> p t b", b=B)
            r = nc.scalar.activation(GI[:, :, a:a + B], pi, ACT.Identity, bias=gib[:, m:m + 1], scale=1 / WSCALE)
        if n == 2:
            r.then_inc(c["gi_done"], 1)

    def act_step(z, osc, gru, xs=None):
        c, prev = sets[z], sets[1 - z]
        if gru and not osc:
            gru_candidate(z)
        for s in range(4):
            if osc:
                q = SQP[s][z]
                for i, (a, b) in enumerate(half):
                    if s == 0:
                        nc.scalar.wait_ge(prev["q_ready"], 7 + i)
                    else:
                        nc.scalar.wait_ge(c["q_ready"], 2 * s - 1 + i)
                    nc.scalar.activation(TX[s % 2][:, a:b, 0:B], kcols(q, a, b).rearrange("p (k b) -> p k b", b=B),
                                         ACT.Tanh).then_inc(c["hi_ready"], 1)
                    if gru and s == 0 and i == 0:
                        gru_candidate(z)
                nc.scalar.activation(T32[:, :], q[:, 0:S], ACT.Tanh).then_inc(c["t32_ready"], 1)
                nc.scalar.activation(SQ[:, :], q[:, 0:S], ACT.Square,
                                     scale=(STEP[s] / 3.0) ** 0.5).then_inc(c["sq_ready"], 1)
                if s == 0:
                    nc.scalar.wait_ge(prev["drive_ready"], 1)
                    nc.scalar.mul(DFULL[z][:, :], DBX[z][:, :], STEP[2]).then_inc(c["cd_ready"], 1)
                    nc.scalar.mul(DSIXTH[:, :], DBX[z][:, :], 3 * STEP[3]).then_inc(c["cd_ready"], 1)
                if s == 2:
                    nc.scalar.wait_ge(c["e_done"], 4)
                    nc.scalar.mul(ESIXTH[:, :], ED[:, :], 1 / 3.0).then_inc(c["fb_ready"], 1)
                    nc.scalar.wait_ge(c["drive_ready"], 1)
                    nc.scalar.mul(DHALF[1 - z][:, :], DBX[1 - z][:, :], STEP[0]).then_inc(c["ch_ready"], 1)
            if xs is not None and s < 3:
                gates_in(z, s, xs)
            if gru and s == 3:
                nc.scalar.wait_ge(c["s2_ready"], 1)
                nc.scalar.activation(RZ[:, 0:2 * S], S2[:, 0:2 * S], ACT.Sigmoid).then_inc(c["rz_ready"], 1)
                nc.scalar.wait_ge(c["rz_ready"], 1)
                nc.scalar.activation(OMZ[:, :], RZ[:, S:2 * S], ACT.Copy, scale=-1.0, bias=1.0)

    def pool_step(z, t, osc, gru):
        c, prev = sets[z], sets[1 - z]
        st = [SQP[s][z] for s in range(4)]
        add = lambda o, a, b, op=ALU.add: nc.gpsimd.tensor_tensor(o, a, b, op)
        if osc:
            nc.gpsimd.wait_ge(prev["p_ready"], 4)
            nc.gpsimd.wait_ge(prev["q_ready"], 8)
            nc.gpsimd.wait_ge(prev["ch_ready"], 1)
            add(GH[:, :], DHALF[z][:, :], st[0][:, :]).then_inc(c["g_done"], 1)
            nc.gpsimd.wait_ge(c["cd_ready"], 1)
            add(GD[:, :], DFULL[z][:, :], st[0][:, :]).then_inc(c["g_done"], 1)
            if not (isinstance(t, int) and t == 0):
                pool_x1(z, t)
        elif isinstance(t, int) and t == T:
            nc.gpsimd.wait_ge(prev["q_ready"], 8)
            pool_x1(z, t)
        if gru:
            nc.gpsimd.wait_ge(c["h_ready"], 1)
            add(at(t - LAG - 1), at(t - LAG - 1), H[z][:, :]).then_inc(c["x2_done"], 1)
        if osc:
            nc.gpsimd.wait_ge(c["p_ready"], 1)
            nc.gpsimd.wait_ge(c["q_ready"], 2)
            add(EA[:, :], st[1][:, :], st[0][:, :], ALU.subtract).then_inc(c["e_done"], 1)
            nc.gpsimd.wait_ge(c["e_done"], 1)
            nc.gpsimd.wait_ge(c["cd_ready"], 2)
            add(EB[:, :], EA[:, :], DSIXTH[:, :]).then_inc(c["e_done"], 1)
            nc.gpsimd.wait_ge(c["p_ready"], 2)
            nc.gpsimd.wait_ge(c["q_ready"], 4)
            nc.gpsimd.wait_ge(c["e_done"], 2)
            add(EC[:, :], EB[:, :], st[2][:, :]).then_inc(c["e_done"], 1)
            nc.gpsimd.wait_ge(c["e_done"], 3)
            add(ED[:, :], EC[:, :], st[2][:, :]).then_inc(c["e_done"], 1)
            add(DBX[1 - z][:, 0:S], at(t + 1), biasq[:, :]).then_inc(c["drive_ready"], 1)
        if gru:
            nc.gpsimd.wait_ge(c["rz_ready"], 1)
            add(ZH[:, :], RZ[:, S:2 * S], H[z][:, :], ALU.mult).then_inc(c["zh_done"], 1)
        if not osc:
            nc.gpsimd.wait_ge(c["s2_ready"], 1)
            nc.gpsimd.sem_inc(pool_passed, 1)

    def pool_x1(z, t):
        c = sets[z]
        x1 = at(t - 1).rearrange("p (k b) -> p k b", b=B)
        hi, lo = (XH[n][:, :, ds((t - 1) * B, B)] for n in range(2))
        nc.gpsimd.tensor_tensor(at(t - 1), at(t - 1), SQP[0][z][:, 0:S], ALU.add).then_inc(c["x1_done"], 1)
        nc.gpsimd.wait_ge(c["x1_done"], 1)
        nc.gpsimd.tensor_copy(hi, x1).then_inc(c["x1_done"], 1)
        nc.gpsimd.wait_ge(c["x1_done"], 2)
        nc.gpsimd.tensor_tensor(lo, x1, hi, ALU.subtract).then_inc(xs_done, 1)

    def gru_update(z):
        c, prev = sets[z], sets[1 - z]
        v = lambda x: x[:, :].rearrange("p (k b) -> p k b", b=B)
        nc.vector.wait_ge(c["nn_ready"], 1)
        nc.vector.tensor_tensor(ON[:, :], OMZ[:, :], NN[:, :], ALU.mult).then_inc(c["on_done"], 1)
        yield
        nc.vector.wait_ge(prev["zh_done"], 1)
        nc.vector.wait_ge(c["on_done"], 1)
        nc.vector.tensor_tensor(HX[:, :, 0:B], v(ON), v(ZH), ALU.add).then_inc(c["hhi_done"], 1)
        nc.vector.tensor_tensor(H[z][:, :], ON[:, :], ZH[:, :], ALU.add).then_inc(c["h_ready"], 1)
        yield
        nc.vector.wait_ge(c["h_ready"], 1)
        nc.vector.tensor_tensor(HX[:, :, B:2 * B], v(H[z]), HX[:, :, 0:B], ALU.subtract).then_inc(c["hx_ready"], 1)
        yield

    def gru_gates(z, j, xs):
        c = sets[z]
        gi = lambda a, b: GI[:, ds(j, 1), a * S:b * S].rearrange("p o c -> p (o c)")
        pg = PG[:, 0:G3 * 8].rearrange("p (m c) -> p m c", c=8)
        v3 = lambda x: x.rearrange("p (m b) -> p m b", b=B)
        if xs is not None:
            nc.vector.wait_ge(c["gi_done"], 1)
        nc.vector.wait_ge(c["gates_done"], 1)
        nc.vector.scalar_tensor_tensor(v3(S1[:, :]), pg[:, :, 0:B], 1 / WSCALE, v3(gi(0, 3)),
                                       ALU.mult, ALU.add).then_inc(c["s1_done"], 1)
        yield
        nc.vector.wait_ge(c["s1_done"], 1)
        nc.vector.scalar_tensor_tensor(v3(S2[:, :]), pg[:, :, B:2 * B], 1 / WSCALE, v3(S1[:, :]),
                                       ALU.mult, ALU.add).then_inc(c["s2_ready"], 1)
        yield
        nc.vector.wait_ge(c["rz_ready"], 1)
        nc.vector.tensor_tensor(M1[:, :], RZ[:, 0:S], S2[:, 2 * S:3 * S], ALU.mult).then_inc(c["m1_done"], 1)
        yield
        nc.vector.wait_ge(c["m1_done"], 1)
        nc.vector.tensor_tensor(M2[:, :], M1[:, :], gi(3, 4), ALU.add).then_inc(c["m2_ready"], 1)
        yield

    def dve_step(z, j, osc, gru, xs=None):
        c, prev = sets[z], sets[1 - z]
        update, gates = gru_update(z), gru_gates(z, j, xs)
        if not osc:
            for _ in update:
                pass
            nc.vector.wait_ge(c["gates_done"], 1)
            nc.vector.wait_ge(c["x2_done"], 1)
            nc.vector.sem_clear(ranges[1 - z])
            for _ in gates:
                pass
            return

        def gru_part(work):
            if gru:
                next(work)
        st = [SQP[s][z] for s in range(4)]
        nxt = SQP[0][1 - z]
        stt = nc.vector.scalar_tensor_tensor
        for s in range(4):
            h = STEP[s]
            g = (GH, GH, GD, G6)[s]
            stt(PRATE[:, :], st[s][:, S:2 * S], -BETA, st[s][:, 0:S], ALU.mult, ALU.add).then_inc(c["a_done"], 1)
            if s == 3:
                nc.vector.wait_ge(c["fb_ready"], 1)
                stt(G6[:, :], st[3][:, :], 1 / 3.0, ESIXTH[:, :], ALU.mult, ALU.add).then_inc(c["g6_done"], 1)

            def without_product():
                stt(FS[:, :], st[s][:, S:2 * S], -h, g[:, 0:S], ALU.mult, ALU.add).then_inc(c["f_done"], 1)

            def tanh_low():
                nc.vector.wait_ge(c["t32_ready"], s + 1)
                nc.vector.tensor_tensor(TX[s % 2][:, :, B:2 * B], T32[:, :].rearrange("p (k b) -> p k b", b=B),
                                        TX[s % 2][:, :, 0:B], ALU.subtract).then_inc(c["lo_ready"], 1)

            def cube():
                nc.vector.wait_ge(c["sq_ready"], s + 1)
                stt(W3[:, :], SQ[:, :], h, st[s][:, 0:S], ALU.subtract, ALU.mult).then_inc(c["w3_done"], 1)
            if s == 0:
                gru_part(update)
                tanh_low()
                nc.vector.wait_ge(c["g_done"], 1)
                without_product()
                cube()
                gru_part(update)
            elif s == 3:
                tanh_low()
                nc.vector.wait_ge(c["g6_done"], 1)
                without_product()
                cube()
                gru_part(gates)
            else:
                if s == 2:
                    nc.vector.wait_ge(c["g_done"], 2)
                without_product()
                tanh_low()
                cube()
            def next_p():
                nc.vector.wait_ge(c["a_done"], s + 1)
                out, done = (raw, c["p_raw"]) if s == 3 else (st[s + 1], c["p_ready"])
                stt(out[:, S:2 * S], PRATE[:, :], h * EPS_P, g[:, S:2 * S], ALU.mult, ALU.add).then_inc(done, 1)
            if 0 < s < 3:
                next_p()
            nc.vector.wait_ge(c["f_done"], s + 1)
            nc.vector.wait_ge(c["w3_done"], s + 1)
            nc.vector.tensor_tensor(PRE[:, :], FS[:, :], W3[:, :], ALU.subtract).then_inc(c["pre_ready"], 1)
            if s == 0:
                gru_part(update)
                next_p()
            if s == 3:
                next_p()
                gru_part(gates)
            if s == 2:
                nc.vector.wait_ge(c["e_done"], 4)
                nc.vector.sem_clear(ranges[1 - z])
            if s == 3:
                nc.vector.wait_ge(c["p_raw"], 1)
                nc.vector.tensor_scalar(nxt[:, S:2 * S], raw[:, S:2 * S], CLAMP, -CLAMP, ALU.min,
                                        ALU.max).then_inc(c["p_ready"], 1)
            out = raw if s == 3 else st[s + 1]
            pv = [PL[s % 2][i][:, 0:HB * 2 * B].rearrange("p (m c) -> p m c", c=2 * B) for i in range(2)]
            k3 = lambda x, i: kcols(x, *half[i]).rearrange("p (k b) -> p k b", b=B)

            def with_high(i):
                if i == 0:
                    nc.vector.wait_ge(c["pre_ready"], s + 1)
                nc.vector.wait_ge(c["mm_done"], 2 * s + 1 + i)
                stt(k3(U, i), pv[i][:, :, 0:B], h / WSCALE, k3(PRE, i), ALU.mult, ALU.add).then_inc(c["u_done"], 1)

            def with_low(i):
                nc.vector.wait_ge(c["u_done"], 2 * s + 1 + i)
                r = stt(k3(out, i), pv[i][:, :, B:2 * B], h / WSCALE, k3(U, i), ALU.mult, ALU.add)
                r.then_inc(c["q_raw" if s == 3 else "q_ready"], 1)

            def clip(i):
                nc.vector.wait_ge(c["q_raw"], 1 + i)
                nc.vector.tensor_scalar(kcols(nxt, *half[i]), kcols(raw, *half[i]), CLAMP, -CLAMP, ALU.min,
                                        ALU.max).then_inc(c["q_ready"], 1)
            with_high(0)
            with_low(0)
            with_high(1)
            if s == 3:
                gru_part(gates)
                clip(0)
            with_low(1)
            if s == 3:
                gru_part(gates)
                clip(1)
            nc.vector.wait_ge(c["q_ready"], 2 * s + 2)

    block = phase_block

    def chunks(eng, step):
        def chunk(c, osc, gi, gru):
            for i in range(CH):
                step(i % 2, c, i, osc, gru, c if gru and i == 0 else None, gi and i < GIN)
        chunk(0, True, False, False)
        chunk(1, True, True, False)
        yield
        with eng.Fori(2, NCH) as c:
            chunk(c, True, True, True)
        chunk(NCH, False, True, True)
        chunk(NCH + 1, False, False, True)
        yield

    @block.sync
    def _(sp):
        sp.dma_start(XT[:, S:(T + 1) * S], x).then_inc(xload, 16)
        for n, (tile, src) in enumerate([(biasq, bias0), (gib, b_ih), (bhh, b_hh), (SQP[0][0][:, 0:S], q0),
                                         (SQP[0][0][:, S:2 * S], q0), (ZH, q0)]):
            sp.dma_start(tile[:, :] if n < 3 or n == 5 else tile, src).then_inc(loaded, 16)
        for j in range(CH):
            sp.dma_start(GI[:, j, 2 * S:3 * S], hn_bias).then_inc(loaded, 16)
        for n, (w, cols) in enumerate([(coupling, D), (w_ih, 3 * D), (w_hh, 3 * D)]):
            if n:
                sp.wait_ge(w_free, n)
            sp.dma_start(stage_w[:, :, 0:cols], w.rearrange("(k p) n -> p k n", p=P)).then_inc(staged, 16)
        for tile, src in later.sources:
            sp.dma_start(tile, src).then_inc(later.loaded, 16)

    @block.tensor
    def _(pe):
        pe.wait_ge(wdone, 3)
        pe.wait_ge(w_free, 3)
        for _ in chunks(pe, lambda z, c, j, o, g, x, gi: pe_step(z, c, j, o, g, gi)):
            pass

    @block.scalar
    def _(act):
        nc.scalar.wait_ge(init, 1)
        nc.scalar.activation(warm[:, 1:2], warm[:, 0:1], ACT.Sigmoid)
        nc.scalar.wait_ge(sets[1]["drive_ready"], 1)
        nc.scalar.mul(DHALF[0][:, :], DBX[0][:, :], STEP[0]).then_inc(sets[1]["ch_ready"], 1)
        for _ in chunks(act, lambda z, c, j, o, g, x, gi: act_step(z, o, g, x)):
            pass
        gru_candidate(0)

    @block.gpsimd
    def _(pool):
        pool.wait_ge(xload, 16)
        pool.wait_ge(loaded, 16 * (6 + CH))
        pool.wait_ge(init, 2)

        nc.gpsimd.tensor_tensor(DBX[0][:, 0:S], at(0), biasq[:, :], ALU.add).then_inc(sets[1]["drive_ready"], 1)
        for _ in chunks(pool, lambda z, c, j, o, g, x, gi: pool_step(z, c * CH + j, o, g)):
            pass

    @block.vector
    def _(dve):
        nc.vector.memset(warm[:, :], 0.0).then_inc(init, 1)
        nc.vector.memset(DBX[0][:, S:2 * S], EPS_P * ALPHA)
        nc.vector.memset(DBX[1][:, S:2 * S], EPS_P * ALPHA)
        nc.vector.memset(XT[:, 0:S], 0.0)
        nc.vector.memset(XT[:, (T + 1) * S:], 0.0)
        nc.vector.memset(M2[:, :], 0.0)
        nc.vector.memset(OMZ[:, :], 0.0).then_inc(init, 1)
        dve.wait_ge(init, 2)
        for n, (w, cols) in enumerate([(C, D), (WI, 3 * D), (WH, 3 * D)]):
            dve.wait_ge(staged, 16 * (n + 1))
            nc.vector.tensor_scalar(w[0][:, :, :], stage_w[:, :, 0:cols], WSCALE, None, ALU.mult).then_inc(wdone, 1)
            dve.wait_ge(wdone, n + 1)
            for k in range(K):
                r = nc.vector.scalar_tensor_tensor(w[1][:, k, :], stage_w[:, k, 0:cols], WSCALE, w[0][:, k, :],
                                                   ALU.mult, ALU.subtract)
            r.then_inc(w_free, 1)
        dve.wait_ge(w_free, 3)
        dve.wait_ge(loaded, 16 * (6 + CH))
        nc.vector.tensor_tensor(gib[:, 0:2 * K], gib[:, 0:2 * K], bhh[:, 0:2 * K], ALU.add).then_inc(gib_done, 1)
        dve.wait_ge(gib_done, 1)
        dve.sem_inc(sets[1]["p_ready"], 4)
        dve.sem_inc(sets[1]["q_ready"], 8)

        for n, _ in enumerate(chunks(dve, lambda z, c, j, o, g, x, gi: dve_step(z, j, o, g, x))):
            if n == 0:
                dve.sem_inc(sets[1]["m2_ready"], 1)
                dve.sem_inc(sets[1]["zh_done"], 1)
        for _ in gru_update(0):
            pass
        dve.wait_ge(sets[0]["h_ready"], 1)
        dve.wait_ge(sets[1]["x2_done"], 1)
        nc.vector.tensor_tensor(at(T - 1), at(T - 1), H[0][:, :], ALU.add)

class Layer2Weights:

    def __init__(self, nc, ctx, cond, w_emb, b_emb, g_norm, w_qkv, g_qk, w_out):
        def sb(name, shape):
            return ctx.enter_context(nc.sbuf_tensor("l2_" + name, shape, F32))
        self.qkv, self.out, self.emb = sb("w_qkv", [P, K, 3 * D]), sb("w_out", [P, K, D]), sb("w_emb", [P, K, 2 * D])
        self.b_emb, self.g_norm, self.g_qk = sb("bemb", [P, 2 * K]), sb("gn", [P, K]), sb("gqk", [P, 2])
        self.cond = sb("cond", [P, K, B])
        self.sources = ((self.cond[:, :, :], cond), (self.emb[:, :, :], w_emb.rearrange("(k p) n -> p k n", p=P)),
                        (self.b_emb[:, :], b_emb), (self.g_norm[:, :], g_norm), (self.g_qk[:, :], g_qk),
                        (self.qkv[:, :, :], w_qkv.rearrange("(k p) n -> p k n", p=P)),
                        (self.out[:, :, :], w_out.rearrange("(k p) n -> p k n", p=P)))
        self.loaded = ctx.enter_context(nc.semaphore("l2_loaded"))


def layer2(nc, ctx, sems, phase_block, XT, weights):
    def sb(name, shape, dt=F32):
        return ctx.enter_context(nc.sbuf_tensor("l2_" + name, shape, dt))

    def sem(name):
        return sems.take(nc, "l2_" + name)

    HEADS, DH = 16, 32
    XV = XT[:, S:(T + 1) * S].rearrange("p (t k b) -> p k b t", k=K, b=B)
    WQKV, WO, WE, CT = weights.qkv, weights.out, weights.emb, weights.cond
    bemb, gn, gqk = weights.b_emb, weights.g_norm, weights.g_qk
    ones_d, ones_h, ident = sb("ones_d", [P, P]), sb("ones_h", [P, P]), sb("ident", [P, P])
    eps = sb("eps", [P, 1])
    MOD = sb("mod", [P, 2 * K, B])
    SQX, XN, TMP = sb("sqx", [P, K, T]), sb("xn", [P, K, T]), sb("tmp", [P, K, T])
    STD, RSTD = sb("std", [P, T]), sb("rstd", [P, T])
    SQH, STDH, RH = ([sb(f"{n}{i}", [P, T]) for i in range(2)] for n in ("sqh", "stdh", "rh"))
    QK, V = sb("qk", [P, 2 * K, T]), sb("v", [P, K, D])
    PR = [sb(f"prob{i}", [P, T]) for i in range(4)]
    PT = [sb(f"probT{i}", [P, K, T]) for i in range(2)]
    NM, RSUM, RINV = (sb(n, [P, 4]) for n in ("negmax", "rowsum", "rowinv"))
    OT = sb("oT", [P, K, T])
    YS = [sb(f"ys{i}", [P, T]) for i in range(2)]

    PA = [ctx.enter_context(nc.psum_tensor(f"l2_pa{i}", [P, T], F32)) for i in range(4)]
    PB = [ctx.enter_context(nc.psum_tensor(f"l2_pb{i}", [P, T], F32)) for i in range(2)]
    PO = [ctx.enter_context(nc.psum_tensor(f"l2_po{i}", [P, T], F32)) for i in range(2)]

    consts, emb_mm, mod_done, mod_raw = (sem(n) for n in ("consts", "emb_mm", "mod_done", "mod_raw"))
    sqx, ms, std, rstd, xt, xn = (sem(n) for n in ("sqx", "ms", "std", "rstd", "xt", "xn"))
    qk_mm, sqh, nh_mm, stdh, rh, qn, v_mm, v_done = (
        sem(n) for n in ("qk_mm", "sqh", "nh_mm", "stdh", "rh", "qn", "v_mm", "v_done"))
    sc, nmax, ex, rinv, pr, tr, ev, o_mm, o_done = (
        sem(n) for n in ("sc", "nmax", "ex", "rinv", "pr", "tr", "ev", "o_mm", "o_done"))
    y_mm, ys, x_done, ident_done = (sem(n) for n in ("y_mm", "ys", "x_done", "ident_done"))
    NU = HEADS * K

    block = phase_block

    @block.gpsimd
    def _(pool):
        nc.gpsimd.memset(ident[:, :], 0.0).then_inc(ident_done, 1)
        pool.wait_ge(ident_done, 1)
        nc.gpsimd.affine_select(out=ident[:, :], in_=ident[:, :], compare_op=ALU.not_equal, fill=1.0, base=0,
                                pattern=[[-1, P]], channel_multiplier=1).then_inc(ident_done, 1)

    @block.tensor
    def _(pe):
        mm = nc.tensor.matmul
        pe.wait_ge(weights.loaded, 16 * len(weights.sources))
        for m in range(2 * K):
            for k in range(K):
                r = mm(PA[0][:, m * B:(m + 1) * B], WE[:, k, m * P:(m + 1) * P], CT[:, k, :],
                       start=(k == 0), stop=(k == K - 1))
        r.then_inc(emb_mm, 1)
        pe.wait_ge(consts, 3)
        pe.wait_ge(ident_done, 2)
        pe.wait_ge(mod_done, 1)
        with pe.Fori(0, B) as b:
            for k in range(K):
                pe.wait_ge(sqx, b * K + k + 1)
                r = mm(PB[0][:, :], ones_d[:, :], SQX[:, k, :], start=(k == 0), stop=(k == K - 1))
            r.then_inc(ms, 1)
            pe.wait_ge(xn, (b + 1) * K)

            def head_norm(c):
                pe.wait_ge(sqh, b * 2 * K + c + 1)
                mm(PB[c % 2][:, :], ones_h[:, :], SQH[c % 2][:, :], start=True, stop=True).then_inc(nh_mm, 1)
            for c in range(2 * K):
                if c >= 2:
                    pe.wait_ge(qn, b * 2 * K + c - 1)
                for k in range(K):
                    r = mm(PA[c % 2][:, :], WQKV[:, k, c * P:(c + 1) * P], XN[:, k, :], start=(k == 0), stop=(k == K - 1))
                r.then_inc(qk_mm, 1)
                if c >= 1:
                    head_norm(c - 1)
            head_norm(2 * K - 1)
            for tc in range(K):
                if tc >= 2:
                    pe.wait_ge(v_done, b * K + tc - 1)
                for k in range(K):
                    r = mm(PO[tc % 2][:, :], XN[:, k, tc * P:(tc + 1) * P], WQKV[:, k, 2 * D:3 * D],
                           start=(k == 0), stop=(k == K - 1))
                r.then_inc(v_mm, 1)
            pe.wait_ge(qn, (b + 1) * 2 * K)
            pe.wait_ge(v_done, (b + 1) * K)

            def scores(n):
                h, i = divmod(n, K)
                c, j = divmod(h, 4)
                r0 = 32 * j
                if n >= 4:
                    pe.wait_ge(ex, b * NU + n - 3)
                mm(PA[n % 4][:, :], QK[r0:r0 + 32, c, i * P:(i + 1) * P], QK[r0:r0 + 32, K + c, :],
                   start=True, stop=True, tile_position=(r0, 0)).then_inc(sc, 1)

            def transposes(n):
                pe.wait_ge(pr, b * NU + n + 1)
                if n >= 2:
                    pe.wait_ge(ev, b * NU + n - 1)
                for kc in range(K):
                    r = nc.tensor.transpose(PB[n % 2][:, kc * P:(kc + 1) * P], PR[n % 4][:, kc * P:(kc + 1) * P],
                                            ident[:, :])
                r.then_inc(tr, 1)

            def values(h):
                c, j = divmod(h, 4)
                pe.wait_ge(ev, b * NU + (h + 1) * K)
                if j == 0 and c >= 2:
                    pe.wait_ge(o_done, b * K + c - 1)
                for kc in range(K):
                    r = mm(PO[c % 2][32 * j:32 * j + 32, :], V[:, kc, h * DH:(h + 1) * DH], PT[h % 2][:, kc, :],
                           start=(kc == 0), stop=(kc == K - 1), tile_position=(0, 32 * j))
                r.then_inc(o_mm, 1)
            scores(0)
            scores(1)
            for n in range(NU):
                if n + 2 < NU:
                    scores(n + 2)
                transposes(n)
                if n % K == 1 and n > K:
                    values(n // K - 1)
            values(HEADS - 1)
            pe.wait_ge(o_done, (b + 1) * K)
            for m in range(K):
                if m >= 2:
                    pe.wait_ge(ys, b * K + m - 1)
                for k in range(K):
                    r = mm(PA[m % 2][:, :], WO[:, k, m * P:(m + 1) * P], OT[:, k, :], start=(k == 0), stop=(k == K - 1))
                r.then_inc(y_mm, 1)
            pe.wait_ge(ys, (b + 1) * K)

    @block.scalar
    def _(act):
        act.wait_ge(consts, 3)
        with act.Fori(0, B) as b:
            for k in range(K):
                nc.scalar.activation(SQX[:, k, :], XV[:, k, bass.ds(b, 1), :].rearrange("p o t -> p (o t)"),
                                     ACT.Square).then_inc(sqx, 1)
            act.wait_ge(ms, b + 1)
            nc.scalar.activation(STD[:, :], PB[0][:, :], ACT.Sqrt, bias=eps[:, :]).then_inc(std, 1)

            def head_rstd(c):
                act.wait_ge(nh_mm, b * 2 * K + c + 1)
                nc.scalar.activation(STDH[c % 2][:, :], PB[c % 2][:, :], ACT.Sqrt, bias=eps[:, :]).then_inc(stdh, 1)
            for c in range(2 * K):
                act.wait_ge(qk_mm, b * 2 * K + c + 1)
                nc.scalar.activation(SQH[c % 2][:, :], PA[c % 2][:, :], ACT.Square).then_inc(sqh, 1)
                if c >= 1:
                    head_rstd(c - 1)
            head_rstd(2 * K - 1)
            for tc in range(K):
                act.wait_ge(v_mm, b * K + tc + 1)
                nc.scalar.copy(V[:, tc, :], PO[tc % 2][:, :]).then_inc(v_done, 1)

            def evacuate(n):
                h, i = divmod(n, K)
                act.wait_ge(tr, b * NU + n + 1)
                if i == 0 and h >= 2:
                    act.wait_ge(o_mm, b * HEADS + h - 1)
                nc.scalar.copy(PT[h % 2][:, :, i * P:(i + 1) * P],
                               PB[n % 2][:, :].rearrange("p (k q) -> p k q", k=K)).then_inc(ev, 1)
            for n in range(NU):
                act.wait_ge(nmax, b * NU + n + 1)
                j = n % 4
                nc.scalar.activation(PR[j][:, :], PA[j][:, :], ACT.Exp, bias=NM[:, j:j + 1],
                                     accum_out=RSUM[:, j:j + 1]).then_inc(ex, 1)
                if n >= 2:
                    evacuate(n - 2)
            evacuate(NU - 2)
            evacuate(NU - 1)
            act.wait_ge(x_done, (b + 1) * K)

    @block.vector
    def _(dve):
        stt, tt, ts = nc.vector.scalar_tensor_tensor, nc.vector.tensor_tensor, nc.vector.tensor_scalar
        nc.vector.memset(ones_d[:, :], 1.0 / D)
        nc.vector.memset(eps[:, :], 1e-6)
        nc.vector.memset(ones_h[:, :], 0.0).then_inc(consts, 1)
        dve.wait_ge(consts, 1)
        for j in range(4):
            r = nc.vector.memset(ones_h[32 * j:32 * j + 32, 32 * j:32 * j + 32], 1.0 / DH)
        r.then_inc(consts, 1)
        dve.wait_ge(weights.loaded, 16 * len(weights.sources))
        dve.wait_ge(emb_mm, 1)
        tt(MOD[:, :, :], PA[0][:, 0:2 * K * B].rearrange("p (m b) -> p m b", b=B),
           bemb[:, :].unsqueeze(2).to_broadcast([P, 2 * K, B]), ALU.add).then_inc(mod_raw, 1)
        dve.wait_ge(mod_raw, 1)
        stt(MOD[:, 0:K, :], MOD[:, 0:K, :], 1.0, gn[:, :].unsqueeze(2).to_broadcast([P, K, B]), ALU.add,
            ALU.mult).then_inc(mod_done, 1)
        ts(gqk[:, 0:1], gqk[:, 0:1], DH ** -0.5, None, ALU.mult).then_inc(consts, 1)
        dve.wait_ge(consts, 3)
        dve.wait_ge(mod_done, 1)
        with dve.Fori(0, B) as b:
            xb = lambda k: XV[:, k, bass.ds(b, 1), :].rearrange("p o t -> p (o t)")
            dve.wait_ge(std, b + 1)
            nc.vector.reciprocal(RSTD[:, :], STD[:, :]).then_inc(rstd, 1)
            dve.wait_ge(rstd, b + 1)
            for k in range(K):
                tt(TMP[:, k, :], xb(k), RSTD[:, :], ALU.mult).then_inc(xt, 1)
            for k in range(K):
                dve.wait_ge(xt, b * K + k + 1)
                ts(XN[:, k, :], TMP[:, k, :], MOD[:, k, bass.ds(b, 1)], MOD[:, K + k, bass.ds(b, 1)],
                   ALU.mult, ALU.add).then_inc(xn, 1)
            for c in range(2 * K):
                dve.wait_ge(stdh, b * 2 * K + c + 1)
                nc.vector.reciprocal(RH[c % 2][:, :], STDH[c % 2][:, :]).then_inc(rh, 1)
                dve.wait_ge(rh, b * 2 * K + c + 1)
                stt(QK[:, c, :], PA[c % 2][:, :], gqk[:, c // K:c // K + 1], RH[c % 2][:, :], ALU.mult,
                    ALU.mult).then_inc(qn, 1)

            def normalise(n):
                dve.wait_ge(ex, b * NU + n + 1)
                j = n % 4
                nc.vector.reciprocal(RINV[:, j:j + 1], RSUM[:, j:j + 1]).then_inc(rinv, 1)
                dve.wait_ge(rinv, b * NU + n + 1)
                ts(PR[j][:, :], PR[j][:, :], RINV[:, j:j + 1], None, ALU.mult).then_inc(pr, 1)
            for n in range(NU):
                dve.wait_ge(sc, b * NU + n + 1)
                nc.vector.tensor_reduce(NM[:, n % 4:n % 4 + 1], PA[n % 4][:, :], AX.X, ALU.max,
                                        negate=True).then_inc(nmax, 1)
                if n >= 1:
                    normalise(n - 1)
                if n % 16 == 8 and n > 16:
                    c = n // 16 - 1
                    dve.wait_ge(o_mm, b * HEADS + 4 * (c + 1))
                    nc.vector.tensor_copy(OT[:, c, :], PO[c % 2][:, :]).then_inc(o_done, 1)
            normalise(NU - 1)
            dve.wait_ge(o_mm, (b + 1) * HEADS)
            nc.vector.tensor_copy(OT[:, K - 1, :], PO[(K - 1) % 2][:, :]).then_inc(o_done, 1)
            for m in range(K):
                dve.wait_ge(y_mm, b * K + m + 1)
                tt(YS[m % 2][:, :], PA[m % 2][:, :], OT[:, m, :], ALU.add).then_inc(ys, 1)
                dve.wait_ge(ys, b * K + m + 1)
                tt(xb(m), xb(m), YS[m % 2][:, :], ALU.add).then_inc(x_done, 1)

def layer3(nc, ctx, sems, XT, cond, ada_w, ada_b, qkv_w, qkv_b, out_w, out_b, w1, b1, w2, b2, out):
    def sb(name, shape, dt=F32, c=ctx):
        return c.enter_context(nc.sbuf_tensor("l3_" + name, shape, dt))

    def sem(name):
        return sems.take(nc, "l3_" + name)

    HEADS, DH, F = 16, 128, 4 * D // P
    SHIFT1, SCALE1, GATE1, SHIFT2, SCALE2, GATE2 = (K * n for n in range(6))
    XV = XT[:, S:(T + 1) * S].rearrange("p (t k b) -> p k b t", k=K, b=B)
    ones_d, ident, identh, eps = sb("ones_d", [P, P]), sb("ident", [P, P]), sb("ident16", [P, P], F16), sb("eps", [P, 1])
    MOD = sb("mod", [P, 6 * K, B])
    Y = sb("y", [P, B, K, T])
    ob, bb2, bb1, bqkv = sb("ob", [P, K]), sb("bb2", [P, K]), sb("bb1", [P, F]), sb("bqkv", [P, 3 * HEADS])
    BH = [sb(f"bias_head{i}", [P, 3]) for i in range(2)]
    PA, PO, PY = ([ctx.enter_context(nc.psum_tensor(f"l3_{n}{i}", [P, T], F32)) for i in range(2)]
                      for n in ("pa", "po", "py"))
    mm = nc.tensor.matmul
    stt, tt, ts = nc.vector.scalar_tensor_tensor, nc.vector.tensor_tensor, nc.vector.tensor_scalar
    ds = bass.ds

    PARTS = ((0, 0), (0, 1), (1, 0))

    def normed(tag, out, scale, shift, before=None, weights=None):
        with ExitStack() as c:
            SQX, XC = sb(tag + "_sqx", [P, K, T], c=c), [sb(f"{tag}_xc{i}", [P, K, T], c=c) for i in range(2)]
            STD, RSTD = sb(tag + "_std", [P, T], c=c), sb(tag + "_rstd", [P, T], c=c)
            gated, src, mean, xc, sqx, var, std, rstd, xt, xn, hi, split = (
                sem(tag + "_" + n) for n in ("gated", "src", "mean", "xc", "sqx", "var", "std", "rstd", "xt", "xn",
                                             "hi", "split"))
            if weights:
                STAGE = [sb(f"stage{i}", [P, 4 * D], c=c) for i in range(2)]
                staged = [sem(f"{tag}_staged{i}") for i in range(2)]
                w_hi, w_lo = sem(tag + "_w_hi"), sem(tag + "_w_lo")
            x_in = (lambda b, k: Y[:, b, k, :]) if before else (lambda b, k: XV[:, k, b, :])
            with nc.Block() as block:
                @block.sync
                def _(sp):
                    if weights:
                        for n, (dram, _) in enumerate(weights):
                            if n >= 2:
                                sp.wait_ge(w_lo, n - 1)
                            tile = STAGE[n % 2][:, :]
                            if n >= K:
                                tile = tile.rearrange("p (k n) -> p k n", k=4)
                            sp.dma_start(tile, dram).then_inc(staged[n % 2], 16)

                @block.tensor
                def _(pe):
                    def mean_of(b):
                        if before:
                            pe.wait_ge(src, (b + 1) * K)
                        if b >= 2:
                            pe.wait_ge(xc, (b - 1) * K)
                        for k in range(K):
                            r = mm(PA[b % 2][:, :], ones_d[:, :], x_in(b, k), start=(k == 0), stop=(k == K - 1))
                        r.then_inc(mean, 1)

                    def variance_of(b):
                        if b >= 2:
                            pe.wait_ge(std, b - 1)
                        for k in range(K):
                            pe.wait_ge(sqx, b * K + k + 1)
                            r = mm(PO[b % 2][:, :], ones_d[:, :], SQX[:, k, :], start=(k == 0), stop=(k == K - 1))
                        r.then_inc(var, 1)
                    mean_of(0)
                    for b in range(B):
                        if b + 1 < B:
                            mean_of(b + 1)
                        variance_of(b)

                @block.scalar
                def _(act):
                    def high(b):
                        for k in range(K):
                            act.wait_ge(xn, b * K + k + 1)
                            nc.scalar.copy(out[0][:, b, k, :], XC[b % 2][:, k, :]).then_inc(hi, 1)
                    for b in range(B):
                        for k in range(K):
                            act.wait_ge(xc, b * K + k + 1)
                            if b:
                                act.wait_ge(var, b)
                            nc.scalar.activation(SQX[:, k, :], XC[b % 2][:, k, :], ACT.Square).then_inc(sqx, 1)
                        for n in range(2 * b, 2 * b + 2 if weights else 0):
                            act.wait_ge(staged[n % 2], 16 * (n // 2 + 1))
                            nc.scalar.mul(weights[n][1][0], STAGE[n % 2][:, :], WSCALE).then_inc(w_hi, 1)
                        if b:
                            high(b - 1)
                        act.wait_ge(var, b + 1)
                        if b:
                            act.wait_ge(rstd, b)
                        nc.scalar.activation(STD[:, :], PO[b % 2][:, :], ACT.Sqrt, bias=eps[:, :]).then_inc(std, 1)
                    high(B - 1)

                @block.gpsimd
                def _(pool):
                    def source(b):
                        for k in range(K):
                            pool.wait_ge(gated, b * K + k + 1)
                            nc.gpsimd.tensor_tensor(Y[:, b, k, :], Y[:, b, k, :], XV[:, k, b, :], ALU.add
                                                    ).then_inc(src, 1)
                    if before:
                        source(0)
                        source(1)
                    for b in range(B):
                        if before and b + 2 < B:
                            source(b + 2)
                        for k in range(K):
                            pool.wait_ge(hi, b * K + k + 1)
                            nc.gpsimd.tensor_tensor(out[1][:, b, k, :], XC[b % 2][:, k, :], out[0][:, b, k, :],
                                                    ALU.subtract).then_inc(split, 1)
                    pool.wait_ge(split, B * K)

                @block.vector
                def _(dve):
                    def gate(b):
                        for k in range(K):
                            ts(Y[:, b, k, :], Y[:, b, k, :], before[1][:, k:k + 1], MOD[:, before[0] + k, ds(b, 1)],
                               ALU.add, ALU.mult).then_inc(gated, 1)

                    def centre(b):
                        dve.wait_ge(mean, b + 1)
                        if b >= 2:
                            dve.wait_ge(split, (b - 1) * K)
                        for k in range(K):
                            tt(XC[b % 2][:, k, :], x_in(b, k), PA[b % 2][:, :], ALU.subtract).then_inc(xc, 1)

                    def finish(b):
                        x = XC[b % 2]
                        dve.wait_ge(std, b + 1)
                        nc.vector.reciprocal(RSTD[:, :], STD[:, :]).then_inc(rstd, 1)
                        dve.wait_ge(rstd, b + 1)
                        dve.wait_ge(sqx, (b + 1) * K)
                        for k in range(K):
                            tt(x[:, k, :], x[:, k, :], RSTD[:, :], ALU.mult).then_inc(xt, 1)
                        for k in range(K):
                            dve.wait_ge(xt, b * K + k + 1)
                            ts(x[:, k, :], x[:, k, :], MOD[:, scale + k, ds(b, 1)], MOD[:, shift + k, ds(b, 1)],
                               ALU.mult, ALU.add).then_inc(xn, 1)
                    if before:
                        for b in range(B):
                            gate(b)
                    centre(0)
                    for b in range(B):
                        if b + 1 < B:
                            centre(b + 1)
                        for n in range(2 * b, 2 * b + 2 if weights else 0):
                            dve.wait_ge(w_hi, n + 1)
                            stt(weights[n][1][1], STAGE[n % 2][:, :], WSCALE, weights[n][1][0], ALU.mult,
                                ALU.subtract).then_inc(w_lo, 1)
                        finish(b)
                    dve.wait_ge(xn, B * K)
                    if weights:
                        dve.wait_ge(w_lo, len(weights))

    loaded, consts, ident_done, ada_mm, mod_raw, mod_done, y0 = (
        sem(n) for n in ("loaded", "consts", "ident_done", "ada_mm", "mod_raw", "mod_done", "y0"))

    with ExitStack() as c:
        AW, CT, ab = sb("ada_w", [P, K, 6 * D], c=c), sb("cond", [P, K, B], c=c), sb("ada_b", [P, 6 * K], c=c)
        with nc.Block() as block:
            @block.sync
            def _(sp):
                for tile, src in ((CT[:, :, :], cond), (AW[:, :, :], ada_w.rearrange("(k p) n -> p k n", p=P)),
                                  (ab[:, :], ada_b), (ob[:, :], out_b), (bb2[:, :], b2), (bb1[:, :], b1),
                                  (bqkv[:, :], qkv_b)):
                    sp.dma_start(tile, src).then_inc(loaded, 16)

            @block.gpsimd
            def _(pool):
                nc.gpsimd.memset(ident[:, :], 0.0).then_inc(ident_done, 1)
                pool.wait_ge(ident_done, 1)
                nc.gpsimd.affine_select(out=ident[:, :], in_=ident[:, :], compare_op=ALU.not_equal, fill=1.0, base=0,
                                        pattern=[[-1, P]], channel_multiplier=1).then_inc(ident_done, 1)
                nc.gpsimd.memset(Y[:, :, :, :], 0.0).then_inc(y0, 1)

            @block.tensor
            def _(pe):
                pe.wait_ge(loaded, 16 * 7)
                for m in range(6 * K):
                    for k in range(K):
                        r = mm(PA[0][:, m * B:(m + 1) * B], AW[:, k, m * P:(m + 1) * P], CT[:, k, :],
                               start=(k == 0), stop=(k == K - 1))
                r.then_inc(ada_mm, 1)

            @block.vector
            def _(dve):
                nc.vector.memset(ones_d[:, :], 1.0 / D)
                nc.vector.memset(eps[:, :], 1e-6).then_inc(consts, 1)
                dve.wait_ge(loaded, 16 * 7)
                dve.wait_ge(ada_mm, 1)
                tt(MOD[:, :, :], PA[0][:, 0:6 * K * B].rearrange("p (m b) -> p m b", b=B),
                   ab[:, :].unsqueeze(2).to_broadcast([P, 6 * K, B]), ALU.add).then_inc(mod_raw, 1)
                dve.wait_ge(mod_raw, 1)
                for m in (SCALE1, SCALE2):
                    ts(MOD[:, m:m + K, :], MOD[:, m:m + K, :], 1.0, None, ALU.add).then_inc(mod_done, 1)
                ts(bqkv[:, 0:HEADS], bqkv[:, 0:HEADS], DH ** -0.5, None, ALU.mult).then_inc(mod_done, 1)
                dve.wait_ge(ident_done, 2)
                nc.vector.tensor_copy(identh[:, :], ident[:, :]).then_inc(mod_done, 1)
                dve.wait_ge(mod_done, 4)
                dve.wait_ge(consts, 1)

    with ExitStack() as c:
        X1 = [sb(f"x1_{n}", [P, B, K, T], F16, c=c) for n in ("hi", "lo")]
        normed("n1", X1, SCALE1, SHIFT1)

        PSCALE = 4096.0
        WF = sb("w_head", [P, 4 * D], c=c)
        WQ = [[sb(f"wq{i}_{n}", [P, 4 * D], F16, c=c) for n in ("hi", "lo")] for i in range(2)]
        Q, KT, V = ([[sb(f"{n}{i}_{m}", [P, T], F16, c=c) for m in ("hi", "lo")] for i in range(2)]
                    for n in ("q", "kT", "v"))
        FULL = [sb(f"{n}_full", [P, T], c=c) for n in ("q", "k", "v", "o")]
        O = [sb(f"o_{n}", [P, T], F16, c=c) for n in ("hi", "lo")]
        PR = [sb(f"prob{i}", [P, T], c=c) for i in range(2)]
        PH = [[sb(f"prob{i}_{n}", [P, T], F16, c=c) for n in ("hi", "lo")] for i in range(2)]
        PT = sb("probT", [P, 2, K, T], F16, c=c)
        PB16 = [c.enter_context(nc.psum_tensor(f"l3_pb16_{i}", [P, 2, T], F16)) for i in range(2)]
        NM, RSUM, RINV = (sb(n, [P, 2], c=c) for n in ("negmax", "rowsum", "rowinv"))
        (bias_in, qk_mm, qk, v_mm, v_done, sc, nmax, ex, rinv, pr, tr, ev, o_mm, o_done, y_mm, y_done) = (
            sem("a_" + n) for n in ("bias_in", "qk_mm", "qk", "v_mm", "v_done", "sc", "nmax", "ex", "rinv",
                                    "pr", "tr", "ev", "o_mm", "o_done", "y_mm", "y_done"))
        w_in, w_hi, w_lo, full, high, p_hi, o_full, o_hi = (
            sem("a_" + n) for n in ("w_in", "w_hi", "w_lo", "full", "high", "p_hi", "o_full", "o_hi"))
        NH, NIT = 2 * B, HEADS // 2
        qkv_h = qkv_w.rearrange("(k p) (w h d) -> h p k w d", p=P, w=3, d=DH)
        out_h = out_w.rearrange("(h p) n -> h p n", p=P)

        def wait(eng, s, value):
            if not isinstance(value, int) or value > 0:
                eng.wait_ge(s, value)

        def head_batch(n):
            return n // B % 2, n % B

        def iterations(eng, body):
            body(0, True, False)
            with eng.Fori(1, NIT - 1) as it:
                body(it, False, False)
            body(NIT - 1, False, True)
        with nc.Block() as block:
            def wq(i, part, w, k):
                return WQ[i][part][:, (w * K + k) * P:(w * K + k + 1) * P]

            def wo(i, part, m):
                return WQ[i][part][:, 3 * D + m * P:3 * D + (m + 1) * P]

            @block.sync
            def _(sp):
                def load(head):
                    wait(sp, w_lo, head)
                    for w in range(3):
                        sp.dma_start(WF[:, w * D:(w + 1) * D].rearrange("p (k d) -> p k d", k=K),
                                     qkv_h[ds(head, 1), :, :, w, :].rearrange("o p k d -> (o p) k d")).then_inc(w_in, 16)
                    sp.dma_start(WF[:, 3 * D:], out_h[ds(head, 1), :, :].rearrange("o p n -> (o p) n")
                                 ).then_inc(w_in, 16)
                load(0)
                with sp.Fori(1, HEADS) as head:
                    load(head)

            @block.tensor
            def _(pe):
                def project_qk(g, n, w):
                    i, b = head_batch(n)
                    if isinstance(g, int) and g < 3 - w:
                        wait(pe, full, 3 * (g - 1) + w + 1)
                    else:
                        wait(pe, y_done, (g - 2) * K + (0, 3)[w])
                    last = len(PARTS) * K - 1
                    for n_, (a, x, k) in enumerate((a, x, k) for a, x in PARTS for k in range(K)):
                        r = mm(PY[w][:, :], wq(i, a, w, k), X1[x][:, b, k, :], start=(n_ == 0), stop=(n_ == last))
                    r.then_inc(qk_mm, 1)

                def project_v(g, n, half):
                    i, b = head_batch(n)
                    if half == 0:
                        wait(pe, o_full, g - 1)
                    last = len(PARTS) * K - 1
                    for tc in (2 * half, 2 * half + 1):
                        for n_, (a, x, k) in enumerate((a, x, k) for a, x in PARTS for k in range(K)):
                            r = mm(PO[n % 2][:, tc * P:(tc + 1) * P], X1[a][:, b, k, tc * P:(tc + 1) * P],
                                   wq(i, x, 2, k), start=(n_ == 0), stop=(n_ == last))
                    if half:
                        r.then_inc(v_mm, 1)

                def scores(g, n, t):
                    j = t % 2
                    if t == 0:
                        wait(pe, qk, 2 * (g + 1))
                    wait(pe, ex, g * K + t - 1)
                    for a, x in PARTS:
                        r = mm(PA[j][:, :], Q[n % 2][a][:, t * P:(t + 1) * P], KT[n % 2][x][:, :],
                               start=(a == x), stop=(a > x))
                    r.then_inc(sc, 1)

                def transposes(g, t):
                    j = t % 2
                    wait(pe, ev, g * K + t - 1)
                    wait(pe, pr, g * K + t + 1)
                    for a in range(2):
                        for kc in range(K):
                            r = nc.tensor.transpose(PB16[j][:, a, kc * P:(kc + 1) * P],
                                                    PH[j][a][:, kc * P:(kc + 1) * P], identh[:, :])
                    r.then_inc(tr, 1)

                def values(g, n):
                    wait(pe, v_done, g + 1)
                    wait(pe, ev, (g + 1) * K)
                    last = len(PARTS) * K - 1
                    for n_, (a, x, k) in enumerate((a, x, k) for a, x in PARTS for k in range(K)):
                        r = mm(PO[n % 2][:, :], V[n % 2][a][:, k * P:(k + 1) * P], PT[:, x, k, :], start=(n_ == 0),
                               stop=(n_ == last))
                    r.then_inc(o_mm, 1)

                def project_out(g, n, ahead, last=False):
                    i, b = head_batch(n)
                    wait(pe, o_done, g + 1)
                    for m in range(K):
                        if m == 0 and not last:
                            wait(pe, full, 3 * (g + 1) + 2)
                        elif m == 1 and ahead:
                            wait(pe, full, 3 * (g + 2) + 1)
                        else:
                            wait(pe, y_done, g * K + m - 1)
                        for a, x in PARTS:
                            r = mm(PY[1 - m % 2][:, :], wo(i, a, m), O[x][:, :], start=(a == x), stop=(a > x))
                        r.then_inc(y_mm, 1)

                def body(it, first, last):
                    for n in range(NH):
                        g = it * NH + n
                        ahead = not (last and n == NH - 1)
                        scores(g, n, 1)
                        if ahead:
                            if (n + 1) % B == 0:
                                wait(pe, w_lo, it * 2 + (n + 1) // B + 1)
                            project_qk(g + 1, n + 1, 0)
                        if n or not first:
                            project_out(g - 1, n - 1, ahead)
                        transposes(g, 0)
                        scores(g, n, 2)
                        transposes(g, 1)
                        scores(g, n, 3)
                        if ahead:
                            project_qk(g + 1, n + 1, 1)
                            project_v(g + 1, n + 1, 0)
                        transposes(g, 2)
                        if ahead:
                            project_v(g + 1, n + 1, 1)
                        transposes(g, 3)
                        if ahead:
                            scores(g + 1, n + 1, 0)
                        values(g, n)
                pe.wait_ge(y0, 1)
                pe.wait_ge(w_lo, 1)
                project_qk(0, 0, 0)
                project_qk(0, 0, 1)
                project_v(0, 0, 0)
                project_v(0, 0, 1)
                scores(0, 0, 0)
                iterations(pe, body)
                project_out(NIT * NH - 1, NH - 1, False, last=True)

            @block.scalar
            def _(act):
                def split_weights(head, i):
                    if not (isinstance(head, int) and head < 2):
                        wait(act, y_mm, (head - 1) * B * K)
                    wait(act, w_in, (head + 1) * 64)
                    nc.scalar.mul(WQ[i][0][:, :], WF[:, :], WSCALE).then_inc(w_hi, 1)

                def evacuate_qkv(g, n, w):
                    i, b = head_batch(n)
                    src = (PY[0], PY[1], PO[n % 2])[w]
                    if w < 2:
                        wait(act, qk_mm, g * 2 + w + 1)
                    else:
                        wait(act, v_mm, g + 1)
                    if w < 2:
                        wait(act, qk, 2 * (g - 1) + w + 1)
                        nc.scalar.activation(FULL[w][:, :], src[:, :], ACT.Identity, bias=BH[i][:, w:w + 1],
                                             scale=(DH ** -0.5, 1.0)[w] / WSCALE).then_inc(full, 1)
                    else:
                        wait(act, v_done, g)
                        nc.scalar.mul(FULL[2][:, :], src[:, :], 1 / WSCALE).then_inc(full, 1)

                def head_out(g, n):
                    wait(act, o_done, g)
                    wait(act, o_mm, g + 1)
                    nc.scalar.activation(FULL[3][:, :], PO[n % 2][:, :], ACT.Identity,
                                         bias=BH[head_batch(n)[0]][:, 2:3], scale=1 / PSCALE).then_inc(o_full, 1)

                def exps(g, t):
                    j = t % 2
                    wait(act, pr, g * K + t - 1)
                    wait(act, nmax, g * K + t + 1)
                    nc.scalar.activation(PR[j][:, :], PA[j][:, :], ACT.Exp, bias=NM[:, j:j + 1],
                                         accum_out=RSUM[:, j:j + 1]).then_inc(ex, 1)

                def evacuate_t(g, t):
                    wait(act, tr, g * K + t + 1)
                    nc.scalar.copy(PT[:, :, :, t * P:(t + 1) * P],
                                   PB16[t % 2][:, :, :].rearrange("p a (k q) -> p a k q", k=K)).then_inc(ev, 1)

                def body(it, first, last):
                    for n in range(NH):
                        g = it * NH + n
                        ahead = not (last and n == NH - 1)
                        if n or not first:
                            head_out(g - 1, n - 1)
                        exps(g, 1)
                        if ahead:
                            if (n + 1) % B == 0:
                                wait(act, bias_in, it * 2 + (n + 1) // B + 1)
                            evacuate_qkv(g + 1, n + 1, 0)
                        if n % B == 1 and not (last and n > B):
                            split_weights(it * 2 + n // B + 1, head_batch(n + B)[0])
                        evacuate_t(g, 0)
                        exps(g, 2)
                        evacuate_t(g, 1)
                        exps(g, 3)
                        if ahead:
                            evacuate_qkv(g + 1, n + 1, 1)
                        evacuate_t(g, 2)
                        if ahead:
                            evacuate_qkv(g + 1, n + 1, 2)
                        evacuate_t(g, 3)
                        if ahead:
                            exps(g + 1, 0)
                split_weights(0, 0)
                act.wait_ge(bias_in, 1)
                for w in range(3):
                    evacuate_qkv(0, 0, w)
                exps(0, 0)
                iterations(act, body)
                head_out(NIT * NH - 1, NH - 1)

            @block.gpsimd
            def _(pool):
                def low(g, n, w):
                    part = (Q, KT, V)[w][n % 2]
                    wait(pool, full, 3 * g + w + 1)
                    wait(pool, high, 3 * g + w + 1)
                    nc.gpsimd.tensor_tensor(part[1][:, :], FULL[w][:, :], part[0][:, :], ALU.subtract
                                            ).then_inc(v_done if w == 2 else qk, 1)

                def body(it, first, last):
                    for n in range(NH):
                        for w in range(3):
                            if not (last and n == NH - 1):
                                low(it * NH + n + 1, n + 1, w)
                for w in range(3):
                    low(0, 0, w)
                iterations(pool, body)

            @block.vector
            def _(dve):
                def biases(head, i):
                    for w in range(3):
                        r = nc.vector.tensor_copy(BH[i][:, w:w + 1], bqkv[:, ds(head + w * HEADS, 1)])
                    r.then_inc(bias_in, 1)
                    wait(dve, bias_in, head + 1)

                def low_weights(head, i):
                    wait(dve, w_hi, head + 1)
                    stt(WQ[i][1][:, :], WF[:, :], WSCALE, WQ[i][0][:, :], ALU.mult, ALU.subtract).then_inc(w_lo, 1)

                def high_part(g, n, w):
                    wait(dve, full, 3 * g + w + 1)
                    nc.vector.tensor_copy((Q, KT, V)[w][n % 2][0][:, :], FULL[w][:, :]).then_inc(high, 1)

                def maximum(g, t):
                    j = t % 2
                    wait(dve, sc, g * K + t + 1)
                    nc.vector.tensor_reduce(NM[:, j:j + 1], PA[j][:, :], AX.X, ALU.max, negate=True
                                            ).then_inc(nmax, 1)

                def normalise(g, t):
                    j = t % 2
                    wait(dve, ex, g * K + t + 1)
                    ts(RSUM[:, j:j + 1], RSUM[:, j:j + 1], 1 / PSCALE, None, ALU.mult).then_inc(rinv, 1)
                    wait(dve, rinv, 2 * (g * K + t) + 1)
                    nc.vector.reciprocal(RINV[:, j:j + 1], RSUM[:, j:j + 1]).then_inc(rinv, 1)
                    wait(dve, tr, g * K + t - 1)
                    wait(dve, rinv, 2 * (g * K + t) + 2)
                    ts(PH[j][0][:, :], PR[j][:, :], RINV[:, j:j + 1], None, ALU.mult).then_inc(p_hi, 1)
                    wait(dve, p_hi, g * K + t + 1)
                    stt(PH[j][1][:, :], PR[j][:, :], RINV[:, j:j + 1], PH[j][0][:, :], ALU.mult, ALU.subtract
                        ).then_inc(pr, 1)

                def head_out(g, n):
                    wait(dve, y_mm, g * K)
                    wait(dve, o_full, g + 1)
                    nc.vector.tensor_copy(O[0][:, :], FULL[3][:, :]).then_inc(o_hi, 1)

                def head_out_low(g):
                    wait(dve, o_hi, g + 1)
                    tt(O[1][:, :], FULL[3][:, :], O[0][:, :], ALU.subtract).then_inc(o_done, 1)

                def add_out(g, n, m):
                    b = head_batch(n)[1]
                    wait(dve, y_mm, g * K + m + 1)
                    stt(Y[:, b, m, :], PY[1 - m % 2][:, :], 1 / WSCALE, Y[:, b, m, :], ALU.mult, ALU.add
                        ).then_inc(y_done, 1)

                def body(it, first, last):
                    for n in range(NH):
                        g = it * NH + n
                        before = n > 0 or not first
                        ahead = not (last and n == NH - 1)
                        if before:
                            head_out(g - 1, n - 1)
                        maximum(g, 1)
                        if before:
                            head_out_low(g - 1)
                        if (n + 1) % B == 0 and ahead:
                            biases(it * 2 + (n + 1) // B, head_batch(n + 1)[0])
                        normalise(g, 0)
                        if before:
                            add_out(g - 1, n - 1, 0)
                            add_out(g - 1, n - 1, 1)
                        normalise(g, 1)
                        if ahead:
                            high_part(g + 1, n + 1, 0)
                        if before:
                            add_out(g - 1, n - 1, 2)
                            add_out(g - 1, n - 1, 3)
                        maximum(g, 2)
                        maximum(g, 3)
                        normalise(g, 2)
                        if ahead:
                            high_part(g + 1, n + 1, 1)
                        normalise(g, 3)
                        if n % B == 1 and not (last and n > B):
                            low_weights(it * 2 + n // B + 1, head_batch(n + B)[0])
                        if ahead:
                            high_part(g + 1, n + 1, 2)
                            maximum(g + 1, 0)
                biases(0, 0)
                low_weights(0, 0)
                for w in range(3):
                    high_part(0, 0, w)
                maximum(0, 0)
                iterations(dve, body)
                head_out(NIT * NH - 1, NH - 1)
                head_out_low(NIT * NH - 1)
                for m in range(K):
                    add_out(NIT * NH - 1, NH - 1, m)
                dve.wait_ge(y_done, HEADS * B * K)

    with ExitStack() as c:
        X2 = [sb(f"x2_{n}", [P, B, K, T], F16, c=c) for n in ("hi", "lo")]
        W1 = [sb(f"w1_{n}", [P, K, 4 * D], F16, c=c) for n in ("hi", "lo")]
        W2 = [sb(f"w2_{n}", [P, F, D], F16, c=c) for n in ("hi", "lo")]
        w1_in = w1.rearrange("(k p) n -> k p n", p=P)
        w2_in = w2.rearrange("(g k p) n -> g p k n", k=4, p=P)
        pieces = [(w1_in[k, :, :], [W1[i][:, k, :] for i in range(2)]) for k in range(K)]
        pieces += [(w2_in[g, :, :, :], [W2[i][:, 4 * g:4 * g + 4, :].rearrange("p k n -> p (k n)")
                    for i in range(2)]) for g in range(F // 4)]
        normed("n2", X2, SCALE2, SHIFT2, before=(GATE1, ob), weights=pieces)
        HW = [sb(f"h_full{i}", [P, T], c=c) for i in range(2)]
        HF = [sb(f"h_{n}", [P, F, T], F16, c=c) for n in ("hi", "lo")]
        R, R2 = sb("r", [P, T], c=c), sb("r2", [P, T], c=c)
        h_mm, h_full, h_hi, h_split, z_mm, r1, r2, o_ready, o_out = (
            sem("m_" + n) for n in ("h_mm", "h_full", "h_hi", "h_split", "z_mm", "r1", "r2", "o_ready", "o_out"))
        with nc.Block() as block:
            @block.sync
            def _(sp):
                with sp.Fori(0, B) as b:
                    sp.wait_ge(o_ready, (b + 1) * K)
                    sp.dma_start(out[ds(b, 1), :, :, :].rearrange("o k p t -> p (o k) t"),
                                 Y[:, ds(b, 1), :, :].rearrange("p o k t -> p (o k) t")).then_inc(o_out, 16)
                sp.wait_ge(o_out, 16 * B)

            @block.tensor
            def _(pe):
                with pe.Fori(0, B) as b:
                    last = len(PARTS) * K - 1
                    for m in range(F):
                        if m >= 2:
                            pe.wait_ge(h_full, b * F + m - 1)
                        for n, (a, x, k) in enumerate((a, x, k) for a, x in PARTS for k in range(K)):
                            r = mm(PO[m % 2][:, :], W1[a][:, k, m * P:(m + 1) * P],
                                   X2[x][:, ds(b, 1), k, :].rearrange("p o t -> p (o t)"), start=(n == 0), stop=(n == last))
                        r.then_inc(h_mm, 1)
                    for m in range(K):
                        if m >= 2:
                            pe.wait_ge(r1, b * K + m - 1)
                        for k in range(F):
                            if m == 0:
                                pe.wait_ge(h_split, b * F + k + 1)
                            for a, x in PARTS:
                                r = mm(PY[m % 2][:, :], W2[a][:, k, m * P:(m + 1) * P], HF[x][:, k, :],
                                       start=(k == 0 and a == x), stop=(k == F - 1 and a > x))
                        r.then_inc(z_mm, 1)

            @block.scalar
            def _(act):
                with act.Fori(0, B) as b:
                    for m in range(F):
                        act.wait_ge(h_mm, b * F + m + 1)
                        if m >= 2:
                            act.wait_ge(h_split, b * F + m - 1)
                        nc.scalar.activation(HW[m % 2][:, :], PO[m % 2][:, :], ACT.Gelu, bias=bb1[:, m:m + 1],
                                             scale=1 / WSCALE).then_inc(h_full, 1)

            @block.vector
            def _(dve):
                with dve.Fori(0, B) as b:
                    xb = lambda k: XV[:, k, ds(b, 1), :].rearrange("p o t -> p (o t)")
                    yb = lambda k: Y[:, ds(b, 1), k, :].rearrange("p o t -> p (o t)")
                    for m in range(F):
                        dve.wait_ge(h_full, b * F + m + 1)
                        nc.vector.tensor_copy(HF[0][:, m, :], HW[m % 2][:, :]).then_inc(h_hi, 1)
                        dve.wait_ge(h_hi, b * F + m + 1)
                        tt(HF[1][:, m, :], HW[m % 2][:, :], HF[0][:, m, :], ALU.subtract).then_inc(h_split, 1)
                    for m in range(K):
                        dve.wait_ge(z_mm, b * K + m + 1)
                        ts(R[:, :], PY[m % 2][:, :], 1 / WSCALE, bb2[:, m:m + 1], ALU.mult, ALU.add).then_inc(r1, 1)
                        dve.wait_ge(r1, b * K + m + 1)
                        stt(R2[:, :], R[:, :], MOD[:, GATE2 + m, ds(b, 1)], yb(m), ALU.mult, ALU.add).then_inc(r2, 1)
                        dve.wait_ge(r2, b * K + m + 1)
                        tt(yb(m), R2[:, :], xb(m), ALU.add).then_inc(o_ready, 1)


def program(nc, x, state, coupling, osc_bias, w_ih, w_hh, b_ih, b_hh, hn_bias, l2, l3, out):
    with ExitStack() as ctx:
        XT = ctx.enter_context(nc.sbuf_tensor("x_time_major", [P, (T + 2) * S], F32))
        cond = state.rearrange("p (k b) -> p k b", b=B)
        with ExitStack() as both:
            weights = Layer2Weights(nc, both, cond, *l2)
            sems = PhaseSemaphores()
            with ExitStack() as c:
                with nc.Block() as block:
                    recurrence(nc, c, sems, block, XT, state, coupling, osc_bias, w_ih, w_hh, b_ih, b_hh, hn_bias, x,
                               weights)
            sems.close(nc)
            sems = PhaseSemaphores()
            with ExitStack() as c:
                with nc.Block() as block:
                    layer2(nc, c, sems, block, XT, weights)
            sems.close(nc)
        sems = PhaseSemaphores()
        with ExitStack() as c:
            layer3(nc, c, sems, XT, cond, *l3, out)
        sems.close(nc)


def kernel(**inputs):
    import numpy as np
    import concourse.bacc as bacc
    from concourse.bass_utils import run_bass_kernel_spmd

    def cols(name):
        return inputs[name].reshape(-1, P).T

    inputs = {n: np.asarray(a) for n, a in inputs.items()}
    arrays = {
        "x": inputs["x"].reshape(B, T, K, P).transpose(3, 1, 2, 0).reshape(P, T * S),
        "state": inputs["cond_2048"].reshape(B, K, P).transpose(2, 1, 0).reshape(P, S),
        "coupling": inputs["L0_cond_coupling"].T,
        "osc_bias": np.repeat(cols("L0_cond_bias"), B, axis=1),
        "w_ih": inputs["L1_cond_W_ih"], "w_hh": inputs["L1_cond_W_hh"],
        "b_ih": cols("L1_cond_b_ih"), "b_hh": cols("L1_cond_b_hh"),
        "hn_bias": np.repeat(cols("L1_cond_b_hh")[:, 2 * K:], B, axis=1),
        "w_emb": inputs["L2_cond_W_emb"], "b_emb": cols("L2_cond_b_emb"), "g_norm": cols("L2_cond_g_norm"),
        "w_qkv": inputs["L2_cond_W_qkv"],
        "g_qk": np.stack([np.tile(inputs["L2_cond_g_q"], 4), np.tile(inputs["L2_cond_g_k"], 4)], 1),
        "w_out": inputs["L2_cond_W_out"],
        "ada_w": inputs["L3_cond_ada_w"], "ada_b": cols("L3_cond_ada_b"), "qkv_w": inputs["L3_cond_qkv_w"],
        "qkv_b": cols("L3_cond_qkv_b"), "out_w": inputs["L3_cond_out_w"], "out_b": cols("L3_cond_out_b"),
        "w1": inputs["L3_cond_ffn_w1"], "b1": cols("L3_cond_ffn_b1"), "w2": inputs["L3_cond_ffn_w2"],
        "b2": cols("L3_cond_ffn_b2"),
    }
    arrays = {n: np.ascontiguousarray(a) for n, a in arrays.items()}
    nc = bacc.Bacc("TRN2", target_bir_lowering=False, num_devices=1)
    ap = {n: nc.dram_tensor("in_" + n, a.shape, mybir.dt.from_np(a.dtype), kind="ExternalInput").ap()
          for n, a in arrays.items()}
    out = nc.dram_tensor("out", (B, K, P, T), F32, kind="ExternalOutput").ap()
    names = list(ap)
    i2, i3 = names.index("w_emb"), names.index("ada_w")
    program(nc, *(ap[n] for n in names[:i2]), [ap[n] for n in names[i2:i3]], [ap[n] for n in names[i3:]], out)
    r = run_bass_kernel_spmd(nc, [{"in_" + n: a for n, a in arrays.items()}], core_ids=[0])
    return r.results[0]["out"].transpose(0, 3, 1, 2).reshape(B, T, D)
```
